# Optimizing a Trainium2 kernel written in Bass

```python
import numpy as np
import jax
import jax.numpy as jnp

def _softmax(x, axis=-1):
    return jax.nn.softmax(x, axis=axis)

def _gelu(x):
    return jax.nn.gelu(x, approximate=True)

def _silu(x):
    return jax.nn.silu(x)

def _sigmoid(x):
    return jax.nn.sigmoid(x)

def _layernorm(x, axis=-1, eps=1e-05):
    m = jnp.mean(x, axis=axis, keepdims=True)
    v = jnp.var(x, axis=axis, keepdims=True)
    return (x - m) / jnp.sqrt(v + eps)

def _scatter_add(tgt, idx, src, axis=0):
    return tgt.at[idx].add(src)

def _segment_sum(src, seg, n):
    return jax.ops.segment_sum(src, seg, n)
kernel_name = 'mk_audio_tower_d1_tok_audfeat256_r4_f64404'

def setup_inputs(seed: int=0):
    np.random.seed(seed)
    _w = jnp.asarray

    def _rec_inputs():
        import jax
        import jax.numpy as jnp
        _rk = jax.random.key(seed)
        x = 7.22013e-05 + 1.00017 * jax.random.normal(jax.random.fold_in(_rk, 1), (8, 512, 128), jnp.float32)
        return x
    x = _rec_inputs()

    def _L0_tok_setup():
        import jax, jax.numpy as jnp
        import numpy as np
        FILTER_SIZE = 8
        INPUT_DIM = 128
        KERNEL_SIZE = 64
        key = jax.random.key(seed)
        k1, k2, k3, k4 = jax.random.split(key, 4)
        user_batch = jax.random.normal(k1, (32, 512, INPUT_DIM), dtype=jnp.float32)
        filt = jax.random.uniform(k2, (FILTER_SIZE, INPUT_DIM), dtype=jnp.float32)
        W_k = jax.random.uniform(k3, (FILTER_SIZE * INPUT_DIM, KERNEL_SIZE), dtype=jnp.float32)
        b_k = jax.random.uniform(k4, (KERNEL_SIZE,), dtype=jnp.float32)
        return {'user_batch': user_batch, 'filt': filt, 'W_k': W_k, 'b_k': b_k}
    _L0_tok_all = _L0_tok_setup()
    _L0_tok_in = {k: v for k, v in _L0_tok_all.items() if k in ('filt', 'W_k', 'b_k')}
    del _L0_tok_all

    def _L0_attn_setup():
        import jax, jax.numpy as jnp
        import numpy as np
        B, N, C = (8, 2048, 64)
        HEADS, DH, KR = (8, 32, 4)
        INNER = HEADS * DH
        FF = 4 * C
        EPS = 1e-05

        def layernorm(x, g, b):
            mu = jnp.mean(x, axis=-1, keepdims=True)
            var = jnp.mean((x - mu) ** 2, axis=-1, keepdims=True)
            return (x - mu) * jax.lax.rsqrt(var + EPS) * g + b
        key = jax.random.key(seed)
        ks = jax.random.split(key, 16)
        s = 0.02
        return {'x': jax.random.normal(ks[0], (B, N, C), jnp.float32), 'ln1_g': jnp.ones((C,), jnp.float32), 'ln1_b': jnp.zeros((C,), jnp.float32), 'Wx': jax.random.normal(ks[1], (C, INNER), jnp.float32) * s, 'bx': jnp.zeros((INNER,), jnp.float32), 'Wq': jax.random.normal(ks[2], (DH, KR), jnp.float32) * s, 'Wk': jax.random.normal(ks[3], (DH, KR), jnp.float32) * s, 'Wv': jax.random.normal(ks[4], (DH, DH), jnp.float32) * s, 'Wo': jax.random.normal(ks[5], (INNER, C), jnp.float32) * s, 'bo': jnp.zeros((C,), jnp.float32), 'ln2_g': jnp.ones((C,), jnp.float32), 'ln2_b': jnp.zeros((C,), jnp.float32), 'W1': jax.random.normal(ks[6], (C, FF), jnp.float32) * s, 'b1': jnp.zeros((FF,), jnp.float32), 'W2': jax.random.normal(ks[7], (FF, C), jnp.float32) * s, 'b2': jnp.zeros((C,), jnp.float32)}
    _L0_attn_all = _L0_attn_setup()
    _L0_attn_in = {k: v for k, v in _L0_attn_all.items() if k in ('ln1_g', 'ln1_b', 'Wx', 'bx', 'Wq', 'Wk', 'Wv', 'Wo', 'bo', 'ln2_g', 'ln2_b', 'W1', 'b1', 'W2', 'b2')}
    del _L0_attn_all

    def _L0_ffn_setup():
        import jax, jax.numpy as jnp
        import numpy as np
        E = 8
        K = 2
        D = 64
        H = 128
        DOUT = 64
        EPS = 1e-05
        key = jax.random.key(seed)
        ks = jax.random.split(key, 9)
        s = 0.02
        return {'x': jax.random.normal(ks[0], (4, 2048, D), jnp.float32), 'gamma': 1.0 + 0.05 * jax.random.normal(ks[1], (D,), jnp.float32), 'beta': 0.05 * jax.random.normal(ks[2], (D,), jnp.float32), 'Wr': 0.01 * jax.random.normal(ks[3], (D, E), jnp.float32), 'br': jnp.zeros((E,), jnp.float32), 'W1': s * jax.random.normal(ks[4], (E, D, H), jnp.float32), 'b1': s * jax.random.normal(ks[5], (E, H), jnp.float32), 'W2': s * jax.random.normal(ks[6], (E, H, DOUT), jnp.float32), 'b2': s * jax.random.normal(ks[7], (E, DOUT), jnp.float32)}
    _L0_ffn_all = _L0_ffn_setup()
    _L0_ffn_in = {k: v for k, v in _L0_ffn_all.items() if k in ('gamma', 'beta', 'Wr', 'br', 'W1', 'b1', 'W2', 'b2')}
    del _L0_ffn_all
    return {'x': x, 'L0_tok_filt': _L0_tok_in['filt'], 'L0_tok_W_k': _L0_tok_in['W_k'], 'L0_tok_b_k': _L0_tok_in['b_k'], 'L0_attn_ln1_g': _L0_attn_in['ln1_g'], 'L0_attn_ln1_b': _L0_attn_in['ln1_b'], 'L0_attn_Wx': _L0_attn_in['Wx'], 'L0_attn_bx': _L0_attn_in['bx'], 'L0_attn_Wq': _L0_attn_in['Wq'], 'L0_attn_Wk': _L0_attn_in['Wk'], 'L0_attn_Wv': _L0_attn_in['Wv'], 'L0_attn_Wo': _L0_attn_in['Wo'], 'L0_attn_bo': _L0_attn_in['bo'], 'L0_attn_ln2_g': _L0_attn_in['ln2_g'], 'L0_attn_ln2_b': _L0_attn_in['ln2_b'], 'L0_attn_W1': _L0_attn_in['W1'], 'L0_attn_b1': _L0_attn_in['b1'], 'L0_attn_W2': _L0_attn_in['W2'], 'L0_attn_b2': _L0_attn_in['b2'], 'L0_ffn_gamma': _L0_ffn_in['gamma'], 'L0_ffn_beta': _L0_ffn_in['beta'], 'L0_ffn_Wr': _L0_ffn_in['Wr'], 'L0_ffn_br': _L0_ffn_in['br'], 'L0_ffn_W1': _L0_ffn_in['W1'], 'L0_ffn_b1': _L0_ffn_in['b1'], 'L0_ffn_W2': _L0_ffn_in['W2'], 'L0_ffn_b2': _L0_ffn_in['b2']}

def reference(x, L0_tok_filt, L0_tok_W_k, L0_tok_b_k, L0_attn_ln1_g, L0_attn_ln1_b, L0_attn_Wx, L0_attn_bx, L0_attn_Wq, L0_attn_Wk, L0_attn_Wv, L0_attn_Wo, L0_attn_bo, L0_attn_ln2_g, L0_attn_ln2_b, L0_attn_W1, L0_attn_b1, L0_attn_W2, L0_attn_b2, L0_ffn_gamma, L0_ffn_beta, L0_ffn_Wr, L0_ffn_br, L0_ffn_W1, L0_ffn_b1, L0_ffn_W2, L0_ffn_b2):
    import jax
    import jax.numpy as jnp

    def _L0_tok_ref(user_batch, filt, W_k, b_k):
        import jax, jax.numpy as jnp
        import numpy as np
        FILTER_SIZE = 8
        INPUT_DIM = 128
        KERNEL_SIZE = 64
        B, L, D = user_batch.shape
        F = filt.shape[0]
        n_win = L - F
        idx = jnp.arange(n_win)[:, None] + jnp.arange(F)[None, :]
        windows = user_batch[:, idx, :]
        W = W_k.reshape(F, D, -1)
        out = jnp.einsum('blfd,fd,fdk->blk', windows, filt, W)
        return jax.nn.relu(out + b_k)

    def _L0_attn_ref(x, ln1_g, ln1_b, Wx, bx, Wq, Wk, Wv, Wo, bo, ln2_g, ln2_b, W1, b1, W2, b2):
        import jax, jax.numpy as jnp
        import numpy as np
        B, N, C = (8, 2048, 64)
        HEADS, DH, KR = (8, 32, 4)
        INNER = HEADS * DH
        FF = 4 * C
        EPS = 1e-05

        def layernorm(x, g, b):
            mu = jnp.mean(x, axis=-1, keepdims=True)
            var = jnp.mean((x - mu) ** 2, axis=-1, keepdims=True)
            return (x - mu) * jax.lax.rsqrt(var + EPS) * g + b
        b, n, c = x.shape
        h = layernorm(x, ln1_g, ln1_b)
        xm = h @ Wx + bx
        xm = xm.reshape(b, n, HEADS, DH).transpose(0, 2, 1, 3)
        q = jax.nn.softmax(xm @ Wq, axis=-1)
        k = jax.nn.softmax(xm @ Wk, axis=-2)
        v = xm @ Wv
        kv = jnp.einsum('bhnr,bhnd->bhrd', k, v)
        qkv = jnp.einsum('bhnr,bhrd->bhnd', q, kv)
        attn = qkv.transpose(0, 2, 1, 3).reshape(b, n, INNER) @ Wo + bo
        fx = attn + x
        h2 = layernorm(fx, ln2_g, ln2_b)
        m = jax.nn.gelu(h2 @ W1 + b1, approximate=False) @ W2 + b2
        return m + fx

    def _L0_ffn_ref(x, gamma, beta, Wr, br, W1, b1, W2, b2):
        import jax, jax.numpy as jnp
        import numpy as np
        E = 8
        K = 2
        D = 64
        H = 128
        DOUT = 64
        EPS = 1e-05
        mu = jnp.mean(x, axis=-1, keepdims=True)
        var = jnp.mean(jnp.square(x - mu), axis=-1, keepdims=True)
        xn = (x - mu) * jax.lax.rsqrt(var + EPS) * gamma + beta
        logits = jnp.einsum('bsd,de->bse', xn, Wr) + br
        top_vals, top_idx = jax.lax.top_k(logits, K)
        w = jax.nn.softmax(top_vals, axis=-1)
        w_full = jnp.einsum('bsk,bske->bse', w, jax.nn.one_hot(top_idx, E, dtype=w.dtype))
        y = jnp.zeros(x.shape[:-1] + (DOUT,), x.dtype)
        for e in range(E):
            h = jax.nn.gelu(jnp.einsum('bsd,dh->bsh', xn, W1[e]) + b1[e], approximate=False)
            y_e = jnp.einsum('bsh,hd->bsd', h, W2[e]) + b2[e]
            y = y + y_e * w_full[..., e, None]
        return y
    h = _L0_tok_ref(x, L0_tok_filt, L0_tok_W_k, L0_tok_b_k)
    h = h + _L0_attn_ref(_layernorm(h, axis=-1), L0_attn_ln1_g, L0_attn_ln1_b, L0_attn_Wx, L0_attn_bx, L0_attn_Wq, L0_attn_Wk, L0_attn_Wv, L0_attn_Wo, L0_attn_bo, L0_attn_ln2_g, L0_attn_ln2_b, L0_attn_W1, L0_attn_b1, L0_attn_W2, L0_attn_b2)
    h = h + _L0_ffn_ref(_layernorm(h, axis=-1), L0_ffn_gamma, L0_ffn_beta, L0_ffn_Wr, L0_ffn_br, L0_ffn_W1, L0_ffn_b1, L0_ffn_W2, L0_ffn_b2)
    return h

_drawn_inputs = setup_inputs


def setup_inputs(seed=0):
    import zlib

    import numpy as np

    out = dict(_drawn_inputs(seed))
    spreads = {'L0_attn_ln1_g': (1.0, 0.6),
     'L0_attn_ln1_b': (0.0, 0.8),
     'L0_attn_bx': (0.0, 0.8),
     'L0_attn_bo': (0.0, 0.737),
     'L0_attn_ln2_g': (1.0, 0.6),
     'L0_attn_ln2_b': (0.0, 0.8),
     'L0_attn_b1': (0.0, 0.8),
     'L0_attn_b2': (0.0, 0.637),
     'L0_ffn_br': (0.0, 0.8)}
    factors = {'L0_attn_Wx': 8.0,
     'L0_attn_Wq': 8.0,
     'L0_attn_Wk': 8.0,
     'L0_attn_Wv': 8.0,
     'L0_attn_Wo': 8.0,
     'L0_attn_W1': 8.0,
     'L0_attn_W2': 8.0,
     'L0_ffn_gamma': 8.0,
     'L0_ffn_beta': 8.0,
     'L0_ffn_Wr': 8.0,
     'L0_ffn_W1': 8.0,
     'L0_ffn_b1': 35.988,
     'L0_ffn_W2': 8.0,
     'L0_ffn_b2': 47.26}
    for name, (base, spread) in spreads.items():
        noise = np.random.default_rng([zlib.crc32(name.encode()), seed]).standard_normal(out[name].shape)
        drawn = base * np.exp(spread * noise) if base else spread * noise
        out[name] = jnp.asarray(drawn.astype(out[name].dtype))
    for name, factor in factors.items():
        out[name] = (out[name] * factor).astype(out[name].dtype)
    return out
```

```python
from contextlib import ExitStack

import concourse.bass as bass
from concourse import mybir

F32 = mybir.dt.float32
F32R = mybir.dt.float32r
U32 = mybir.dt.uint32
ALU = mybir.AluOpType
ACT = mybir.ActivationFunctionType
AX_X = mybir.AxisListType.X
EPS = 1e-05

PE_DONE = """ps_xT ps_conv ps_pre ps_zT ps_L ps_q ps_k ps_G ps_GT ps_M ps_qT ps_at ps_z2T ps_m0 ps_m1
ps_m2 ps_mT ps_z3T ps_route ps_lg ps_w ps_out"""
ACT_DONE = """x_hi conv_hi_taps h1 z_hi zT L k_exp q_exp qT z2_hi z2T mlp_g0 mlp_g1 mlp_F z3_hi z3T
h2_kept route th wT"""
DVE_DONE = """x_lo pre a_stats a_mv a_var a_hc z z_lo k_negmax k_rden EkT q_max q_sub q_sum q_rec q_norm
q_hi q_lo G_norm G_heads M_sum M_hi M_stack fx b_stats b_mv b_var b_hc z2 z2_lo m_half h2 m_stats m_mv
m_var m_hc z3 z3_lo lg top idx gap p hot hot_p w w_hi w_lo o_half o"""
POOL_DONE = "a_rstd z_res0 z_res b_rstd fxh m_rstd sum0 sum1 sum_all"


def audio_tower_kernel(nc, a, out):
    NB, L, D = a["x"].shape
    TAPS = a["tok_filt"].shape[0]
    C = a["tok_W_k"].shape[1]
    NT = L - TAPS
    CH = 4
    P = NT // CH
    HALF = TAPS // 2
    DH, KR = a["attn_Wq"].shape
    H = a["attn_Wx"].shape[1] // DH
    HR = H * KR
    FF = a["attn_W1"].shape[1]
    NE, _, EH = a["ffn_W1"].shape
    NP = NE // 2
    XC = L // 128
    assert P * CH == NT and 2 * C == 128 and D == 128 and EH == 128 and FF == 256 and HR == 32

    with ExitStack() as ctx:
        def sb(name, shape, dt=F32):
            return ctx.enter_context(nc.sbuf_tensor(name, shape, dt))

        def sem(name):
            return ctx.enter_context(nc.semaphore(name))

        bank = [ctx.enter_context(nc.psum_tensor(f"bank{i}", [128, 512], F32)) for i in range(8)]
        BA, B1, B2, BM, BH0, BH1, BY, BW = bank
        BH = [BH0, BH1]

        ident = sb("ident", [128, 128])
        iota8 = sb("iota8", [128, NE])
        ones11 = sb("ones11", [1, 2])
        head_rows = sb("head_rows", [32, H, HR])
        head_mask = sb("head_mask", [128, H // 2, HR])
        sel32 = sb("sel32", [128, NP, 2, C])
        sel = sb("sel", [128, NP, 2 * C], F32R)
        minus_half = sb("minus_half", [128, 8])
        filt_sb = sb("filt_sb", [TAPS, D])
        filtT = sb("filtT", [D, TAPS])
        wk_sb = sb("wk_sb", [D, TAPS, C])
        wc32 = sb("wc32", [D, HALF, 2, C])
        wc_hi = sb("wc_hi", [D, HALF, 2 * C], F32R)
        wc_lo = sb("wc_lo", [D, HALF, 2 * C], F32R)
        bk_col = sb("bk_col", [C, 1])
        g1_col = sb("g1_col", [128, 1])
        b1_col = sb("b1_col", [C, 1])
        wx_sb = sb("wx_sb", [C, H * DH])
        wxT2 = sb("wxT2", [DH, H, 2, C])
        bxT = sb("bxT", [DH, H])
        bxg = sb("bxg", [DH, H])
        wkq_sb = sb("wkq_sb", [DH, 2 * KR])
        wv_sb = sb("wv_sb", [DH, DH])
        wvT = sb("wvT", [DH, DH])
        wo_sb = sb("wo_sb", [DH, H, C])
        wvo = sb("wvo", [DH, H, C])
        bx_heads = sb("bx_heads", [DH, H, HR])
        u_pair = sb("u_pair", [128, H // 2, C])
        u_bias = sb("u_bias", [HR, C])
        wqk32 = sb("wqk32", [128, 2 * HR])
        wqk_hi = sb("wqk_hi", [128, 2 * HR], F32R)
        wqk_lo = sb("wqk_lo", [128, 2 * HR], F32R)
        bqk_row = sb("bqk_row", [1, 2 * HR])
        bqk_col = sb("bqk_col", [2 * HR, 1])
        bo_rows = sb("bo_rows", [128, C])
        g2_col = sb("g2_col", [128, 1])
        b2ln_col = sb("b2ln_col", [C, 1])
        w1_raw = sb("w1_raw", [128, FF])
        w1_32 = sb("w1_32", [128, FF])
        w1_hi = sb("w1_hi", [128, FF], F32R)
        w1_lo = sb("w1_lo", [128, FF], F32R)
        b1mT = sb("b1mT", [128, 2])
        b1m = sb("b1m", [128, 2])
        w2_sb = sb("w2_sb", [128, 2, C])
        b2m_col = sb("b2m_col", [128, 1])
        gam_col = sb("gam_col", [128, 1])
        bet_col = sb("bet_col", [C, 1])
        wr_raw = sb("wr_raw", [128, NE])
        wr32 = sb("wr32", [128, NE])
        wr_hi = sb("wr_hi", [128, NE], F32R)
        wr_lo = sb("wr_lo", [128, NE], F32R)
        brc = sb("brc", [NE, 1])
        br_col = sb("br_col", [NE, 1])
        ew1_raw = sb("ew1_raw", [128, NE, EH])
        ew1_32 = sb("ew1_32", [128, NE * EH])
        ew1_hi = sb("ew1_hi", [128, NE * EH], F32R)
        ew1_lo = sb("ew1_lo", [128, NE * EH], F32R)
        eb1T = sb("eb1T", [128, NE])
        eb1 = sb("eb1", [128, NE])
        ew2 = sb("ew2", [EH, NE, C])
        eb2 = sb("eb2", [128, NP])

        x_sb = sb("x_sb", [128, XC, D])
        x_hi = sb("x_hi", [D, L], F32R)
        x_lo = sb("x_lo", [D, L], F32R)
        late_taps = sb("late_taps", [C, NT])
        pre = sb("pre", [C, NT])
        h1 = sb("h1", [P, CH, C])
        a_st = sb("a_st", [P, CH, 6])
        a_mv = sb("a_mv", [P, CH, 2])
        a_var = sb("a_var", [P, 2, CH])
        a_rs = sb("a_rs", [P, 2, CH])
        hc = sb("hc", [P, CH, C])
        z = sb("z", [P, CH, C])
        zhl = sb("zhl", [P, CH, 2, C], F32R)
        zr0 = sb("zr0", [P, CH, C])
        zr = sb("zr", [P, CH, C])
        zT = sb("zT", [128, NT], F32R)
        kq = sb("kq", [2 * HR, NT])
        k_negmax = sb("k_negmax", [HR, 1])
        k_den = sb("k_den", [HR, 1])
        k_rden = sb("k_rden", [HR, 1])
        EkT = sb("EkT", [P, CH, HR])
        q_max = sb("q_max", [P, CH * H])
        q_sub = sb("q_sub", [P, CH * H, KR])
        q_e = sb("q_e", [P, CH * H, KR])
        q_sum = sb("q_sum", [P, CH * H])
        q_rec = sb("q_rec", [P, CH * H])
        q_n = sb("q_n", [P, CH, HR])
        qhl = sb("qhl", [P, CH, 3, HR], F32R)
        qT = sb("qT", [3 * HR, NT], F32R)
        Gd = sb("Gd", [HR, 2, C])
        Gx = sb("Gx", [128, H // 2, HR])
        Mf = sb("Mf", [HR, C])
        M3 = sb("M3", [3 * HR, C], F32R)
        fx = sb("fx", [P, CH, C])
        fxh = sb("fxh", [P, CH, C])
        b_st = sb("b_st", [P, CH, 6])
        b_mv = sb("b_mv", [P, CH, 2])
        b_var = sb("b_var", [P, CH])
        b_rs = sb("b_rs", [P, CH])
        b_hc = sb("b_hc", [P, CH, C])
        z2 = sb("z2", [P, CH, C])
        z2hl = sb("z2hl", [P, CH, 2, C], F32R)
        z2T = sb("z2T", [128, NT], F32R)
        mg = [sb(f"mg{k}", [128, NT]) for k in range(2)]
        mF = sb("mF", [128, NT])
        m_half = sb("m_half", [P, CH, C])
        h2 = sb("h2", [P, CH, C])
        h2_kept = sb("h2_kept", [P, CH, C])
        m_st = sb("m_st", [P, CH, 6])
        m_mv = sb("m_mv", [P, CH, 2])
        m_var = sb("m_var", [P, CH])
        m_rs = sb("m_rs", [P, CH])
        m_hc = sb("m_hc", [P, CH, C])
        z3 = sb("z3", [P, CH, C])
        z3hl = sb("z3hl", [P, CH, 2, C], F32R)
        z3T = sb("z3T", [128, NT], F32R)
        routeT = sb("routeT", [NE, NT])
        lg = sb("lg", [P, CH, NE])
        top = sb("top", [P, CH, 8])
        idx = sb("idx", [P, CH, 8], U32)
        gap = sb("gap", [P, CH])
        th = sb("th", [P, CH])
        p12 = sb("p12", [P, CH, 2])
        hot = sb("hot", [P, CH, 2, NE])
        hot_p = sb("hot_p", [P, CH, 2, NE])
        w = sb("w", [P, CH, NE])
        whl = sb("whl", [P, CH, 2, NE], F32R)
        wT = sb("wT", [128, NT], F32R)
        eg = [sb(f"eg{k}", [EH, NT]) for k in range(4)]
        y_ev = [sb(f"y_ev{k}", [128, NT]) for k in range(2)]
        yg = [sb(f"yg{k}", [128, NT]) for k in range(NP)]
        sum0 = sb("sum0", [128, NT])
        sum1 = sb("sum1", [128, NT])
        sum_all = sb("sum_all", [128, NT])
        o_half = sb("o_half", [P, CH, C])
        o_sb = sb("o_sb", [P, CH, C])

        x_in = sem("x_in")
        out_stored = sem("out_stored")
        conv_w_in = sem("conv_w_in")
        attn_w_in = sem("attn_w_in")
        mlp_w_in = sem("mlp_w_in")
        ffn_w_in = sem("ffn_w_in")
        consts = sem("consts")
        prep_pe = sem("prep_pe")
        prep_dve = sem("prep_dve")
        S = {n: sem("s_" + n) for part in (PE_DONE, ACT_DONE, DVE_DONE, POOL_DONE) for n in part.split()}
        ps_h = [sem(f"ps_h{e}") for e in range(NE)]
        gelu = [sem(f"gelu{e}") for e in range(NE)]
        ps_y = [sem(f"ps_y{j}") for j in range(NP)]
        ps_wb = [sem(f"ps_wb{j}") for j in range(NP)]
        yev = [sem(f"yev{j}") for j in range(NP)]
        gated = [sem(f"gated{j}") for j in range(NP)]

        PE_PREP = ["filtT", "wxT", "wvT", "ln_bx", "b1m", "eb1", "br", "wvo", "u", "wqk", "u_bias",
                   "bqk_row", "bqk_col"]
        DVE_PREP = ["filtT", "wc32", "wc_hi", "wc_lo", "wxT2", "wvT", "bxg", "b1m", "eb1", "br",
                    "w1_32", "w1_hi", "w1_lo", "ew1_32", "ew1_hi", "ew1_lo", "wr32", "wr_hi", "wr_lo",
                    "sel", "bx_heads", "wvo", "u_lo", "u_hi", "wqk32", "wqk_hi", "wqk_lo",
                    "u_bias", "bqk_row", "bqk_col"]

        def place(names, n):
            return names.index(n) + 1

        def freed(engine, done, b):
            if not (isinstance(b, int) and b == 0):
                engine.wait_ge(done, b)

        def plain(engine):
            engine.wait_ge(consts, 18)

        def cols(b, n=NT):
            return b[:, 0:n]

        def chunk(t, c):
            return t[:, c * P:(c + 1) * P]

        def row3(b, n, p=P):
            return b[0:p, 0:CH * n].rearrange("p (c n) -> p c n", c=CH)

        def each(t, n=C):
            return t.unsqueeze(2).to_broadcast([P, CH, n])

        CONV_DMAS, ATTN_DMAS, MLP_DMAS, FFN_DMAS = 16 * 3, 16 * 10, 16 * 8, 16 * 12

        LAST = 3
        FULL = LAST + 1

        def run(engine, step, after_first=None):
            for i in range(FULL):
                step(i, *(i - n if i >= n else None for n in (1, 2, 3)))
                if i == 0 and after_first is not None:
                    after_first()
            with engine.Fori(FULL, NB) as i:
                step(i, i - 1, i - 2, i - 3)
            for i in range(NB, NB + LAST):
                step(None, *(i - n if i - n < NB else None for n in (1, 2, 3)))

        block = ctx.enter_context(nc.Block())

        @block.sync
        def _(sp):
            x_dram = a["x"].rearrange("b (c p) d -> b p c d", p=128)
            out_dram = out.rearrange("b (c p) k -> b p c k", p=P)

            def load(b):
                sp.wait_ge(S["ps_xT"], b)
                sp.dma_start(x_sb[:], x_dram[b]).then_inc(x_in, 16)

            def store(b):
                sp.wait_ge(S["o"], b + 1)
                sp.dma_start(out_dram[b], o_sb[:]).then_inc(out_stored, 16)

            sp.dma_start(x_sb[:], x_dram[0]).then_inc(x_in, 16)
            sp.dma_start(wk_sb[:], a["tok_W_k"].rearrange("(f d) k -> d f k", d=D)).then_inc(conv_w_in, 16)
            sp.dma_start(w1_raw[0:C, :], a["attn_W1"]).then_inc(mlp_w_in, 16)
            sp.dma_start(w1_raw[C:128, :], a["attn_W1"]).then_inc(mlp_w_in, 16)
            sp.dma_start(w2_sb[:], a["attn_W2"].rearrange("(k p) c -> p k c", p=128)).then_inc(mlp_w_in, 16)
            ew1_src = a["ffn_W1"].rearrange("e c h -> c e h")
            sp.dma_start(ew1_raw[0:C, :, :], ew1_src).then_inc(ffn_w_in, 16)
            sp.dma_start(ew1_raw[C:128, :, :], ew1_src).then_inc(ffn_w_in, 16)
            sp.dma_start(ew2[:], a["ffn_W2"].rearrange("e h c -> h e c")).then_inc(ffn_w_in, 16)
            with sp.Fori(1, LAST + 2) as b:
                load(b)
            with sp.Fori(LAST + 2, NB) as b:
                store(b - LAST - 2)
                load(b)
            with sp.Fori(NB - LAST - 2, NB) as b:
                store(b)
            sp.wait_ge(out_stored, 16 * NB)

        @block.gpsimd
        def _(pool):
            pool.memset(ident[:], 0.0).then_inc(consts, 1)
            pool.memset(minus_half[:], -0.5).then_inc(consts, 1)
            pool.memset(ones11[:], 1.0).then_inc(consts, 1)
            pool.memset(sel32[:], 0.0).then_inc(consts, 1)
            pool.memset(head_rows[:], 1.0).then_inc(consts, 1)
            pool.memset(head_mask[:], 1.0).then_inc(consts, 1)
            pool.memset(wT[:].bitcast(F32), 0.0).then_inc(consts, 1)
            pool.memset(b2m_col[:], 0.0).then_inc(consts, 1)
            pool.iota(iota8[:], [[1, NE]], base=0, channel_multiplier=0,
                      allow_small_or_imprecise_dtypes=True).then_inc(consts, 1)
            pool.wait_ge(consts, 1)
            pool.affine_select(out=ident[:], in_=ident[:], compare_op=ALU.not_equal, fill=1.0, base=0,
                               pattern=[[-1, 128]], channel_multiplier=1).then_inc(consts, 1)
            pool.wait_ge(consts, 9)
            for n, off in enumerate((0, NE)):
                if n:
                    pool.wait_ge(consts, 11)
                pool.affine_select(out=sel32[:], in_=sel32[:], compare_op=ALU.not_equal, fill=1.0,
                                   base=-off, pattern=[[-2, NP], [-1, 2], [0, C]],
                                   channel_multiplier=1).then_inc(consts, 1)
            pool.affine_select(out=head_rows[:], in_=head_rows[:], compare_op=ALU.is_ge, fill=0.0, base=0,
                               pattern=[[-KR, H], [1, HR]], channel_multiplier=0).then_inc(consts, 1)
            for s in range(2):
                pool.wait_ge(consts, 13 + s)
                m = head_mask[s * C:(s + 1) * C, :, :]
                pool.affine_select(out=m, in_=m, compare_op=ALU.is_ge, fill=0.0, base=-KR * s,
                                   pattern=[[-2 * KR, H // 2], [1, HR]], channel_multiplier=0).then_inc(consts, 1)
            pool.wait_ge(consts, 15)
            pool.affine_select(out=head_rows[:], in_=head_rows[:], compare_op=ALU.is_ge, fill=0.0,
                               base=KR - 1, pattern=[[KR, H], [-1, HR]], channel_multiplier=0).then_inc(consts, 1)
            for s in range(2):
                pool.wait_ge(consts, 16 + s)
                m = head_mask[s * C:(s + 1) * C, :, :]
                pool.affine_select(out=m, in_=m, compare_op=ALU.is_ge, fill=0.0, base=KR * s + KR - 1,
                                   pattern=[[2 * KR, H // 2], [-1, HR]], channel_multiplier=0).then_inc(consts, 1)
            pool.wait_ge(consts, 18)

            def step(A, B, M, E):
                if B is not None:
                    pool.wait_ge(S["b_var"], B + 1)
                    freed(pool, S["z2"], B)
                    pool.tensor_tensor(b_rs[:], b_var[:], minus_half[0:P, 0:CH], ALU.pow).then_inc(S["b_rstd"], 1)
                    pool.wait_ge(S["fx"], B + 1)
                    freed(pool, S["m_half"], B)
                    pool.tensor_tensor(fxh[:], fx[:], h1[:], ALU.add).then_inc(S["fxh"], 1)
                if E is not None:
                    pool.wait_ge(gated[0], E + 1)
                    pool.wait_ge(gated[1], E + 1)
                    freed(pool, S["sum_all"], E)
                    pool.tensor_tensor(sum0[:], yg[0][:], yg[1][:], ALU.add).then_inc(S["sum0"], 1)
                if M is not None:
                    pool.wait_ge(S["m_var"], M + 1)
                    freed(pool, S["z3"], M)
                    pool.tensor_tensor(m_rs[:], m_var[:], minus_half[0:P, 0:CH], ALU.pow).then_inc(S["m_rstd"], 1)
                if A is not None:
                    pool.wait_ge(S["a_var"], A + 1)
                    freed(pool, S["z"], A)
                    freed(pool, S["z_res0"], A)
                    pool.tensor_tensor(a_rs[:], a_var[:],
                                       minus_half[0:P, 0:2 * CH].rearrange("p (a c) -> p a c", a=2),
                                       ALU.pow).then_inc(S["a_rstd"], 1)
                    pool.wait_ge(S["a_hc"], A + 1)
                    pool.wait_ge(S["a_rstd"], A + 1)
                    freed(pool, S["z_res"], A)
                    pool.tensor_tensor(zr0[:], hc[:], each(a_rs[:, 0, :]), ALU.mult).then_inc(S["z_res0"], 1)
                    pool.wait_ge(S["z_res0"], A + 1)
                    freed(pool, S["fx"], A)
                    if isinstance(A, int) and A == 0:
                        pool.wait_ge(attn_w_in, ATTN_DMAS)
                    pool.tensor_tensor(zr[:], zr0[:], bo_rows[0:P, :].unsqueeze(1).to_broadcast([P, CH, C]),
                                       ALU.add).then_inc(S["z_res"], 1)
                if E is not None:
                    pool.wait_ge(gated[2], E + 1)
                    pool.wait_ge(gated[3], E + 1)
                    pool.tensor_tensor(sum1[:], yg[2][:], yg[3][:], ALU.add).then_inc(S["sum1"], 1)
                    pool.wait_ge(S["sum0"], E + 1)
                    pool.wait_ge(S["sum1"], E + 1)
                    freed(pool, S["ps_out"], E)
                    pool.tensor_tensor(sum_all[:], sum0[:], sum1[:], ALU.add).then_inc(S["sum_all"], 1)

            run(pool, step)

        @block.scalar
        def _(act):
            def column(v):
                return v.rearrange("(p o) -> p o", o=1)

            act.dma_start(filt_sb[:], a["tok_filt"]).then_inc(conv_w_in, 16)
            act.dma_start(bk_col[:], column(a["tok_b_k"])).then_inc(conv_w_in, 16)
            act.dma_start(wx_sb[:], a["attn_Wx"]).then_inc(attn_w_in, 16)
            act.dma_start(wkq_sb[:, 0:KR], a["attn_Wk"]).then_inc(attn_w_in, 16)
            act.dma_start(wkq_sb[:, KR:2 * KR], a["attn_Wq"]).then_inc(attn_w_in, 16)
            act.dma_start(wv_sb[:], a["attn_Wv"]).then_inc(attn_w_in, 16)
            act.dma_start(wo_sb[:], a["attn_Wo"].rearrange("(h d) c -> d h c", d=DH)).then_inc(attn_w_in, 16)
            act.dma_start(bxT[:], a["attn_bx"].rearrange("(h d) -> d h", d=DH), allow_slow_non_contiguous=True).then_inc(attn_w_in, 16)
            act.dma_start(g1_col[0:C, :], column(a["attn_ln1_g"])).then_inc(attn_w_in, 16)
            act.dma_start(g1_col[C:128, :], column(a["attn_ln1_g"])).then_inc(attn_w_in, 16)
            act.dma_start(b1_col[:], column(a["attn_ln1_b"])).then_inc(attn_w_in, 16)
            act.dma_start(bo_rows[:], a["attn_bo"].unsqueeze(0).to_broadcast([128, C])).then_inc(attn_w_in, 16)
            act.dma_start(b2ln_col[:], column(a["attn_ln2_b"])).then_inc(mlp_w_in, 16)
            act.dma_start(g2_col[0:C, :], column(a["attn_ln2_g"])).then_inc(mlp_w_in, 16)
            act.dma_start(g2_col[C:128, :], column(a["attn_ln2_g"])).then_inc(mlp_w_in, 16)
            act.dma_start(b1mT[:], a["attn_b1"].rearrange("(k p) -> p k", p=128), allow_slow_non_contiguous=True).then_inc(mlp_w_in, 16)
            act.wait_ge(consts, 8)
            act.dma_start(b2m_col[0:C, :], column(a["attn_b2"])).then_inc(mlp_w_in, 16)
            act.dma_start(gam_col[0:C, :], column(a["ffn_gamma"])).then_inc(ffn_w_in, 16)
            act.dma_start(gam_col[C:128, :], column(a["ffn_gamma"])).then_inc(ffn_w_in, 16)
            act.dma_start(bet_col[:], column(a["ffn_beta"])).then_inc(ffn_w_in, 16)
            act.dma_start(wr_raw[0:C, :], a["ffn_Wr"]).then_inc(ffn_w_in, 16)
            act.dma_start(wr_raw[C:128, :], a["ffn_Wr"]).then_inc(ffn_w_in, 16)
            act.dma_start(brc[:], column(a["ffn_br"])).then_inc(ffn_w_in, 16)
            act.dma_start(eb1T[:], a["ffn_b1"].rearrange("e h -> h e"), allow_slow_non_contiguous=True).then_inc(ffn_w_in, 16)
            for s in range(2):
                act.dma_start(eb2[s * C:(s + 1) * C, :],
                              a["ffn_b2"].rearrange("(j s) c -> s c j", s=2)[s], allow_slow_non_contiguous=True).then_inc(ffn_w_in, 16)

            def step(A, B, M, E):
                if B is not None:
                    act.wait_ge(S["ps_zT"], B + 1)
                    freed(act, S["ps_L"], B)
                    act.activation(zT[:], cols(B1), ACT.Copy).then_inc(S["zT"], 1)
                if E is not None:
                    act.wait_ge(S["ps_z3T"], E + 1)
                    freed(act, ps_h[NE - 1], E)
                    act.activation(z3T[:], cols(BH0), ACT.Copy).then_inc(S["z3T"], 1)
                    act.wait_ge(S["h2"], E + 1)
                    freed(act, S["o_half"], E)
                    act.activation(h2_kept[:], h2[:], ACT.Copy).then_inc(S["h2_kept"], 1)
                if A is not None:
                    act.wait_ge(S["ps_xT"], A + 1)
                    freed(act, S["ps_conv"], A)
                    act.activation(x_hi[:], BA[:, 0:L], ACT.Copy).then_inc(S["x_hi"], 1)
                if B is not None:
                    act.wait_ge(S["ps_L"], B + 1)
                    freed(act, S["ps_k"], B)
                    act.activation(kq[:], B2[0:2 * HR, 0:NT], ACT.Identity, bias=bqk_col[:, 0:1]).then_inc(S["L"], 1)
                if E is not None:
                    act.wait_ge(S["ps_route"], E + 1)
                    freed(act, S["ps_lg"], E)
                    act.activation(routeT[:], BH1[0:NE, 0:NT], ACT.Identity, bias=br_col[:, 0:1]).then_inc(S["route"], 1)
                if M is not None:
                    act.wait_ge(S["ps_z2T"], M + 1)
                    freed(act, S["ps_m1"], M)
                    act.activation(z2T[:], cols(BM), ACT.Copy).then_inc(S["z2T"], 1)
                if B is not None:
                    act.wait_ge(S["k_negmax"], B + 1)
                    act.wait_ge(S["L"], B + 1)
                    freed(act, S["k_rden"], B)
                    act.activation(kq[0:HR, :], kq[0:HR, :], ACT.Exp, bias=k_negmax[:, 0:1],
                                   accum_out=k_den[:, 0:1]).then_inc(S["k_exp"], 1)
                    act.wait_ge(S["q_sub"], B + 1)
                    freed(act, S["q_norm"], B)
                    act.activation(q_e[:], q_sub[:], ACT.Exp).then_inc(S["q_exp"], 1)
                if E is not None:
                    hidden(E, 0)
                    hidden(E, 1)
                if M is not None:
                    mlp_hidden(M, 0)
                if E is not None:
                    act.wait_ge(S["gap"], E + 1)
                    freed(act, S["p"], E)
                    act.activation(th[:], gap[:], ACT.Tanh, scale=0.5).then_inc(S["th"], 1)
                if A is not None:
                    act.wait_ge(S["ps_conv"], A + 1)
                    freed(act, S["pre"], A)
                    act.activation(late_taps[:], BA[C:128, HALF:HALF + NT], ACT.Copy).then_inc(S["conv_hi_taps"], 1)
                if E is not None:
                    hidden(E, 2)
                    hidden(E, 3)
                if M is not None:
                    mlp_hidden(M, 1)
                if B is not None:
                    act.wait_ge(S["ps_qT"], B + 1)
                    freed(act, S["ps_at"], B)
                    act.activation(qT[:], B1[0:3 * HR, 0:NT], ACT.Copy).then_inc(S["qT"], 1)
                if E is not None:
                    act.wait_ge(S["ps_w"], E + 1)
                    freed(act, ps_wb[NP - 1], E)
                    act.activation(wT[0:2 * NE, :], BW[0:2 * NE, 0:NT], ACT.Copy).then_inc(S["wT"], 1)
                    outputs(E, 0)
                    hidden(E, 4)
                    hidden(E, 5)
                if M is not None:
                    act.wait_ge(S["ps_m2"], M + 1)
                    freed(act, S["ps_mT"], M)
                    act.activation(mF[:], cols(BM), ACT.Identity, bias=b2m_col[:, 0:1]).then_inc(S["mlp_F"], 1)
                if E is not None:
                    outputs(E, 1)
                if B is not None:
                    act.wait_ge(S["z2"], B + 1)
                    freed(act, S["ps_z2T"], B)
                    act.activation(z2hl[:, :, 0, :], z2[:], ACT.Copy).then_inc(S["z2_hi"], 1)
                if A is not None:
                    act.wait_ge(S["ps_pre"], A + 1)
                    freed(act, S["fxh"], A)
                    act.activation(h1[:], row3(BA, C), ACT.Relu).then_inc(S["h1"], 1)
                if E is not None:
                    hidden(E, 6)
                    hidden(E, 7)
                    outputs(E, 2)
                if M is not None:
                    act.wait_ge(S["z3"], M + 1)
                    freed(act, S["ps_z3T"], M)
                    act.activation(z3hl[:, :, 0, :], z3[:], ACT.Copy).then_inc(S["z3_hi"], 1)
                if A is not None:
                    act.wait_ge(S["z"], A + 1)
                    freed(act, S["ps_zT"], A)
                    act.activation(zhl[:, :, 0, :], z[:], ACT.Copy).then_inc(S["z_hi"], 1)
                if E is not None:
                    outputs(E, 3)

            def hidden(E, e):
                act.wait_ge(ps_h[e], E + 1)
                if e < 4:
                    freed(act, ps_y[(e + 4) // 2], E)
                else:
                    act.wait_ge(ps_y[(e - 4) // 2], E + 1)
                act.activation(eg[e % 4][:], cols(BH[e % 2]), ACT.Gelu, bias=eb1[:, e:e + 1]).then_inc(gelu[e], 1)

            def mlp_hidden(M, k):
                act.wait_ge(S["ps_m1"] if k else S["ps_m0"], M + 1)
                freed(act, S["ps_m2"], M)
                act.activation(mg[k][:], cols(BM), ACT.Gelu, bias=b1m[:, k:k + 1]).then_inc(S["mlp_g1"] if k else S["mlp_g0"], 1)

            def outputs(E, j):
                act.wait_ge(ps_y[j], E + 1)
                if j < 2:
                    freed(act, gated[j + 2], E)
                else:
                    act.wait_ge(gated[j - 2], E + 1)
                act.activation(y_ev[j % 2][:], cols(BY), ACT.Identity, bias=eb2[:, j:j + 1]).then_inc(yev[j], 1)

            def prepared():
                act.wait_ge(prep_dve, len(DVE_PREP))
                act.wait_ge(mlp_w_in, MLP_DMAS)
                act.wait_ge(ffn_w_in, FFN_DMAS)
                act.wait_ge(consts, 18)

            run(act, step, prepared)

        @block.vector
        def _(dve):
            def prep(ins):
                ins.then_inc(prep_dve, 1)

            dve.wait_ge(prep_pe, place(PE_PREP, "filtT"))
            prep(dve.tensor_copy(filtT[:], BH0[0:D, 0:TAPS]))
            dve.wait_ge(conv_w_in, CONV_DMAS)
            dve.wait_ge(prep_dve, place(DVE_PREP, "filtT"))
            prep(dve.tensor_tensor(wc32[:].rearrange("d t h k -> d h t k"),
                                   wk_sb[:].rearrange("d (h t) k -> d h t k", h=2),
                                   filtT[:].rearrange("d (h t) -> d h t", h=2).unsqueeze(3)
                                   .to_broadcast([D, 2, HALF, C]), ALU.mult))
            dve.wait_ge(prep_dve, place(DVE_PREP, "wc32"))
            prep(dve.tensor_copy(wc_hi[:], wc32[:].rearrange("d t h k -> d t (h k)")))
            dve.wait_ge(prep_dve, place(DVE_PREP, "wc_hi"))
            prep(dve.tensor_tensor(wc_lo[:], wc32[:].rearrange("d t h k -> d t (h k)"),
                                   wc_hi[:].bitcast(F32), ALU.subtract))

            def prepare():
                def made(n):
                    dve.wait_ge(prep_dve, place(DVE_PREP, n))

                def summed(n):
                    dve.wait_ge(prep_pe, place(PE_PREP, n))

                dve.wait_ge(attn_w_in, ATTN_DMAS)
                dve.wait_ge(mlp_w_in, MLP_DMAS)
                dve.wait_ge(ffn_w_in, FFN_DMAS)
                dve.wait_ge(consts, 18)
                summed("wxT")
                prep(dve.tensor_copy(wxT2[:], B1[0:DH, 0:H * C].rearrange("d (h c) -> d h c", h=H).unsqueeze(2)
                                     .to_broadcast([DH, H, 2, C])))
                summed("wvT")
                prep(dve.tensor_copy(wvT[:], B2[0:DH, 0:DH]))
                summed("ln_bx")
                prep(dve.tensor_tensor(bxg[:], BM[0:DH, 0:H], bxT[:], ALU.add))
                summed("b1m")
                prep(dve.tensor_tensor(b1m[:], BH0[:, 0:2], b1mT[:], ALU.add))
                summed("eb1")
                prep(dve.tensor_tensor(eb1[:], BH1[:, 0:NE], eb1T[:], ALU.add))
                summed("br")
                prep(dve.tensor_tensor(br_col[:], BY[0:NE, 0:1], brc[:], ALU.add))
                prep(dve.tensor_scalar(w1_32[:], w1_raw[:], g2_col[:, 0:1], None, ALU.mult))
                made("w1_32")
                prep(dve.tensor_copy(w1_hi[:], w1_32[:]))
                made("w1_hi")
                prep(dve.tensor_tensor(w1_lo[:], w1_32[:], w1_hi[:].bitcast(F32), ALU.subtract))
                prep(dve.tensor_scalar(ew1_32[:], ew1_raw[:].rearrange("p e h -> p (e h)"), gam_col[:, 0:1], None, ALU.mult))
                made("ew1_32")
                prep(dve.tensor_copy(ew1_hi[:], ew1_32[:]))
                made("ew1_hi")
                prep(dve.tensor_tensor(ew1_lo[:], ew1_32[:], ew1_hi[:].bitcast(F32), ALU.subtract))
                prep(dve.tensor_scalar(wr32[:], wr_raw[:], gam_col[:, 0:1], None, ALU.mult))
                made("wr32")
                prep(dve.tensor_copy(wr_hi[:], wr32[:]))
                made("wr_hi")
                prep(dve.tensor_tensor(wr_lo[:], wr32[:], wr_hi[:].bitcast(F32), ALU.subtract))
                prep(dve.tensor_copy(sel[:], sel32[:].rearrange("p j s c -> p j (s c)")))
                made("bxg")
                prep(dve.tensor_tensor(bx_heads[:], head_rows[:], bxg[:].unsqueeze(2).to_broadcast([DH, H, HR]), ALU.mult))
                summed("wvo")
                prep(dve.tensor_copy(wvo[:], BW[0:DH, 0:H * C].rearrange("d (h c) -> d h c", h=H)))
                summed("u")
                for s in range(2):
                    prep(dve.tensor_scalar(u_pair[s * C:(s + 1) * C, :, :],
                                           B1[s * C:(s + 1) * C, 0:H * C].rearrange("p (j s c) -> p j s c", s=2, c=C)[:, :, s, :],
                                           g1_col[s * C:(s + 1) * C, 0:1], None, ALU.mult))
                summed("wqk")
                prep(dve.tensor_scalar(wqk32[:].rearrange("p (t h r) -> p t h r", t=2, h=H),
                                       B2[:, 0:2 * HR].rearrange("p (h t r) -> p t h r", t=2, h=H),
                                       g1_col[:, 0:1], None, ALU.mult))
                made("wqk32")
                prep(dve.tensor_copy(wqk_hi[:], wqk32[:]))
                made("wqk_hi")
                prep(dve.tensor_tensor(wqk_lo[:], wqk32[:], wqk_hi[:].bitcast(F32), ALU.subtract))
                summed("u_bias")
                prep(dve.tensor_copy(u_bias[:], BM[0:HR, 0:C]))
                summed("bqk_row")
                prep(dve.tensor_copy(bqk_row[:].rearrange("p (t h r) -> p t h r", t=2, h=H),
                                     BH0[0:1, 0:2 * HR].rearrange("p (h t r) -> p t h r", t=2, h=H)))
                summed("bqk_col")
                prep(dve.tensor_copy(bqk_col[:], BH1[0:2 * HR, 0:1]))

            def moments(src, st, mv, stats_done, mv_done, b):
                freed(dve, mv_done, b)
                for c in range(CH):
                    ins = dve.bn_stats(st[:, c, :], src[:, c, :])
                ins.then_inc(stats_done, 1)
                plain(dve)
                dve.wait_ge(stats_done, b + 1)
                for c in range(CH):
                    ins = dve.bn_aggr(mv[:, c, :], st[:, c, :])
                ins.then_inc(mv_done, 1)

            def step(A, B, M, E):
                if A is not None:
                    dve.wait_ge(S["x_hi"], A + 1)
                    freed(dve, S["ps_conv"], A)
                    dve.tensor_tensor(x_lo[:], BA[:, 0:L], x_hi[:].bitcast(F32), ALU.subtract).then_inc(S["x_lo"], 1)
                if B is not None:
                    dve.wait_ge(S["L"], B + 1)
                    freed(dve, S["k_exp"], B)
                    dve.tensor_reduce(k_negmax[:], kq[0:HR, :], AX_X, ALU.max, negate=True).then_inc(S["k_negmax"], 1)
                    dve.wait_ge(S["ps_q"], B + 1)
                    freed(dve, S["q_sub"], B)
                    q_ps = B1[0:P, 0:CH * HR].rearrange("p (g r) -> p g r", r=KR)
                    dve.tensor_reduce(q_max[:], q_ps, AX_X, ALU.max).then_inc(S["q_max"], 1)
                    dve.wait_ge(S["q_max"], B + 1)
                    freed(dve, S["q_exp"], B)
                    dve.tensor_tensor(q_sub[:], q_ps, q_max[:].unsqueeze(2).to_broadcast([P, CH * H, KR]),
                                      ALU.subtract).then_inc(S["q_sub"], 1)
                if E is not None:
                    dve.wait_ge(S["ps_lg"], E + 1)
                    freed(dve, S["idx"], E)
                    dve.tensor_copy(lg[:], row3(BW, NE)).then_inc(S["lg"], 1)
                    plain(dve)
                    dve.wait_ge(S["lg"], E + 1)
                    freed(dve, S["gap"], E)
                    for c in range(CH):
                        ins = dve.max(top[:, c, :], lg[:, c, :])
                    ins.then_inc(S["top"], 1)
                    plain(dve)
                    dve.wait_ge(S["top"], E + 1)
                    freed(dve, S["hot"], E)
                    for c in range(CH):
                        ins = dve.max_index(idx[:, c, :], top[:, c, :], lg[:, c, :])
                    ins.then_inc(S["idx"], 1)
                    freed(dve, S["th"], E)
                    dve.tensor_tensor(gap[:], top[:, :, 1], top[:, :, 0], ALU.subtract).then_inc(S["gap"], 1)
                    dve.wait_ge(S["idx"], E + 1)
                    freed(dve, S["hot_p"], E)
                    dve.tensor_tensor(hot[:], idx[:, :, 0:2].unsqueeze(3).to_broadcast([P, CH, 2, NE]),
                                      iota8[0:P, :].unsqueeze(1).unsqueeze(1).to_broadcast([P, CH, 2, NE]),
                                      ALU.is_equal).then_inc(S["hot"], 1)
                if B is not None:
                    dve.wait_ge(S["q_exp"], B + 1)
                    freed(dve, S["q_rec"], B)
                    dve.tensor_reduce(q_sum[:], q_e[:], AX_X, ALU.add).then_inc(S["q_sum"], 1)
                    dve.wait_ge(S["ps_k"], B + 1)
                    freed(dve, S["ps_G"], B)
                    dve.tensor_copy(EkT[:], row3(B2, HR)).then_inc(S["EkT"], 1)
                    dve.wait_ge(S["q_sum"], B + 1)
                    freed(dve, S["q_norm"], B)
                    dve.reciprocal(q_rec[:], q_sum[:]).then_inc(S["q_rec"], 1)
                    dve.wait_ge(S["k_exp"], B + 1)
                    freed(dve, S["G_norm"], B)
                    dve.reciprocal(k_rden[:], k_den[:]).then_inc(S["k_rden"], 1)
                    dve.wait_ge(S["q_rec"], B + 1)
                    freed(dve, S["q_lo"], B)
                    dve.tensor_tensor(q_n[:].rearrange("p c (h r) -> p (c h) r", r=KR), q_e[:],
                                      q_rec[:].unsqueeze(2).to_broadcast([P, CH * H, KR]),
                                      ALU.mult).then_inc(S["q_norm"], 1)
                    dve.wait_ge(S["q_norm"], B + 1)
                    freed(dve, S["ps_qT"], B)
                    dve.tensor_copy(qhl[:, :, 0, :], q_n[:])
                    dve.tensor_copy(qhl[:, :, 2, :], q_n[:]).then_inc(S["q_hi"], 1)
                    dve.wait_ge(S["q_hi"], B + 1)
                    dve.tensor_tensor(qhl[:, :, 1, :], q_n[:], qhl[:, :, 0, :].bitcast(F32),
                                      ALU.subtract).then_inc(S["q_lo"], 1)
                    dve.wait_ge(S["ps_G"], B + 1)
                    dve.wait_ge(S["k_rden"], B + 1)
                    freed(dve, S["ps_GT"], B)
                    dve.tensor_scalar(Gd[:], B2[0:HR, 0:C].unsqueeze(1).to_broadcast([HR, 2, C]),
                                      k_rden[:, 0:1], None, ALU.mult).then_inc(S["G_norm"], 1)
                if E is not None:
                    dve.wait_ge(S["th"], E + 1)
                    freed(dve, S["hot_p"], E)
                    dve.tensor_scalar(p12[:, :, 0], th[:], -0.5, 0.5, ALU.mult, ALU.add)
                    dve.tensor_scalar(p12[:, :, 1], th[:], 0.5, 0.5, ALU.mult, ALU.add).then_inc(S["p"], 1)
                    dve.wait_ge(S["p"], E + 1)
                    dve.wait_ge(S["hot"], E + 1)
                    freed(dve, S["w"], E)
                    dve.tensor_tensor(hot_p[:], hot[:], p12[:].unsqueeze(3).to_broadcast([P, CH, 2, NE]),
                                      ALU.mult).then_inc(S["hot_p"], 1)
                    dve.wait_ge(S["hot_p"], E + 1)
                    freed(dve, S["w_lo"], E)
                    dve.tensor_tensor(w[:], hot_p[:, :, 0, :], hot_p[:, :, 1, :], ALU.add).then_inc(S["w"], 1)
                    dve.wait_ge(S["w"], E + 1)
                    freed(dve, S["ps_w"], E)
                    dve.tensor_copy(whl[:, :, 0, :], w[:]).then_inc(S["w_hi"], 1)
                    dve.wait_ge(S["w_hi"], E + 1)
                    dve.tensor_tensor(whl[:, :, 1, :], w[:], whl[:, :, 0, :].bitcast(F32),
                                      ALU.subtract).then_inc(S["w_lo"], 1)
                if B is not None:
                    dve.wait_ge(S["ps_GT"], B + 1)
                    freed(dve, S["ps_M"], B)
                    dve.tensor_tensor(Gx[:], B2[:, 0:HR].unsqueeze(1).to_broadcast([128, H // 2, HR]),
                                      head_mask[:], ALU.mult).then_inc(S["G_heads"], 1)
                if A is not None:
                    dve.wait_ge(S["conv_hi_taps"], A + 1)
                    freed(dve, S["ps_pre"], A)
                    dve.scalar_tensor_tensor(out=pre[:], in0=BA[0:C, 0:NT], scalar=bk_col[:, 0:1],
                                             in1=late_taps[:], op0=ALU.add, op1=ALU.add).then_inc(S["pre"], 1)
                if B is not None:
                    dve.wait_ge(S["ps_M"], B + 1)
                    freed(dve, S["M_stack"], B)
                    dve.tensor_tensor(Mf[:], B2[0:HR, 0:C], u_bias[:], ALU.add).then_inc(S["M_sum"], 1)
                    dve.wait_ge(S["M_sum"], B + 1)
                    freed(dve, S["ps_at"], B)
                    dve.tensor_copy(M3[0:HR, :], Mf[:]).then_inc(S["M_hi"], 1)
                    dve.tensor_copy(M3[HR:2 * HR, :], Mf[:])
                    dve.wait_ge(S["M_hi"], B + 1)
                    dve.tensor_tensor(M3[2 * HR:3 * HR, :], Mf[:], M3[0:HR, :].bitcast(F32),
                                      ALU.subtract).then_inc(S["M_stack"], 1)
                if E is not None:
                    gate(E, 0)
                if B is not None:
                    dve.wait_ge(S["ps_at"], B + 1)
                    dve.wait_ge(S["z_res"], B + 1)
                    freed(dve, S["fxh"], B)
                    dve.tensor_tensor(fx[:], row3(B2, C), zr[:], ALU.add).then_inc(S["fx"], 1)
                    dve.wait_ge(S["fx"], B + 1)
                    freed(dve, S["b_hc"], B)
                    moments(fx, b_st, b_mv, S["b_stats"], S["b_mv"], B)
                    dve.wait_ge(S["b_mv"], B + 1)
                    freed(dve, S["b_rstd"], B)
                    dve.tensor_scalar(b_var[:], b_mv[:, :, 1], EPS, None, ALU.add).then_inc(S["b_var"], 1)
                    freed(dve, S["z2"], B)
                    dve.tensor_tensor(b_hc[:], fx[:], each(b_mv[:, :, 0]), ALU.subtract).then_inc(S["b_hc"], 1)
                if E is not None:
                    gate(E, 1)
                if B is not None:
                    dve.wait_ge(S["b_rstd"], B + 1)
                    dve.wait_ge(S["b_hc"], B + 1)
                    freed(dve, S["z2_lo"], B)
                    dve.tensor_tensor(z2[:], b_hc[:], each(b_rs[:]), ALU.mult).then_inc(S["z2"], 1)
                if M is not None:
                    dve.wait_ge(S["ps_mT"], M + 1)
                    dve.wait_ge(S["fxh"], M + 1)
                    freed(dve, S["h2"], M)
                    m_ps = row3(BM, 2 * C)
                    dve.tensor_tensor(m_half[:], m_ps[:, :, 0:C], fxh[:], ALU.add).then_inc(S["m_half"], 1)
                    dve.wait_ge(S["m_half"], M + 1)
                    freed(dve, S["h2_kept"], M)
                    freed(dve, S["m_hc"], M)
                    dve.tensor_tensor(h2[:], m_ps[:, :, C:2 * C], m_half[:], ALU.add).then_inc(S["h2"], 1)
                if B is not None:
                    dve.wait_ge(S["z2_hi"], B + 1)
                    dve.tensor_tensor(z2hl[:, :, 1, :], z2[:], z2hl[:, :, 0, :].bitcast(F32),
                                      ALU.subtract).then_inc(S["z2_lo"], 1)
                if M is not None:
                    dve.wait_ge(S["h2"], M + 1)
                    moments(h2, m_st, m_mv, S["m_stats"], S["m_mv"], M)
                    dve.wait_ge(S["m_mv"], M + 1)
                    freed(dve, S["m_rstd"], M)
                    dve.tensor_scalar(m_var[:], m_mv[:, :, 1], 1.0 + EPS, EPS * EPS, ALU.mult, ALU.add).then_inc(S["m_var"], 1)
                    freed(dve, S["z3"], M)
                    dve.tensor_tensor(m_hc[:], h2[:], each(m_mv[:, :, 0]), ALU.subtract).then_inc(S["m_hc"], 1)
                if A is not None:
                    dve.wait_ge(S["h1"], A + 1)
                    freed(dve, S["a_hc"], A)
                    moments(h1, a_st, a_mv, S["a_stats"], S["a_mv"], A)
                    dve.wait_ge(S["a_mv"], A + 1)
                    freed(dve, S["a_rstd"], A)
                    dve.tensor_scalar(a_var[:, 0, :], a_mv[:, :, 1], EPS, None, ALU.add)
                    dve.tensor_scalar(a_var[:, 1, :], a_mv[:, :, 1], 1.0 + EPS, EPS * EPS, ALU.mult, ALU.add).then_inc(S["a_var"], 1)
                    freed(dve, S["z_res0"], A)
                    freed(dve, S["z"], A)
                    dve.tensor_tensor(hc[:], h1[:], each(a_mv[:, :, 0]), ALU.subtract).then_inc(S["a_hc"], 1)
                if M is not None:
                    dve.wait_ge(S["m_rstd"], M + 1)
                    dve.wait_ge(S["m_hc"], M + 1)
                    freed(dve, S["z3_lo"], M)
                    dve.tensor_tensor(z3[:], m_hc[:], each(m_rs[:]), ALU.mult).then_inc(S["z3"], 1)
                if E is not None:
                    gate(E, 2)
                if A is not None:
                    dve.wait_ge(S["a_rstd"], A + 1)
                    dve.wait_ge(S["a_hc"], A + 1)
                    freed(dve, S["ps_G"], A)
                    freed(dve, S["z_lo"], A)
                    dve.tensor_tensor(z[:], hc[:], each(a_rs[:, 1, :]), ALU.mult).then_inc(S["z"], 1)
                if M is not None:
                    dve.wait_ge(S["z3_hi"], M + 1)
                    dve.tensor_tensor(z3hl[:, :, 1, :], z3[:], z3hl[:, :, 0, :].bitcast(F32),
                                      ALU.subtract).then_inc(S["z3_lo"], 1)
                if A is not None:
                    dve.wait_ge(S["z_hi"], A + 1)
                    dve.tensor_tensor(zhl[:, :, 1, :], z[:], zhl[:, :, 0, :].bitcast(F32),
                                      ALU.subtract).then_inc(S["z_lo"], 1)
                if E is not None:
                    gate(E, 3)
                    dve.wait_ge(S["ps_out"], E + 1)
                    dve.wait_ge(S["h2_kept"], E + 1)
                    freed(dve, S["o"], E)
                    o_ps = row3(BY, 2 * C)
                    dve.tensor_tensor(o_half[:], o_ps[:, :, 0:C], h2_kept[:], ALU.add).then_inc(S["o_half"], 1)
                    dve.wait_ge(S["o_half"], E + 1)
                    freed(dve, out_stored, 16 * E)
                    dve.tensor_tensor(o_sb[:], o_ps[:, :, C:2 * C], o_half[:], ALU.add).then_inc(S["o"], 1)

            def gate(E, j):
                dve.wait_ge(yev[j], E + 1)
                dve.wait_ge(ps_wb[j], E + 1)
                freed(dve, S["sum0"] if j < 2 else S["sum1"], E)
                dve.tensor_tensor(yg[j][:], y_ev[j % 2][:], cols(BW), ALU.mult).then_inc(gated[j], 1)

            run(dve, step, prepare)

        @block.tensor
        def _(pe):
            pe.wait_ge(consts, 10)
            pe.wait_ge(conv_w_in, CONV_DMAS)
            pe.transpose(BH0[0:D, 0:TAPS], filt_sb[:], ident[0:TAPS, 0:TAPS]).then_inc(prep_pe, 1)

            def prepare():
                def made(n):
                    pe.wait_ge(prep_dve, place(DVE_PREP, n))

                pe.wait_ge(attn_w_in, ATTN_DMAS)
                for h in range(H):
                    ins = pe.transpose(B1[0:DH, h * C:(h + 1) * C], wx_sb[:, h * DH:(h + 1) * DH], ident[0:C, 0:C])
                ins.then_inc(prep_pe, 1)
                pe.transpose(B2[0:DH, 0:DH], wv_sb[:], ident[0:DH, 0:DH]).then_inc(prep_pe, 1)
                for h in range(H):
                    ins = pe.matmul(BM[0:DH, h:h + 1], wx_sb[:, h * DH:(h + 1) * DH], b1_col[:], start=True, stop=True)
                ins.then_inc(prep_pe, 1)
                pe.wait_ge(mlp_w_in, MLP_DMAS)
                for k in range(2):
                    ins = pe.matmul(BH0[:, k:k + 1], w1_raw[0:C, k * 128:(k + 1) * 128], b2ln_col[:], start=True, stop=True)
                ins.then_inc(prep_pe, 1)
                pe.wait_ge(ffn_w_in, FFN_DMAS)
                for e in range(NE):
                    ins = pe.matmul(BH1[:, e:e + 1], ew1_raw[0:C, e, :], bet_col[:], start=True, stop=True)
                ins.then_inc(prep_pe, 1)
                pe.matmul(BY[0:NE, 0:1], wr_raw[0:C, :], bet_col[:], start=True, stop=True).then_inc(prep_pe, 1)
                made("wvT")
                pe.matmul(BW[0:DH, 0:H * C], wvT[:], wo_sb[:].rearrange("d h c -> d (h c)"),
                          start=True, stop=True).then_inc(prep_pe, 1)
                made("wvo")
                for h in range(H):
                    ins = pe.matmul(B1[:, h * C:(h + 1) * C], wxT2[:, h, :, :].rearrange("d s c -> d (s c)"),
                                    wvo[:, h, :], start=True, stop=True)
                ins.then_inc(prep_pe, 1)
                for h in range(H):
                    ins = pe.matmul(B2[:, h * 2 * KR:(h + 1) * 2 * KR], wxT2[:, h, :, :].rearrange("d s c -> d (s c)"),
                                    wkq_sb[:], start=True, stop=True)
                ins.then_inc(prep_pe, 1)
                for h in range(H):
                    ins = pe.matmul(BM[0:HR, 0:C], bx_heads[:, h, :], wvo[:, h, :], start=(h == 0), stop=(h == H - 1))
                ins.then_inc(prep_pe, 1)
                for h in range(H):
                    ins = pe.matmul(BH0[0:1, h * 2 * KR:(h + 1) * 2 * KR], bxg[:, h:h + 1], wkq_sb[:], start=True, stop=True)
                ins.then_inc(prep_pe, 1)
                made("bqk_row")
                pe.matmul(BH1[0:2 * HR, 0:1], bqk_row[:], ones11[:, 0:1], start=True, stop=True).then_inc(prep_pe, 1)
                made("bqk_col")

            def turn(dst, src, done):
                for c in range(CH):
                    ins = pe.transpose(chunk(dst, c), src[:, c, :, :].rearrange("p s c -> p (s c)").bitcast(F32), ident[0:P, 0:P])
                ins.then_inc(done, 1)

            def in_parts(dst, w_hi, w_lo, data):
                pe.matmul(dst, w_hi, data, start=True, stop=False)
                return pe.matmul(dst, w_lo, data, start=False, stop=True)

            def hidden(E, e):
                if e < 2:
                    pe.wait_ge(S["z3T"] if e == 0 else S["route"], E + 1)
                else:
                    pe.wait_ge(gelu[e - 2], E + 1)
                in_parts(cols(BH[e % 2]), ew1_hi[:, e * EH:(e + 1) * EH], ew1_lo[:, e * EH:(e + 1) * EH],
                         z3T[:]).then_inc(ps_h[e], 1)

            def outputs(E, j):
                pe.wait_ge(gelu[2 * j], E + 1)
                pe.wait_ge(gelu[2 * j + 1], E + 1)
                if j:
                    pe.wait_ge(yev[j - 1], E + 1)
                else:
                    freed(pe, S["o"], E)
                for s in range(2):
                    ins = pe.matmul(BY[s * C:(s + 1) * C, 0:NT], ew2[:, 2 * j + s, :], eg[(2 * j + s) % 4][:],
                                    start=True, stop=True)
                ins.then_inc(ps_y[j], 1)
                if j:
                    pe.wait_ge(gated[j - 1], E + 1)
                else:
                    pe.wait_ge(S["wT"], E + 1)
                pe.matmul(cols(BW), sel[:, j, :], wT[:], start=True, stop=True).then_inc(ps_wb[j], 1)

            def step(A, B, M, E):
                if B is not None:
                    pe.wait_ge(S["z_hi"], B + 1)
                    pe.wait_ge(S["z_lo"], B + 1)
                    freed(pe, S["qT"], B)
                    turn(B1, zhl, S["ps_zT"])
                if E is not None:
                    pe.wait_ge(S["z3_hi"], E + 1)
                    pe.wait_ge(S["z3_lo"], E + 1)
                    freed(pe, gelu[NE - 2], E)
                    turn(BH0, z3hl, S["ps_z3T"])
                if A is not None:
                    pe.wait_ge(x_in, 16 * A + 16)
                    freed(pe, S["h1"], A)
                    for c in range(XC):
                        ins = pe.transpose(BA[:, c * 128:(c + 1) * 128], x_sb[:, c, :], ident[:])
                    ins.then_inc(S["ps_xT"], 1)
                if B is not None:
                    pe.wait_ge(S["zT"], B + 1)
                    freed(pe, S["fx"], B)
                    in_parts(B2[0:2 * HR, 0:NT], wqk_hi[:], wqk_lo[:], zT[:]).then_inc(S["ps_L"], 1)
                if E is not None:
                    pe.wait_ge(S["z3T"], E + 1)
                    freed(pe, gelu[NE - 1], E)
                    in_parts(BH1[0:NE, 0:NT], wr_hi[:], wr_lo[:], z3T[:]).then_inc(S["ps_route"], 1)
                if A is not None:
                    pe.wait_ge(S["x_hi"], A + 1)
                    pe.wait_ge(S["x_lo"], A + 1)
                    N = NT + HALF
                    if isinstance(A, int) and A == 0:
                        pe.wait_ge(prep_dve, place(DVE_PREP, "wc_lo"))
                    for t in range(HALF):
                        pe.matmul(BA[:, 0:N], wc_hi[:, t, :], x_hi[:, t:t + N], start=(t == 0), stop=False)
                        pe.matmul(BA[:, 0:N], wc_lo[:, t, :], x_hi[:, t:t + N], start=False, stop=False)
                if B is not None:
                    plain(pe)
                    pe.wait_ge(S["L"], B + 1)
                    for c in range(CH):
                        ins = pe.transpose(B1[0:P, c * HR:(c + 1) * HR], kq[HR:2 * HR, c * P:(c + 1) * P],
                                           ident[HR:2 * HR, HR:2 * HR])
                    ins.then_inc(S["ps_q"], 1)
                if A is not None:
                    for t in range(HALF):
                        ins = pe.matmul(BA[:, 0:N], wc_hi[:, t, :], x_lo[:, t:t + N], start=False, stop=(t == HALF - 1))
                    ins.then_inc(S["ps_conv"], 1)
                if M is not None:
                    pe.wait_ge(S["z2_hi"], M + 1)
                    pe.wait_ge(S["z2_lo"], M + 1)
                    freed(pe, S["h2"], M)
                    turn(BM, z2hl, S["ps_z2T"])
                if E is not None:
                    plain(pe)
                    pe.wait_ge(S["route"], E + 1)
                    freed(pe, gated[NP - 1], E)
                    for c in range(CH):
                        ins = pe.transpose(BW[0:P, c * NE:(c + 1) * NE], routeT[:, c * P:(c + 1) * P], ident[0:NE, 0:NE])
                    ins.then_inc(S["ps_lg"], 1)
                    hidden(E, 0)
                    hidden(E, 1)
                if B is not None:
                    plain(pe)
                    pe.wait_ge(S["k_exp"], B + 1)
                    for c in range(CH):
                        ins = pe.transpose(B2[0:P, c * HR:(c + 1) * HR], kq[0:HR, c * P:(c + 1) * P], ident[0:HR, 0:HR])
                    ins.then_inc(S["ps_k"], 1)
                if M is not None:
                    pe.wait_ge(S["z2T"], M + 1)
                    in_parts(cols(BM), w1_hi[:, 0:128], w1_lo[:, 0:128], z2T[:]).then_inc(S["ps_m0"], 1)
                if E is not None:
                    hidden(E, 2)
                    hidden(E, 3)
                if B is not None:
                    pe.wait_ge(S["EkT"], B + 1)
                    for c in range(CH):
                        ins = pe.matmul(B2[0:HR, 0:C], EkT[:, c, :], z[:, c, :], start=(c == 0), stop=(c == CH - 1))
                    ins.then_inc(S["ps_G"], 1)
                if M is not None:
                    pe.wait_ge(S["mlp_g0"], M + 1)
                    in_parts(cols(BM), w1_hi[:, 128:256], w1_lo[:, 128:256], z2T[:]).then_inc(S["ps_m1"], 1)
                if E is not None:
                    pe.wait_ge(S["w_lo"], E + 1)
                    for c in range(CH):
                        ins = pe.transpose(BW[0:2 * NE, c * P:(c + 1) * P],
                                           whl[:, c, :, :].rearrange("p s e -> p (s e)").bitcast(F32), ident[0:P, 0:P])
                    ins.then_inc(S["ps_w"], 1)
                if B is not None:
                    pe.wait_ge(S["q_lo"], B + 1)
                    for c in range(CH):
                        ins = pe.transpose(B1[0:3 * HR, c * P:(c + 1) * P],
                                           qhl[:, c, :, :].rearrange("p s e -> p (s e)").bitcast(F32), ident[0:P, 0:P])
                    ins.then_inc(S["ps_qT"], 1)
                    plain(pe)
                    pe.wait_ge(S["G_norm"], B + 1)
                    pe.transpose(B2[:, 0:HR], Gd[:].rearrange("p s c -> p (s c)"), ident[0:HR, 0:HR]).then_inc(S["ps_GT"], 1)
                if E is not None:
                    outputs(E, 0)
                if B is not None:
                    pe.wait_ge(S["G_heads"], B + 1)
                    for j in range(H // 2):
                        ins = pe.matmul(B2[0:HR, 0:C], Gx[:, j, :], u_pair[:, j, :], start=(j == 0), stop=(j == H // 2 - 1))
                    ins.then_inc(S["ps_M"], 1)
                if M is not None:
                    pe.wait_ge(S["mlp_g1"], M + 1)
                    for k in range(2):
                        ins = pe.matmul(BM[k * C:(k + 1) * C, 0:NT], w2_sb[:, k, :], mg[k][:], start=True, stop=True)
                    ins.then_inc(S["ps_m2"], 1)
                if E is not None:
                    hidden(E, 4)
                    hidden(E, 5)
                if B is not None:
                    pe.wait_ge(S["M_stack"], B + 1)
                    pe.wait_ge(S["qT"], B + 1)
                    for c in range(CH):
                        ins = pe.matmul(B2[0:P, c * C:(c + 1) * C], qT[:, c * P:(c + 1) * P], M3[:], start=True, stop=True)
                    ins.then_inc(S["ps_at"], 1)
                if E is not None:
                    outputs(E, 1)
                if M is not None:
                    pe.wait_ge(S["mlp_F"], M + 1)
                    for c in range(CH):
                        ins = pe.transpose(BM[0:P, c * 2 * C:(c + 1) * 2 * C], mF[:, c * P:(c + 1) * P], ident[:])
                    ins.then_inc(S["ps_mT"], 1)
                if A is not None:
                    plain(pe)
                    pe.wait_ge(S["pre"], A + 1)
                    for c in range(CH):
                        ins = pe.transpose(BA[0:P, c * C:(c + 1) * C], pre[:, c * P:(c + 1) * P], ident[0:C, 0:C])
                    ins.then_inc(S["ps_pre"], 1)
                if E is not None:
                    hidden(E, 6)
                    hidden(E, 7)
                    outputs(E, 2)
                    outputs(E, 3)
                    pe.wait_ge(yev[NP - 1], E + 1)
                    pe.wait_ge(S["sum_all"], E + 1)
                    for c in range(CH):
                        ins = pe.transpose(BY[0:P, c * 2 * C:(c + 1) * 2 * C], sum_all[:, c * P:(c + 1) * P], ident[:])
                    ins.then_inc(S["ps_out"], 1)

            run(pe, step, prepare)


_INS = ['x', 'L0_tok_filt', 'L0_tok_W_k', 'L0_tok_b_k', 'L0_attn_ln1_g', 'L0_attn_ln1_b', 'L0_attn_Wx',
        'L0_attn_bx', 'L0_attn_Wq', 'L0_attn_Wk', 'L0_attn_Wv', 'L0_attn_Wo', 'L0_attn_bo', 'L0_attn_ln2_g',
        'L0_attn_ln2_b', 'L0_attn_W1', 'L0_attn_b1', 'L0_attn_W2', 'L0_attn_b2', 'L0_ffn_gamma',
        'L0_ffn_beta', 'L0_ffn_Wr', 'L0_ffn_br', 'L0_ffn_W1', 'L0_ffn_b1', 'L0_ffn_W2', 'L0_ffn_b2']


def kernel(**inputs):
    import numpy as _np
    import concourse.bacc as _bacc
    from concourse import mybir as _mybir
    from concourse.bass_utils import run_bass_kernel_spmd as _run

    nc = _bacc.Bacc("TRN2", target_bir_lowering=False, num_devices=1)
    arrays, args = {}, {}
    for name in _INS:
        v = _np.ascontiguousarray(inputs[name])
        arrays[f"in_{name}"] = v
        t = nc.dram_tensor(f"in_{name}", v.shape, _mybir.dt.from_np(v.dtype), kind="ExternalInput")
        args[name.removeprefix("L0_")] = t.ap()
    x, filt, wk = (inputs[n] for n in ('x', 'L0_tok_filt', 'L0_tok_W_k'))
    shape = (x.shape[0], x.shape[1] - filt.shape[0], wk.shape[1])
    res = nc.dram_tensor("out_0", shape, _mybir.dt.from_np(_np.dtype("float32")), kind="ExternalOutput")
    audio_tower_kernel(nc, args, res.ap())
    r = _run(nc, [arrays], core_ids=[0])
    return r.results[0]["out_0"]
```

```python
from contextlib import ExitStack

import concourse.bass as bass
from concourse import mybir

F32 = mybir.dt.float32
F32R = mybir.dt.float32r
U32 = mybir.dt.uint32
ALU = mybir.AluOpType
ACT = mybir.ActivationFunctionType
AX_X = mybir.AxisListType.X
EPS = 1e-05

PE_DONE = """ps_xT ps_conv ps_pre ps_zT ps_L ps_q ps_k ps_G ps_GT ps_M ps_qT ps_at ps_z2T ps_m0 ps_m1
ps_m2 ps_mT ps_z3T ps_lg ps_w ps_out"""
ACT_DONE = """x_hi late_taps h1 z_hi zT L k_exp q_exp qT z2_hi z2T mlp_g0 mlp_g1 mlp_F z3_hi z3T
th wT"""
DVE_DONE = """x_lo pre a_stats a_mv a_var a_hc z z_lo k_negmax k_rden EkT q_max q_sub q_sum q_rec q_norm
q_hi q_lo G_norm G_heads M_sum M_hi M_stack fx b_stats b_mv b_var b_hc z2 z2_lo m_half h2 m_stats m_mv
m_var m_hc z3 z3_lo lg top idx gap p hot hot_p w w_hi w_lo o_half o"""
POOL_DONE = "h2_kept a_rstd z_res0 z_res b_rstd fxh m_rstd sum0 sum1 sum_all"


def audio_tower_kernel(nc, a, out):
    NB, L, D = a["x"].shape
    TAPS = a["tok_filt"].shape[0]
    C = a["tok_W_k"].shape[1]
    NT = L - TAPS
    CH = 4
    P = NT // CH
    HALF = TAPS // 2
    DH, KR = a["attn_Wq"].shape
    H = a["attn_Wx"].shape[1] // DH
    HR = H * KR
    FF = a["attn_W1"].shape[1]
    NE, _, EH = a["ffn_W1"].shape
    NP = NE // 2
    XC = L // 128
    assert P * CH == NT and 2 * C == 128 and D == 128 and EH == 128 and FF == 256 and HR == 32

    with ExitStack() as ctx:
        def sb(name, shape, dt=F32):
            return ctx.enter_context(nc.sbuf_tensor(name, shape, dt))

        def sem(name):
            return ctx.enter_context(nc.semaphore(name))

        bank = [ctx.enter_context(nc.psum_tensor(f"bank{i}", [128, 512], F32)) for i in range(8)]
        BA, B1, B2, BM, BH0, BH1, BY, BW = bank
        BH = [BH0, BH1]

        ident = sb("ident", [128, 128])
        ident_r = sb("ident_r", [128, 128], F32R)
        iota8 = sb("iota8", [128, NE])
        ones = sb("ones", [128, CH])
        head_rows = sb("head_rows", [32, H, HR])
        head_mask = sb("head_mask", [128, H // 2, HR])
        sel32 = sb("sel32", [128, NP, 2, C])
        sel = sb("sel", [128, NP, 2 * C], F32R)
        minus_half = sb("minus_half", [128, 8])
        filt_sb = sb("filt_sb", [TAPS, D])
        filtT = sb("filtT", [D, TAPS])
        wk_sb = sb("wk_sb", [D, TAPS, C])
        wc32 = sb("wc32", [D, HALF, 2, C])
        wc_hi = sb("wc_hi", [D, HALF, 2 * C], F32R)
        wc_lo = sb("wc_lo", [D, HALF, 2 * C], F32R)
        bk_col = sb("bk_col", [C, 1])
        g1_col = sb("g1_col", [128, 1])
        b1_col = sb("b1_col", [C, 1])
        wx_sb = sb("wx_sb", [C, H * DH])
        wxT2 = sb("wxT2", [DH, H, 2, C])
        bxT = sb("bxT", [DH, H])
        bxg = sb("bxg", [DH, H])
        wkq_sb = sb("wkq_sb", [DH, 2 * KR])
        wv_sb = sb("wv_sb", [DH, DH])
        wvT = sb("wvT", [DH, DH])
        wo_sb = sb("wo_sb", [DH, H, C])
        wvo = sb("wvo", [DH, H, C])
        bx_heads = sb("bx_heads", [DH, H, HR])
        u_pair = sb("u_pair", [128, H // 2, C])
        u_bias = sb("u_bias", [HR, C])
        wqk32 = sb("wqk32", [128, 2 * HR])
        wqk_hi = sb("wqk_hi", [128, 2 * HR], F32R)
        wqk_lo = sb("wqk_lo", [128, 2 * HR], F32R)
        bqk_row = sb("bqk_row", [1, 2 * HR])
        bqk_col = sb("bqk_col", [2 * HR, 1])
        bo_rows = sb("bo_rows", [128, C])
        g2_col = sb("g2_col", [128, 1])
        b2ln_col = sb("b2ln_col", [C, 1])
        w1_raw = sb("w1_raw", [128, FF])
        w1_32 = sb("w1_32", [128, FF])
        w1_hi = sb("w1_hi", [128, FF], F32R)
        w1_lo = sb("w1_lo", [128, FF], F32R)
        b1mT = sb("b1mT", [128, 2])
        b1m = sb("b1m", [128, 2])
        w2_sb = sb("w2_sb", [128, 2, C])
        b2m_col = sb("b2m_col", [128, 1])
        gam_col = sb("gam_col", [128, 1])
        bet_col = sb("bet_col", [C, 1])
        wr_raw = sb("wr_raw", [128, NE])
        wr32 = sb("wr32", [128, NE])
        wr_hi = sb("wr_hi", [128, NE], F32R)
        wr_lo = sb("wr_lo", [128, NE], F32R)
        brc = sb("brc", [128, NE])
        bet_rows = sb("bet_rows", [C, 128])
        br_rows = sb("br_rows", [128, NE])
        ew1_raw = sb("ew1_raw", [128, NE, EH])
        ew1_32 = sb("ew1_32", [128, NE * EH])
        ew1_hi = sb("ew1_hi", [128, NE * EH], F32R)
        ew1_lo = sb("ew1_lo", [128, NE * EH], F32R)
        eb1T = sb("eb1T", [128, NE])
        eb1 = sb("eb1", [128, NE])
        ew2 = sb("ew2", [EH, NE, C])
        eb2 = sb("eb2", [128, NP])

        x_sb = sb("x_sb", [128, XC, D])
        x_hi = sb("x_hi", [D, L], F32R)
        x_lo = sb("x_lo", [D, L], F32R)
        late_taps = sb("late_taps", [C, NT])
        pre = sb("pre", [C, NT])
        h1 = sb("h1", [P, CH, C])
        a_st = sb("a_st", [P, CH, 6])
        a_mv = sb("a_mv", [P, CH, 2])
        a_var = sb("a_var", [P, 2, CH])
        a_rs = sb("a_rs", [P, 2, CH])
        hc = sb("hc", [P, CH, C])
        z = sb("z", [P, CH, C])
        zhl = sb("zhl", [P, CH, 2, C], F32R)
        zr0 = sb("zr0", [P, CH, C])
        zr = sb("zr", [P, CH, C])
        zT = sb("zT", [128, NT], F32R)
        kq = sb("kq", [2 * HR, NT])
        k_negmax = sb("k_negmax", [HR, 1])
        k_den = sb("k_den", [HR, 1])
        k_rden = sb("k_rden", [HR, 1])
        EkT = sb("EkT", [P, CH, HR])
        q_max = sb("q_max", [P, CH * H])
        q_sub = sb("q_sub", [P, CH * H, KR])
        q_e = sb("q_e", [P, CH * H, KR])
        q_sum = sb("q_sum", [P, CH * H])
        q_rec = sb("q_rec", [P, CH * H])
        q_n = sb("q_n", [P, CH, HR])
        qhl = sb("qhl", [P, CH, 3, HR], F32R)
        qT = sb("qT", [3 * HR, NT], F32R)
        Gd = sb("Gd", [HR, 2, C])
        Gx = sb("Gx", [128, H // 2, HR])
        Mf = sb("Mf", [HR, C])
        M3 = sb("M3", [3 * HR, C], F32R)
        fx = sb("fx", [P, CH, C])
        fxh = sb("fxh", [P, CH, C])
        b_st = sb("b_st", [P, CH, 6])
        b_mv = sb("b_mv", [P, CH, 2])
        b_var = sb("b_var", [P, CH])
        b_rs = sb("b_rs", [P, CH])
        b_hc = sb("b_hc", [P, CH, C])
        z2 = sb("z2", [P, CH, C])
        z2hl = sb("z2hl", [P, CH, 2, C], F32R)
        z2T = sb("z2T", [128, NT], F32R)
        mg = [sb(f"mg{k}", [128, NT]) for k in range(2)]
        mF = sb("mF", [128, NT])
        m_half = sb("m_half", [P, CH, C])
        h2 = sb("h2", [P, CH, C])
        h2_kept = sb("h2_kept", [P, CH, C])
        m_st = sb("m_st", [P, CH, 6])
        m_mv = sb("m_mv", [P, CH, 2])
        m_var = sb("m_var", [P, CH])
        m_rs = sb("m_rs", [P, CH])
        m_hc = sb("m_hc", [P, CH, C])
        z3 = sb("z3", [P, CH, C])
        z3hl = sb("z3hl", [P, CH, 2, C], F32R)
        z3T = sb("z3T", [128, NT], F32R)
        lg = sb("lg", [P, CH, NE])
        top = sb("top", [P, CH, 8])
        idx = sb("idx", [P, CH, 8], U32)
        gap = sb("gap", [P, CH])
        th = sb("th", [P, CH])
        p12 = sb("p12", [P, CH, 2])
        hot = sb("hot", [P, CH, 2, NE])
        hot_p = sb("hot_p", [P, CH, 2, NE])
        w = sb("w", [P, CH, NE])
        whl = sb("whl", [P, CH, 2, NE], F32R)
        wT = sb("wT", [128, NT], F32R)
        eg = [sb(f"eg{k}", [EH, NT]) for k in range(4)]
        y_ev = [sb(f"y_ev{k}", [128, NT]) for k in range(2)]
        yg = [sb(f"yg{k}", [128, NT]) for k in range(NP)]
        sum0 = sb("sum0", [128, NT])
        sum1 = sb("sum1", [128, NT])
        sum_all = sb("sum_all", [128, NT])
        o_half = sb("o_half", [P, CH, C])
        o_sb = sb("o_sb", [P, CH, C])

        x_in = sem("x_in")
        out_stored = sem("out_stored")
        conv_w_in = sem("conv_w_in")
        attn_w_in = sem("attn_w_in")
        mlp_w_in = sem("mlp_w_in")
        ffn_w_in = sem("ffn_w_in")
        consts = sem("consts")
        prep_pe = sem("prep_pe")
        prep_dve = sem("prep_dve")
        prep_pool = sem("prep_pool")
        S = {n: sem("s_" + n) for part in (PE_DONE, ACT_DONE, DVE_DONE, POOL_DONE) for n in part.split()}
        ps_h = [sem(f"ps_h{e}") for e in range(NE)]
        gelu = [sem(f"gelu{e}") for e in range(NE)]
        ps_y = [sem(f"ps_y{j}") for j in range(NP)]
        ps_wb = [sem(f"ps_wb{j}") for j in range(NP)]
        yev = [sem(f"yev{j}") for j in range(NP)]
        gated = [sem(f"gated{j}") for j in range(NP)]

        PE_PREP = ["filtT", "wxT", "wvT", "ln_bx", "wqk", "bqk_row", "wvo", "bqk_col", "u", "u_bias",
                   "b1m", "eb1", "br"]
        DVE_PREP = ["filtT", "wc32", "wc_hi", "wc_lo", "wxT2", "wvT", "bxg", "wqk32", "wqk_hi", "wqk_lo",
                    "bx_heads", "bqk_row", "wvo", "bqk_col", "u_lo", "u_hi", "u_bias", "b1m", "eb1", "br"]
        POOL_PREP = ["w1_32", "w1_hi", "w1_lo", "bet_rows", "wr32", "wr_hi", "wr_lo", "sel", "ew1_32", "ew1_hi",
                     "ew1_lo"]

        def place(names, n):
            return names.index(n) + 1

        def freed(engine, done, b):
            if not (isinstance(b, int) and b == 0):
                engine.wait_ge(done, b)

        def plain(engine):
            engine.wait_ge(consts, 19)

        def cols(b, n=NT):
            return b[:, 0:n]

        def chunk(t, c):
            return t[:, c * P:(c + 1) * P]

        def row3(b, n, p=P):
            return b[0:p, 0:CH * n].rearrange("p (c n) -> p c n", c=CH)

        def each(t, n=C):
            return t.unsqueeze(2).to_broadcast([P, CH, n])

        CONV_DMAS, ATTN_DMAS, MLP_DMAS, FFN_DMAS = 16 * 3, 16 * 10, 16 * 8, 16 * 12

        BEHIND = (0, 1, 2, 3, 4)
        LAST = BEHIND[-1]
        FULL = LAST

        def do(part, b, *which):
            if b is not None:
                part(b, *which)

        def run(engine, step, before, own_first=False):
            for i in range(FULL):
                if i in before:
                    before[i]()
                if i or not own_first:
                    step(*(i - n if i >= n else None for n in BEHIND))
            with engine.Fori(FULL, NB) as i:
                step(*(i - n for n in BEHIND))
            for i in range(NB, NB + LAST):
                step(*(i - n if i - n < NB else None for n in BEHIND))

        block = ctx.enter_context(nc.Block())

        def column(v):
            return v.rearrange("(p o) -> p o", o=1)

        def attn_loads(queue, n):
            if n == 0:
                queue.dma_start(wkq_sb[:, 0:KR], a["attn_Wk"]).then_inc(attn_w_in, 16)
                queue.dma_start(wkq_sb[:, KR:2 * KR], a["attn_Wq"]).then_inc(attn_w_in, 16)
                queue.dma_start(b1_col[:], column(a["attn_ln1_b"])).then_inc(attn_w_in, 16)
                queue.dma_start(bxT[:], a["attn_bx"].rearrange("(h d) -> d h", d=DH), allow_slow_non_contiguous=True).then_inc(attn_w_in, 16)
                queue.dma_start(wo_sb[:], a["attn_Wo"].rearrange("(h d) c -> d h c", d=DH)).then_inc(attn_w_in, 16)
            else:
                queue.dma_start(wx_sb[:], a["attn_Wx"]).then_inc(attn_w_in, 16)
                queue.dma_start(g1_col[0:C, :], column(a["attn_ln1_g"])).then_inc(attn_w_in, 16)
                queue.dma_start(g1_col[C:128, :], column(a["attn_ln1_g"])).then_inc(attn_w_in, 16)
                queue.dma_start(wv_sb[:], a["attn_Wv"]).then_inc(attn_w_in, 16)
                queue.dma_start(bo_rows[:], a["attn_bo"].unsqueeze(0).to_broadcast([128, C])).then_inc(attn_w_in, 16)

        @block.sync
        def _(sp):
            x_dram = a["x"].rearrange("b (c p) d -> b p c d", p=128)
            out_dram = out.rearrange("b (c p) k -> b p c k", p=P)

            def load(b):
                sp.wait_ge(S["ps_xT"], b)
                sp.dma_start(x_sb[:], x_dram[b]).then_inc(x_in, 16)

            def store(b):
                sp.wait_ge(S["o"], b + 1)
                sp.dma_start(out_dram[b], o_sb[:]).then_inc(out_stored, 16)

            sp.sem_inc(out_stored, 16)
            sp.dma_start(x_sb[:], x_dram[0]).then_inc(x_in, 16)
            sp.dma_start(wk_sb[:], a["tok_W_k"].rearrange("(f d) k -> d f k", d=D)).then_inc(conv_w_in, 16)
            attn_loads(sp, 1)
            load(1)
            sp.dma_start(w1_raw[0:C, :], a["attn_W1"]).then_inc(mlp_w_in, 16)
            sp.dma_start(w1_raw[C:128, :], a["attn_W1"]).then_inc(mlp_w_in, 16)
            sp.dma_start(g2_col[0:C, :], column(a["attn_ln2_g"])).then_inc(mlp_w_in, 16)
            sp.dma_start(g2_col[C:128, :], column(a["attn_ln2_g"])).then_inc(mlp_w_in, 16)
            sp.dma_start(w2_sb[:], a["attn_W2"].rearrange("(k p) c -> p k c", p=128)).then_inc(mlp_w_in, 16)
            sp.dma_start(b2ln_col[:], column(a["attn_ln2_b"])).then_inc(mlp_w_in, 16)
            sp.dma_start(b1mT[:], a["attn_b1"].rearrange("(k p) -> p k", p=128), allow_slow_non_contiguous=True).then_inc(mlp_w_in, 16)
            sp.wait_ge(consts, 8)
            sp.dma_start(b2m_col[0:C, :], column(a["attn_b2"])).then_inc(mlp_w_in, 16)
            sp.dma_start(gam_col[0:C, :], column(a["ffn_gamma"])).then_inc(ffn_w_in, 16)
            sp.dma_start(gam_col[C:128, :], column(a["ffn_gamma"])).then_inc(ffn_w_in, 16)
            sp.dma_start(wr_raw[0:C, :], a["ffn_Wr"]).then_inc(ffn_w_in, 16)
            sp.dma_start(wr_raw[C:128, :], a["ffn_Wr"]).then_inc(ffn_w_in, 16)
            ew1_src = a["ffn_W1"].rearrange("e c h -> c e h")
            sp.dma_start(ew1_raw[0:C, :, :], ew1_src).then_inc(ffn_w_in, 16)
            sp.dma_start(ew1_raw[C:128, :, :], ew1_src).then_inc(ffn_w_in, 16)
            sp.dma_start(bet_col[:], column(a["ffn_beta"])).then_inc(ffn_w_in, 16)
            sp.dma_start(brc[:], a["ffn_br"].unsqueeze(0).to_broadcast([128, NE])).then_inc(ffn_w_in, 16)
            sp.dma_start(eb1T[:], a["ffn_b1"].rearrange("e h -> h e"), allow_slow_non_contiguous=True).then_inc(ffn_w_in, 16)
            for s in range(2):
                sp.dma_start(eb2[s * C:(s + 1) * C, :],
                             a["ffn_b2"].rearrange("(j s) c -> s c j", s=2)[s], allow_slow_non_contiguous=True).then_inc(ffn_w_in, 16)
            sp.dma_start(ew2[:], a["ffn_W2"].rearrange("e h c -> h e c")).then_inc(ffn_w_in, 16)
            with sp.Fori(2, LAST + 2) as b:
                load(b)
            with sp.Fori(LAST + 2, NB) as b:
                store(b - LAST - 2)
                load(b)
            with sp.Fori(NB - LAST - 2, NB) as b:
                store(b)
            sp.wait_ge(out_stored, 16 * NB + 16)

        @block.gpsimd
        def _(pool):
            pool.memset(ident[:], 0.0).then_inc(consts, 1)
            pool.memset(minus_half[:], -0.5).then_inc(consts, 1)
            pool.memset(ones[:], 1.0).then_inc(consts, 1)
            pool.memset(sel32[:], 0.0).then_inc(consts, 1)
            pool.memset(head_rows[:], 1.0).then_inc(consts, 1)
            pool.memset(head_mask[:], 1.0).then_inc(consts, 1)
            pool.memset(wT[:].bitcast(F32), 0.0).then_inc(consts, 1)
            pool.memset(b2m_col[:], 0.0).then_inc(consts, 1)
            pool.iota(iota8[:], [[1, NE]], base=0, channel_multiplier=0,
                      allow_small_or_imprecise_dtypes=True).then_inc(consts, 1)
            pool.wait_ge(consts, 1)
            pool.affine_select(out=ident[:], in_=ident[:], compare_op=ALU.not_equal, fill=1.0, base=0,
                               pattern=[[-1, 128]], channel_multiplier=1).then_inc(consts, 1)
            pool.wait_ge(consts, 9)
            for n, off in enumerate((0, NE)):
                if n:
                    pool.wait_ge(consts, 11)
                pool.affine_select(out=sel32[:], in_=sel32[:], compare_op=ALU.not_equal, fill=1.0,
                                   base=-off, pattern=[[-2, NP], [-1, 2], [0, C]],
                                   channel_multiplier=1).then_inc(consts, 1)
            pool.affine_select(out=head_rows[:], in_=head_rows[:], compare_op=ALU.is_ge, fill=0.0, base=0,
                               pattern=[[-KR, H], [1, HR]], channel_multiplier=0).then_inc(consts, 1)
            for s in range(2):
                pool.wait_ge(consts, 13 + s)
                m = head_mask[s * C:(s + 1) * C, :, :]
                pool.affine_select(out=m, in_=m, compare_op=ALU.is_ge, fill=0.0, base=-KR * s,
                                   pattern=[[-2 * KR, H // 2], [1, HR]], channel_multiplier=0).then_inc(consts, 1)
            pool.wait_ge(consts, 15)
            pool.affine_select(out=head_rows[:], in_=head_rows[:], compare_op=ALU.is_ge, fill=0.0,
                               base=KR - 1, pattern=[[KR, H], [-1, HR]], channel_multiplier=0).then_inc(consts, 1)
            for s in range(2):
                pool.wait_ge(consts, 16 + s)
                m = head_mask[s * C:(s + 1) * C, :, :]
                pool.affine_select(out=m, in_=m, compare_op=ALU.is_ge, fill=0.0, base=KR * s + KR - 1,
                                   pattern=[[2 * KR, H // 2], [-1, HR]], channel_multiplier=0).then_inc(consts, 1)
            pool.wait_ge(consts, 18)
            pool.tensor_copy(ident_r[:], ident[:]).then_inc(consts, 1)

            def b_rstd(b):
                pool.wait_ge(S["b_var"], b + 1)
                freed(pool, S["z2"], b)
                pool.tensor_tensor(b_rs[:], b_var[:], minus_half[0:P, 0:CH], ALU.pow).then_inc(S["b_rstd"], 1)

            def m_rstd(b):
                pool.wait_ge(S["m_var"], b + 1)
                freed(pool, S["z3"], b)
                pool.tensor_tensor(m_rs[:], m_var[:], minus_half[0:P, 0:CH], ALU.pow).then_inc(S["m_rstd"], 1)

            def a_rstd(b):
                pool.wait_ge(S["a_var"], b + 1)
                freed(pool, S["z"], b)
                pool.tensor_tensor(a_rs[:], a_var[:],
                                   minus_half[0:P, 0:2 * CH].rearrange("p (a c) -> p a c", a=2),
                                   ALU.pow).then_inc(S["a_rstd"], 1)

            def fx_plus_h1(b):
                pool.wait_ge(S["fx"], b + 1)
                freed(pool, S["m_half"], b)
                pool.tensor_tensor(fxh[:], fx[:], h1[:], ALU.add).then_inc(S["fxh"], 1)

            def residual(b):
                pool.wait_ge(S["a_hc"], b + 1)
                pool.wait_ge(S["a_rstd"], b + 1)
                pool.tensor_tensor(zr0[:], hc[:], each(a_rs[:, 0, :]), ALU.mult).then_inc(S["z_res0"], 1)
                pool.wait_ge(S["z_res0"], b + 1)
                freed(pool, S["fx"], b)
                if isinstance(b, int) and b == 0:
                    pool.wait_ge(attn_w_in, ATTN_DMAS)
                pool.tensor_tensor(zr[:], zr0[:], bo_rows[0:P, :].unsqueeze(1).to_broadcast([P, CH, C]),
                                   ALU.add).then_inc(S["z_res"], 1)

            def keep_h2(b):
                pool.wait_ge(S["h2"], b + 1)
                freed(pool, S["o_half"], b)
                pool.tensor_tensor(h2_kept[:], h2[:], each(ones[0:P, :]), ALU.mult).then_inc(S["h2_kept"], 1)

            def sum_first(b):
                pool.wait_ge(gated[0], b + 1)
                pool.wait_ge(gated[1], b + 1)
                pool.tensor_tensor(sum0[:], yg[0][:], yg[1][:], ALU.add).then_inc(S["sum0"], 1)

            def sum_rest(b):
                pool.wait_ge(gated[2], b + 1)
                pool.wait_ge(gated[3], b + 1)
                pool.tensor_tensor(sum1[:], yg[2][:], yg[3][:], ALU.add).then_inc(S["sum1"], 1)
                pool.wait_ge(S["sum0"], b + 1)
                pool.wait_ge(S["sum1"], b + 1)
                pool.tensor_tensor(sum_all[:], sum0[:], sum1[:], ALU.add).then_inc(S["sum_all"], 1)

            def step(A, B, M, E, T):
                do(b_rstd, M)
                do(sum_first, T)
                do(residual, B)
                do(sum_rest, T)
                do(keep_h2, E)
                do(fx_plus_h1, B)
                do(m_rstd, M)
                do(a_rstd, A)

            def prepare():
                def made(n):
                    pool.wait_ge(prep_pool, place(POOL_PREP, n))

                def prep(ins):
                    ins.then_inc(prep_pool, 1)

                pool.wait_ge(mlp_w_in, MLP_DMAS)
                prep(pool.tensor_scalar(w1_32[:], w1_raw[:], g2_col[:, 0:1], None, ALU.mult))
                made("w1_32")
                prep(pool.tensor_copy(w1_hi[:], w1_32[:]))
                made("w1_hi")
                prep(pool.tensor_tensor(w1_lo[:], w1_32[:], w1_hi[:].bitcast(F32), ALU.subtract))
                pool.wait_ge(ffn_w_in, FFN_DMAS)
                prep(pool.tensor_copy(bet_rows[:], bet_col[:, 0:1].to_broadcast([C, 128])))
                prep(pool.tensor_scalar(wr32[:], wr_raw[:], gam_col[:, 0:1], None, ALU.mult))
                made("wr32")
                prep(pool.tensor_copy(wr_hi[:], wr32[:]))
                made("wr_hi")
                prep(pool.tensor_tensor(wr_lo[:], wr32[:], wr_hi[:].bitcast(F32), ALU.subtract))
                prep(pool.tensor_copy(sel[:], sel32[:].rearrange("p j s c -> p j (s c)")))
                prep(pool.tensor_scalar(ew1_32[:], ew1_raw[:].rearrange("p e h -> p (e h)"), gam_col[:, 0:1], None, ALU.mult))
                made("ew1_32")
                prep(pool.tensor_copy(ew1_hi[:], ew1_32[:]))
                made("ew1_hi")
                prep(pool.tensor_tensor(ew1_lo[:], ew1_32[:], ew1_hi[:].bitcast(F32), ALU.subtract))

            run(pool, step, {1: prepare})

        @block.scalar
        def _(act):
            act.dma_start(filt_sb[:], a["tok_filt"]).then_inc(conv_w_in, 16)
            act.dma_start(bk_col[:], column(a["tok_b_k"])).then_inc(conv_w_in, 16)
            attn_loads(act, 0)

            def copy_zT(b):
                act.wait_ge(S["ps_zT"], b + 1)
                freed(act, S["ps_L"], b)
                act.activation(zT[:], cols(B1), ACT.Copy).then_inc(S["zT"], 1)

            def copy_z2T(b):
                act.wait_ge(S["ps_z2T"], b + 1)
                freed(act, S["ps_m1"], b)
                act.activation(z2T[:], cols(BM), ACT.Copy).then_inc(S["z2T"], 1)

            def copy_z3T(b):
                act.wait_ge(S["ps_z3T"], b + 1)
                freed(act, ps_h[NE - 1], b)
                act.activation(z3T[:], cols(BH0), ACT.Copy).then_inc(S["z3T"], 1)

            def x_high(b):
                act.wait_ge(S["ps_xT"], b + 1)
                freed(act, S["ps_conv"], b)
                act.activation(x_hi[:], BA[:, 0:L], ACT.Copy).then_inc(S["x_hi"], 1)

            def key_query_logits(b):
                act.wait_ge(S["ps_L"], b + 1)
                freed(act, S["ps_k"], b)
                act.activation(kq[:], B2[0:2 * HR, 0:NT], ACT.Identity, bias=bqk_col[:, 0:1]).then_inc(S["L"], 1)

            def key_exp(b):
                act.wait_ge(S["k_negmax"], b + 1)
                act.wait_ge(S["L"], b + 1)
                freed(act, S["k_rden"], b)
                act.activation(kq[0:HR, :], kq[0:HR, :], ACT.Exp, bias=k_negmax[:, 0:1],
                               accum_out=k_den[:, 0:1]).then_inc(S["k_exp"], 1)

            def query_exp(b):
                act.wait_ge(S["q_sub"], b + 1)
                freed(act, S["q_norm"], b)
                act.activation(q_e[:], q_sub[:], ACT.Exp).then_inc(S["q_exp"], 1)

            def gate_tanh(b):
                act.wait_ge(S["gap"], b + 1)
                freed(act, S["p"], b)
                act.activation(th[:], gap[:], ACT.Tanh, scale=0.5).then_inc(S["th"], 1)

            def copy_late_taps(b):
                act.wait_ge(S["ps_conv"], b + 1)
                freed(act, S["pre"], b)
                act.activation(late_taps[:], BA[C:128, HALF:HALF + NT], ACT.Copy).then_inc(S["late_taps"], 1)

            def copy_qT(b):
                act.wait_ge(S["ps_qT"], b + 1)
                freed(act, S["ps_at"], b)
                act.activation(qT[:], B1[0:3 * HR, 0:NT], ACT.Copy).then_inc(S["qT"], 1)

            def copy_wT(b):
                act.wait_ge(S["ps_w"], b + 1)
                freed(act, ps_wb[NP - 1], b)
                act.activation(wT[0:2 * NE, :], BW[0:2 * NE, 0:NT], ACT.Copy).then_inc(S["wT"], 1)

            def mlp_out(b):
                act.wait_ge(S["ps_m2"], b + 1)
                freed(act, S["ps_mT"], b)
                act.activation(mF[:], cols(BM), ACT.Identity, bias=b2m_col[:, 0:1]).then_inc(S["mlp_F"], 1)

            def z2_high(b):
                act.wait_ge(S["z2"], b + 1)
                freed(act, S["ps_z2T"], b)
                act.activation(z2hl[:, :, 0, :], z2[:], ACT.Copy).then_inc(S["z2_hi"], 1)

            def tokens(b):
                act.wait_ge(S["ps_pre"], b + 1)
                freed(act, S["fxh"], b)
                act.activation(h1[:], row3(BA, C), ACT.Relu).then_inc(S["h1"], 1)

            def z3_high(b):
                act.wait_ge(S["z3"], b + 1)
                freed(act, S["ps_z3T"], b)
                act.activation(z3hl[:, :, 0, :], z3[:], ACT.Copy).then_inc(S["z3_hi"], 1)

            def z_high(b):
                act.wait_ge(S["z"], b + 1)
                freed(act, S["ps_zT"], b)
                act.activation(zhl[:, :, 0, :], z[:], ACT.Copy).then_inc(S["z_hi"], 1)

            def hidden(b, e):
                act.wait_ge(ps_h[e], b + 1)
                if e < 4:
                    freed(act, ps_y[(e + 4) // 2], b)
                else:
                    act.wait_ge(ps_y[(e - 4) // 2], b + 1)
                act.activation(eg[e % 4][:], cols(BH[e % 2]), ACT.Gelu, bias=eb1[:, e:e + 1]).then_inc(gelu[e], 1)

            def mlp_hidden(b, k):
                act.wait_ge(S["ps_m1"] if k else S["ps_m0"], b + 1)
                freed(act, S["ps_m2"], b)
                act.activation(mg[k][:], cols(BM), ACT.Gelu,
                               bias=b1m[:, k:k + 1]).then_inc(S["mlp_g1"] if k else S["mlp_g0"], 1)

            def outputs(b, j):
                act.wait_ge(ps_y[j], b + 1)
                if j < 2:
                    freed(act, gated[j + 2], b)
                else:
                    act.wait_ge(gated[j - 2], b + 1)
                act.activation(y_ev[j % 2][:], cols(BY), ACT.Identity, bias=eb2[:, j:j + 1]).then_inc(yev[j], 1)

            def attn_prepared():
                act.wait_ge(prep_dve, place(DVE_PREP, "bqk_col"))
                act.wait_ge(consts, 19)

            def mlp_prepared():
                act.wait_ge(prep_dve, place(DVE_PREP, "b1m"))
                act.wait_ge(mlp_w_in, MLP_DMAS)

            def experts_prepared():
                act.wait_ge(prep_dve, place(DVE_PREP, "br"))
                act.wait_ge(ffn_w_in, FFN_DMAS)

            def step(A, B, M, E, T):
                do(z_high, B)
                do(outputs, T, 2)
                do(x_high, A)
                do(copy_zT, B)
                do(z3_high, E)
                do(key_query_logits, B)
                do(outputs, T, 3)
                do(z2_high, M)
                do(key_exp, B)
                do(copy_z2T, M)
                do(query_exp, B)
                do(copy_z3T, E)
                do(mlp_hidden, M, 0)
                do(copy_late_taps, A)
                do(mlp_hidden, M, 1)
                do(gate_tanh, E)
                do(hidden, E, 1)
                do(copy_qT, B)
                do(mlp_out, M)
                do(hidden, E, 0)
                do(hidden, E, 3)
                do(copy_wT, E)
                do(hidden, E, 2)
                do(tokens, A)
                do(outputs, E, 0)
                do(hidden, E, 4)
                do(hidden, E, 5)
                do(outputs, E, 1)
                do(hidden, E, 6)
                do(hidden, E, 7)

            run(act, step, {1: attn_prepared, 2: mlp_prepared, 3: experts_prepared})

        @block.vector
        def _(dve):
            def prep(ins):
                ins.then_inc(prep_dve, 1)

            dve.wait_ge(prep_pe, place(PE_PREP, "filtT"))
            prep(dve.tensor_copy(filtT[:], BH0[0:D, 0:TAPS]))
            dve.wait_ge(conv_w_in, CONV_DMAS)
            dve.wait_ge(prep_dve, place(DVE_PREP, "filtT"))
            prep(dve.tensor_tensor(wc32[:].rearrange("d t h k -> d h t k"),
                                   wk_sb[:].rearrange("d (h t) k -> d h t k", h=2),
                                   filtT[:].rearrange("d (h t) -> d h t", h=2).unsqueeze(3)
                                   .to_broadcast([D, 2, HALF, C]), ALU.mult))
            dve.wait_ge(prep_dve, place(DVE_PREP, "wc32"))
            prep(dve.tensor_copy(wc_hi[:], wc32[:].rearrange("d t h k -> d t (h k)")))
            dve.wait_ge(prep_dve, place(DVE_PREP, "wc_hi"))
            prep(dve.tensor_tensor(wc_lo[:], wc32[:].rearrange("d t h k -> d t (h k)"),
                                   wc_hi[:].bitcast(F32), ALU.subtract))

            def made(n):
                dve.wait_ge(prep_dve, place(DVE_PREP, n))

            def summed(n):
                dve.wait_ge(prep_pe, place(PE_PREP, n))

            def prepare_first():
                dve.wait_ge(attn_w_in, ATTN_DMAS)
                dve.wait_ge(consts, 19)
                summed("wxT")
                prep(dve.tensor_copy(wxT2[:], B1[0:DH, 0:H * C].rearrange("d (h c) -> d h c", h=H).unsqueeze(2)
                                     .to_broadcast([DH, H, 2, C])))
                summed("wvT")
                prep(dve.tensor_copy(wvT[:], B2[0:DH, 0:DH]))
                summed("ln_bx")
                prep(dve.tensor_tensor(bxg[:], BM[0:DH, 0:H], bxT[:], ALU.add))

            def prepare_logits():
                summed("wqk")
                prep(dve.tensor_scalar(wqk32[:].rearrange("p (t h r) -> p t h r", t=2, h=H),
                                       B2[:, 0:2 * HR].rearrange("p (h t r) -> p t h r", t=2, h=H),
                                       g1_col[:, 0:1], None, ALU.mult))
                made("wqk32")
                prep(dve.tensor_copy(wqk_hi[:], wqk32[:]))
                made("wqk_hi")
                prep(dve.tensor_tensor(wqk_lo[:], wqk32[:], wqk_hi[:].bitcast(F32), ALU.subtract))
                prep(dve.tensor_tensor(bx_heads[:], head_rows[:], bxg[:].unsqueeze(2).to_broadcast([DH, H, HR]), ALU.mult))
                summed("bqk_row")
                prep(dve.tensor_copy(bqk_row[:].rearrange("p (t h r) -> p t h r", t=2, h=H),
                                     BH0[0:1, 0:2 * HR].rearrange("p (h t r) -> p t h r", t=2, h=H)))
                summed("wvo")
                prep(dve.tensor_copy(wvo[:], BW[0:DH, 0:H * C].rearrange("d (h c) -> d h c", h=H)))

            def prepare_values():
                summed("bqk_col")
                prep(dve.tensor_copy(bqk_col[:], BH1[0:2 * HR, 0:1]))
                summed("u")
                for s in range(2):
                    prep(dve.tensor_scalar(u_pair[s * C:(s + 1) * C, :, :],
                                           B1[s * C:(s + 1) * C, 0:H * C].rearrange("p (j s c) -> p j s c", s=2, c=C)[:, :, s, :],
                                           g1_col[s * C:(s + 1) * C, 0:1], None, ALU.mult))
                summed("u_bias")
                prep(dve.tensor_copy(u_bias[:], BM[0:HR, 0:C]))

            def prepare_biases():
                dve.wait_ge(mlp_w_in, MLP_DMAS)
                dve.wait_ge(ffn_w_in, FFN_DMAS)
                summed("b1m")
                prep(dve.tensor_tensor(b1m[:], BH0[:, 0:2], b1mT[:], ALU.add))
                summed("eb1")
                prep(dve.tensor_tensor(eb1[:], BH1[:, 0:NE], eb1T[:], ALU.add))
                summed("br")
                prep(dve.tensor_tensor(br_rows[:], BY[:, 0:NE], brc[:], ALU.add))

            def moments(src, st, mv, stats_done, mv_done, b):
                for c in range(CH):
                    ins = dve.bn_stats(st[:, c, :], src[:, c, :])
                ins.then_inc(stats_done, 1)
                plain(dve)
                dve.wait_ge(stats_done, b + 1)
                for c in range(CH):
                    ins = dve.bn_aggr(mv[:, c, :], st[:, c, :])
                ins.then_inc(mv_done, 1)

            def x_low(b):
                dve.wait_ge(S["x_hi"], b + 1)
                freed(dve, S["ps_conv"], b)
                dve.tensor_tensor(x_lo[:], BA[:, 0:L], x_hi[:].bitcast(F32), ALU.subtract).then_inc(S["x_lo"], 1)

            def key_max(b):
                dve.wait_ge(S["L"], b + 1)
                freed(dve, S["k_exp"], b)
                dve.tensor_reduce(k_negmax[:], kq[0:HR, :], AX_X, ALU.max, negate=True).then_inc(S["k_negmax"], 1)

            def query_shift(b):
                q_ps = B1[0:P, 0:CH * HR].rearrange("p (g r) -> p g r", r=KR)
                dve.wait_ge(S["ps_q"], b + 1)
                dve.tensor_reduce(q_max[:], q_ps, AX_X, ALU.max).then_inc(S["q_max"], 1)
                dve.wait_ge(S["q_max"], b + 1)
                freed(dve, S["q_exp"], b)
                dve.tensor_tensor(q_sub[:], q_ps, q_max[:].unsqueeze(2).to_broadcast([P, CH * H, KR]),
                                  ALU.subtract).then_inc(S["q_sub"], 1)

            def query_norm(b):
                dve.wait_ge(S["q_exp"], b + 1)
                dve.tensor_reduce(q_sum[:], q_e[:], AX_X, ALU.add).then_inc(S["q_sum"], 1)
                dve.wait_ge(S["q_sum"], b + 1)
                dve.reciprocal(q_rec[:], q_sum[:]).then_inc(S["q_rec"], 1)
                dve.wait_ge(S["q_rec"], b + 1)
                dve.tensor_tensor(q_n[:].rearrange("p c (h r) -> p (c h) r", r=KR), q_e[:],
                                  q_rec[:].unsqueeze(2).to_broadcast([P, CH * H, KR]),
                                  ALU.mult).then_inc(S["q_norm"], 1)

            def query_parts(b):
                dve.wait_ge(S["q_norm"], b + 1)
                freed(dve, S["ps_qT"], b)
                dve.tensor_copy(qhl[:, :, 0, :], q_n[:])
                dve.tensor_copy(qhl[:, :, 2, :], q_n[:]).then_inc(S["q_hi"], 1)
                dve.wait_ge(S["q_hi"], b + 1)
                dve.tensor_tensor(qhl[:, :, 1, :], q_n[:], qhl[:, :, 0, :].bitcast(F32),
                                  ALU.subtract).then_inc(S["q_lo"], 1)

            def keys(b):
                dve.wait_ge(S["ps_k"], b + 1)
                freed(dve, S["ps_G"], b)
                dve.tensor_copy(EkT[:], row3(B2, HR)).then_inc(S["EkT"], 1)
                dve.wait_ge(S["k_exp"], b + 1)
                dve.reciprocal(k_rden[:], k_den[:]).then_inc(S["k_rden"], 1)

            def key_sums(b):
                dve.wait_ge(S["ps_G"], b + 1)
                dve.wait_ge(S["k_rden"], b + 1)
                freed(dve, S["ps_GT"], b)
                dve.tensor_scalar(Gd[:], B2[0:HR, 0:C].unsqueeze(1).to_broadcast([HR, 2, C]),
                                  k_rden[:, 0:1], None, ALU.mult).then_inc(S["G_norm"], 1)

            def key_sums_by_head(b):
                dve.wait_ge(S["ps_GT"], b + 1)
                freed(dve, S["ps_M"], b)
                dve.tensor_tensor(Gx[:], B2[:, 0:HR].unsqueeze(1).to_broadcast([128, H // 2, HR]),
                                  head_mask[:], ALU.mult).then_inc(S["G_heads"], 1)

            def value_rows(b):
                dve.wait_ge(S["ps_M"], b + 1)
                dve.tensor_tensor(Mf[:], B2[0:HR, 0:C], u_bias[:], ALU.add).then_inc(S["M_sum"], 1)
                dve.wait_ge(S["M_sum"], b + 1)
                freed(dve, S["ps_at"], b)
                dve.tensor_copy(M3[0:HR, :], Mf[:]).then_inc(S["M_hi"], 1)
                dve.tensor_copy(M3[HR:2 * HR, :], Mf[:])
                dve.wait_ge(S["M_hi"], b + 1)
                dve.tensor_tensor(M3[2 * HR:3 * HR, :], Mf[:], M3[0:HR, :].bitcast(F32),
                                  ALU.subtract).then_inc(S["M_stack"], 1)

            def top_two(b):
                dve.wait_ge(S["ps_lg"], b + 1)
                dve.tensor_tensor(lg[:], row3(BW, NE), br_rows[0:P, :].unsqueeze(1).to_broadcast([P, CH, NE]),
                                  ALU.add).then_inc(S["lg"], 1)
                plain(dve)
                dve.wait_ge(S["lg"], b + 1)
                for c in range(CH):
                    ins = dve.max(top[:, c, :], lg[:, c, :])
                ins.then_inc(S["top"], 1)
                plain(dve)
                dve.wait_ge(S["top"], b + 1)
                for c in range(CH):
                    ins = dve.max_index(idx[:, c, :], top[:, c, :], lg[:, c, :])
                ins.then_inc(S["idx"], 1)
                freed(dve, S["th"], b)
                dve.tensor_tensor(gap[:], top[:, :, 1], top[:, :, 0], ALU.subtract).then_inc(S["gap"], 1)
                dve.wait_ge(S["idx"], b + 1)
                dve.tensor_tensor(hot[:], idx[:, :, 0:2].unsqueeze(3).to_broadcast([P, CH, 2, NE]),
                                  iota8[0:P, :].unsqueeze(1).unsqueeze(1).to_broadcast([P, CH, 2, NE]),
                                  ALU.is_equal).then_inc(S["hot"], 1)

            def gates(b):
                dve.wait_ge(S["th"], b + 1)
                dve.tensor_scalar(p12[:, :, 0], th[:], -0.5, 0.5, ALU.mult, ALU.add)
                dve.tensor_scalar(p12[:, :, 1], th[:], 0.5, 0.5, ALU.mult, ALU.add).then_inc(S["p"], 1)
                dve.wait_ge(S["p"], b + 1)
                dve.wait_ge(S["hot"], b + 1)
                dve.tensor_tensor(hot_p[:], hot[:], p12[:].unsqueeze(3).to_broadcast([P, CH, 2, NE]),
                                  ALU.mult).then_inc(S["hot_p"], 1)
                dve.wait_ge(S["hot_p"], b + 1)
                dve.tensor_tensor(w[:], hot_p[:, :, 0, :], hot_p[:, :, 1, :], ALU.add).then_inc(S["w"], 1)
                dve.wait_ge(S["w"], b + 1)
                freed(dve, S["ps_w"], b)
                dve.tensor_copy(whl[:, :, 0, :], w[:]).then_inc(S["w_hi"], 1)
                dve.wait_ge(S["w_hi"], b + 1)
                dve.tensor_tensor(whl[:, :, 1, :], w[:], whl[:, :, 0, :].bitcast(F32),
                                  ALU.subtract).then_inc(S["w_lo"], 1)

            def windows(b):
                dve.wait_ge(S["late_taps"], b + 1)
                freed(dve, S["ps_pre"], b)
                dve.scalar_tensor_tensor(out=pre[:], in0=BA[0:C, 0:NT], scalar=bk_col[:, 0:1],
                                         in1=late_taps[:], op0=ALU.add, op1=ALU.add).then_inc(S["pre"], 1)

            def gate(b, j):
                dve.wait_ge(yev[j], b + 1)
                dve.wait_ge(ps_wb[j], b + 1)
                if j < 2:
                    freed(dve, S["sum0"], b)
                dve.tensor_tensor(yg[j][:], y_ev[j % 2][:], cols(BW), ALU.mult).then_inc(gated[j], 1)

            def attn_residual(b):
                dve.wait_ge(S["ps_at"], b + 1)
                dve.wait_ge(S["z_res"], b + 1)
                freed(dve, S["fxh"], b)
                dve.tensor_tensor(fx[:], row3(B2, C), zr[:], ALU.add).then_inc(S["fx"], 1)

            def b_moments(b):
                dve.wait_ge(S["fx"], b + 1)
                moments(fx, b_st, b_mv, S["b_stats"], S["b_mv"], b)
                dve.wait_ge(S["b_mv"], b + 1)
                freed(dve, S["b_rstd"], b)
                dve.tensor_scalar(b_var[:], b_mv[:, :, 1], EPS, None, ALU.add).then_inc(S["b_var"], 1)
                dve.tensor_tensor(b_hc[:], fx[:], each(b_mv[:, :, 0]), ALU.subtract).then_inc(S["b_hc"], 1)

            def b_normed(b):
                dve.wait_ge(S["b_rstd"], b + 1)
                dve.wait_ge(S["b_hc"], b + 1)
                freed(dve, S["z2_hi"], b)
                dve.tensor_tensor(z2[:], b_hc[:], each(b_rs[:]), ALU.mult).then_inc(S["z2"], 1)

            def z2_low(b):
                dve.wait_ge(S["z2_hi"], b + 1)
                dve.tensor_tensor(z2hl[:, :, 1, :], z2[:], z2hl[:, :, 0, :].bitcast(F32),
                                  ALU.subtract).then_inc(S["z2_lo"], 1)

            def mlp_residual(b):
                m_ps = row3(BM, 2 * C)
                dve.wait_ge(S["ps_mT"], b + 1)
                dve.wait_ge(S["fxh"], b + 1)
                dve.tensor_tensor(m_half[:], m_ps[:, :, 0:C], fxh[:], ALU.add).then_inc(S["m_half"], 1)
                dve.wait_ge(S["m_half"], b + 1)
                freed(dve, S["h2_kept"], b)
                dve.tensor_tensor(h2[:], m_ps[:, :, C:2 * C], m_half[:], ALU.add).then_inc(S["h2"], 1)

            def m_moments(b):
                dve.wait_ge(S["h2"], b + 1)
                moments(h2, m_st, m_mv, S["m_stats"], S["m_mv"], b)
                dve.wait_ge(S["m_mv"], b + 1)
                freed(dve, S["m_rstd"], b)
                dve.tensor_scalar(m_var[:], m_mv[:, :, 1], 1.0 + EPS, EPS * EPS, ALU.mult, ALU.add).then_inc(S["m_var"], 1)
                dve.tensor_tensor(m_hc[:], h2[:], each(m_mv[:, :, 0]), ALU.subtract).then_inc(S["m_hc"], 1)

            def m_normed(b):
                dve.wait_ge(S["m_rstd"], b + 1)
                dve.wait_ge(S["m_hc"], b + 1)
                freed(dve, S["z3_hi"], b)
                dve.tensor_tensor(z3[:], m_hc[:], each(m_rs[:]), ALU.mult).then_inc(S["z3"], 1)

            def z3_low(b):
                dve.wait_ge(S["z3_hi"], b + 1)
                dve.tensor_tensor(z3hl[:, :, 1, :], z3[:], z3hl[:, :, 0, :].bitcast(F32),
                                  ALU.subtract).then_inc(S["z3_lo"], 1)

            def a_moments(b):
                dve.wait_ge(S["h1"], b + 1)
                moments(h1, a_st, a_mv, S["a_stats"], S["a_mv"], b)
                dve.wait_ge(S["a_mv"], b + 1)
                freed(dve, S["a_rstd"], b)
                dve.tensor_scalar(a_var[:, 0, :], a_mv[:, :, 1], EPS, None, ALU.add)
                dve.tensor_scalar(a_var[:, 1, :], a_mv[:, :, 1], 1.0 + EPS, EPS * EPS, ALU.mult,
                                  ALU.add).then_inc(S["a_var"], 1)
                freed(dve, S["z_res0"], b)
                dve.tensor_tensor(hc[:], h1[:], each(a_mv[:, :, 0]), ALU.subtract).then_inc(S["a_hc"], 1)

            def a_normed(b):
                dve.wait_ge(S["a_rstd"], b + 1)
                dve.wait_ge(S["a_hc"], b + 1)
                freed(dve, S["ps_G"], b)
                freed(dve, S["z_hi"], b)
                dve.tensor_tensor(z[:], hc[:], each(a_rs[:, 1, :]), ALU.mult).then_inc(S["z"], 1)

            def z_low(b):
                dve.wait_ge(S["z_hi"], b + 1)
                dve.tensor_tensor(zhl[:, :, 1, :], z[:], zhl[:, :, 0, :].bitcast(F32),
                                  ALU.subtract).then_inc(S["z_lo"], 1)

            def result(b):
                o_ps = row3(BY, 2 * C)
                dve.wait_ge(S["ps_out"], b + 1)
                dve.wait_ge(S["h2_kept"], b + 1)
                dve.tensor_tensor(o_half[:], o_ps[:, :, 0:C], h2_kept[:], ALU.add).then_inc(S["o_half"], 1)
                dve.wait_ge(S["o_half"], b + 1)
                dve.wait_ge(out_stored, 16 * b + 16)
                dve.tensor_tensor(o_sb[:], o_ps[:, :, C:2 * C], o_half[:], ALU.add).then_inc(S["o"], 1)

            def step(A, B, M, E, T):
                do(z_low, B)
                do(b_moments, M)
                do(x_low, A)
                do(b_normed, M)
                do(key_max, B)
                do(gate, T, 2)
                do(z2_low, M)
                do(z3_low, E)
                do(query_shift, B)
                do(gate, T, 3)
                do(keys, B)
                do(query_norm, B)
                do(key_sums, B)
                do(query_parts, B)
                do(top_two, E)
                do(key_sums_by_head, B)
                do(windows, A)
                do(gates, E)
                do(value_rows, B)
                do(result, T)
                do(mlp_residual, M)
                do(attn_residual, B)
                do(m_moments, M)
                do(a_moments, A)
                do(gate, E, 0)
                do(m_normed, M)
                do(a_normed, A)
                do(gate, E, 1)

            def first_step():
                x_low(0)
                windows(0)
                prepare_first()
                a_moments(0)
                prepare_logits()
                a_normed(0)
                prepare_values()

            run(dve, step, {0: first_step, 2: prepare_biases}, own_first=True)

        @block.tensor
        def _(pe):
            pe.wait_ge(consts, 10)
            pe.wait_ge(conv_w_in, CONV_DMAS)
            pe.transpose(BH0[0:D, 0:TAPS], filt_sb[:], ident[0:TAPS, 0:TAPS]).then_inc(prep_pe, 1)

            def made(n):
                pe.wait_ge(prep_dve, place(DVE_PREP, n))

            def prepare_first():
                pe.wait_ge(attn_w_in, ATTN_DMAS)
                for h in range(H):
                    ins = pe.transpose(B1[0:DH, h * C:(h + 1) * C], wx_sb[:, h * DH:(h + 1) * DH], ident[0:C, 0:C])
                ins.then_inc(prep_pe, 1)
                pe.transpose(B2[0:DH, 0:DH], wv_sb[:], ident[0:DH, 0:DH]).then_inc(prep_pe, 1)
                for h in range(H):
                    ins = pe.matmul(BM[0:DH, h:h + 1], wx_sb[:, h * DH:(h + 1) * DH], b1_col[:], start=True, stop=True)
                ins.then_inc(prep_pe, 1)

            def prepare_rest():
                made("bxg")
                for h in range(H):
                    ins = pe.matmul(B2[:, h * 2 * KR:(h + 1) * 2 * KR], wxT2[:, h, :, :].rearrange("d s c -> d (s c)"),
                                    wkq_sb[:], start=True, stop=True)
                ins.then_inc(prep_pe, 1)
                for h in range(H):
                    ins = pe.matmul(BH0[0:1, h * 2 * KR:(h + 1) * 2 * KR], bxg[:, h:h + 1], wkq_sb[:], start=True, stop=True)
                ins.then_inc(prep_pe, 1)
                pe.matmul(BW[0:DH, 0:H * C], wvT[:], wo_sb[:].rearrange("d h c -> d (h c)"),
                          start=True, stop=True).then_inc(prep_pe, 1)
                made("bqk_row")
                pe.matmul(BH1[0:2 * HR, 0:1], bqk_row[:], ones[0:1, 0:1], start=True, stop=True).then_inc(prep_pe, 1)
                made("wvo")
                for h in range(H):
                    ins = pe.matmul(B1[:, h * C:(h + 1) * C], wxT2[:, h, :, :].rearrange("d s c -> d (s c)"),
                                    wvo[:, h, :], start=True, stop=True)
                ins.then_inc(prep_pe, 1)
                for h in range(H):
                    ins = pe.matmul(BM[0:HR, 0:C], bx_heads[:, h, :], wvo[:, h, :], start=(h == 0), stop=(h == H - 1))
                ins.then_inc(prep_pe, 1)

            def first_step():
                turn_x(0)
                conv_high(0)
                conv_low(0)
                prepare_first()
                turn_tokens(0)
                prepare_rest()

            def attn_prepared():
                made("u_bias")

            def prepare_biases():
                pe.wait_ge(mlp_w_in, MLP_DMAS)
                for k in range(2):
                    ins = pe.matmul(BH0[:, k:k + 1], w1_raw[0:C, k * 128:(k + 1) * 128], b2ln_col[:], start=True, stop=True)
                ins.then_inc(prep_pe, 1)
                pe.wait_ge(ffn_w_in, FFN_DMAS)
                for e in range(NE):
                    ins = pe.matmul(BH1[:, e:e + 1], ew1_raw[0:C, e, :], bet_col[:], start=True, stop=True)
                ins.then_inc(prep_pe, 1)
                pe.wait_ge(prep_pool, place(POOL_PREP, "bet_rows"))
                pe.matmul(BY[:, 0:NE], bet_rows[:], wr_raw[0:C, :], start=True, stop=True).then_inc(prep_pe, 1)
                pe.wait_ge(prep_pool, place(POOL_PREP, "w1_lo"))

            def experts_prepared():
                made("br")
                pe.wait_ge(prep_pool, place(POOL_PREP, "ew1_lo"))

            def turn(dst, src, done):
                for c in range(CH):
                    ins = pe.transpose(chunk(dst, c).bitcast(F32R), src[:, c, :, :].rearrange("p s c -> p (s c)"), ident_r[0:P, 0:P])
                ins.then_inc(done, 1)

            def in_parts(dst, w_hi, w_lo, data):
                pe.matmul(dst, w_hi, data, start=True, stop=False)
                return pe.matmul(dst, w_lo, data, start=False, stop=True)

            def turn_z(b):
                pe.wait_ge(S["z_hi"], b + 1)
                pe.wait_ge(S["z_lo"], b + 1)
                freed(pe, S["qT"], b)
                turn(B1, zhl, S["ps_zT"])

            def turn_z2(b):
                pe.wait_ge(S["z2_hi"], b + 1)
                pe.wait_ge(S["z2_lo"], b + 1)
                freed(pe, S["h2"], b)
                turn(BM, z2hl, S["ps_z2T"])

            def turn_z3(b):
                pe.wait_ge(S["z3_hi"], b + 1)
                pe.wait_ge(S["z3_lo"], b + 1)
                freed(pe, gelu[NE - 2], b)
                turn(BH0, z3hl, S["ps_z3T"])

            def turn_x(b):
                pe.wait_ge(x_in, 16 * b + 16)
                freed(pe, S["h1"], b)
                for c in range(XC):
                    ins = pe.transpose(BA[:, c * 128:(c + 1) * 128], x_sb[:, c, :], ident[:])
                ins.then_inc(S["ps_xT"], 1)

            def key_query_logits(b):
                pe.wait_ge(S["zT"], b + 1)
                freed(pe, S["fx"], b)
                in_parts(B2[0:2 * HR, 0:NT], wqk_hi[:], wqk_lo[:], zT[:]).then_inc(S["ps_L"], 1)

            N = NT + HALF

            def conv_high(b):
                pe.wait_ge(S["x_hi"], b + 1)
                pe.wait_ge(S["x_lo"], b + 1)
                if isinstance(b, int) and b == 0:
                    pe.wait_ge(prep_dve, place(DVE_PREP, "wc_lo"))
                for t in range(HALF):
                    pe.matmul(BA[:, 0:N], wc_hi[:, t, :], x_hi[:, t:t + N], start=(t == 0), stop=False)
                    pe.matmul(BA[:, 0:N], wc_lo[:, t, :], x_hi[:, t:t + N], start=False, stop=False)

            def conv_low(b):
                for t in range(HALF):
                    ins = pe.matmul(BA[:, 0:N], wc_hi[:, t, :], x_lo[:, t:t + N], start=False, stop=(t == HALF - 1))
                ins.then_inc(S["ps_conv"], 1)

            def turn_queries(b):
                plain(pe)
                pe.wait_ge(S["L"], b + 1)
                for c in range(CH):
                    ins = pe.transpose(B1[0:P, c * HR:(c + 1) * HR], kq[HR:2 * HR, c * P:(c + 1) * P],
                                       ident[HR:2 * HR, HR:2 * HR])
                ins.then_inc(S["ps_q"], 1)

            def turn_keys(b):
                plain(pe)
                pe.wait_ge(S["k_exp"], b + 1)
                for c in range(CH):
                    ins = pe.transpose(B2[0:P, c * HR:(c + 1) * HR], kq[0:HR, c * P:(c + 1) * P], ident[0:HR, 0:HR])
                ins.then_inc(S["ps_k"], 1)

            def route(b):
                pe.wait_ge(S["z3T"], b + 1)
                freed(pe, gated[NP - 1], b)
                for c in range(CH):
                    pe.matmul(BW[0:P, c * NE:(c + 1) * NE], z3T[:, c * P:(c + 1) * P], wr_hi[:], start=True, stop=False)
                    ins = pe.matmul(BW[0:P, c * NE:(c + 1) * NE], z3T[:, c * P:(c + 1) * P], wr_lo[:], start=False, stop=True)
                ins.then_inc(S["ps_lg"], 1)

            def turn_gates(b):
                pe.wait_ge(S["w_lo"], b + 1)
                for c in range(CH):
                    ins = pe.transpose(BW[0:2 * NE, c * P:(c + 1) * P].bitcast(F32R),
                                       whl[:, c, :, :].rearrange("p s e -> p (s e)"), ident_r[0:P, 0:P])
                ins.then_inc(S["ps_w"], 1)

            def mlp_hidden(b, k):
                pe.wait_ge(S["mlp_g0"] if k else S["z2T"], b + 1)
                in_parts(cols(BM), w1_hi[:, k * 128:(k + 1) * 128], w1_lo[:, k * 128:(k + 1) * 128],
                         z2T[:]).then_inc(S["ps_m1"] if k else S["ps_m0"], 1)

            def mlp_out(b):
                pe.wait_ge(S["mlp_g1"], b + 1)
                for k in range(2):
                    ins = pe.matmul(BM[k * C:(k + 1) * C, 0:NT], w2_sb[:, k, :], mg[k][:], start=True, stop=True)
                ins.then_inc(S["ps_m2"], 1)

            def turn_mlp(b):
                pe.wait_ge(S["mlp_F"], b + 1)
                for c in range(CH):
                    ins = pe.transpose(BM[0:P, c * 2 * C:(c + 1) * 2 * C], mF[:, c * P:(c + 1) * P], ident[:])
                ins.then_inc(S["ps_mT"], 1)

            def key_sums(b):
                pe.wait_ge(S["EkT"], b + 1)
                for c in range(CH):
                    ins = pe.matmul(B2[0:HR, 0:C], EkT[:, c, :], z[:, c, :], start=(c == 0), stop=(c == CH - 1))
                ins.then_inc(S["ps_G"], 1)

            def turn_key_sums(b):
                plain(pe)
                pe.wait_ge(S["G_norm"], b + 1)
                pe.transpose(B2[:, 0:HR], Gd[:].rearrange("p s c -> p (s c)"), ident[0:HR, 0:HR]).then_inc(S["ps_GT"], 1)

            def value_rows(b):
                pe.wait_ge(S["G_heads"], b + 1)
                for j in range(H // 2):
                    ins = pe.matmul(B2[0:HR, 0:C], Gx[:, j, :], u_pair[:, j, :], start=(j == 0), stop=(j == H // 2 - 1))
                ins.then_inc(S["ps_M"], 1)

            def turn_query_parts(b):
                pe.wait_ge(S["q_lo"], b + 1)
                for c in range(CH):
                    ins = pe.transpose(B1[0:3 * HR, c * P:(c + 1) * P].bitcast(F32R),
                                       qhl[:, c, :, :].rearrange("p s e -> p (s e)"), ident_r[0:P, 0:P])
                ins.then_inc(S["ps_qT"], 1)

            def attend(b):
                pe.wait_ge(S["M_stack"], b + 1)
                pe.wait_ge(S["qT"], b + 1)
                for c in range(CH):
                    ins = pe.matmul(B2[0:P, c * C:(c + 1) * C], qT[:, c * P:(c + 1) * P], M3[:], start=True, stop=True)
                ins.then_inc(S["ps_at"], 1)

            def turn_tokens(b):
                plain(pe)
                pe.wait_ge(S["pre"], b + 1)
                for c in range(CH):
                    ins = pe.transpose(BA[0:P, c * C:(c + 1) * C], pre[:, c * P:(c + 1) * P], ident[0:C, 0:C])
                ins.then_inc(S["ps_pre"], 1)

            def hidden(b, e):
                if e < 2:
                    pe.wait_ge(S["z3T"], b + 1)
                    if e:
                        freed(pe, gelu[NE - 1], b)
                else:
                    pe.wait_ge(gelu[e - 2], b + 1)
                in_parts(cols(BH[e % 2]), ew1_hi[:, e * EH:(e + 1) * EH], ew1_lo[:, e * EH:(e + 1) * EH],
                         z3T[:]).then_inc(ps_h[e], 1)

            def outputs(b, j):
                pe.wait_ge(gelu[2 * j], b + 1)
                pe.wait_ge(gelu[2 * j + 1], b + 1)
                if j:
                    pe.wait_ge(yev[j - 1], b + 1)
                else:
                    freed(pe, S["o"], b)
                for s in range(2):
                    ins = pe.matmul(BY[s * C:(s + 1) * C, 0:NT], ew2[:, 2 * j + s, :], eg[(2 * j + s) % 4][:],
                                    start=True, stop=True)
                ins.then_inc(ps_y[j], 1)

            def spread_gates(b, j):
                pe.wait_ge(gated[j - 1] if j else S["wT"], b + 1)
                pe.matmul(cols(BW), sel[:, j, :], wT[:], start=True, stop=True).then_inc(ps_wb[j], 1)

            def turn_result(b):
                pe.wait_ge(yev[NP - 1], b + 1)
                pe.wait_ge(S["sum_all"], b + 1)
                for c in range(CH):
                    ins = pe.transpose(BY[0:P, c * 2 * C:(c + 1) * 2 * C], sum_all[:, c * P:(c + 1) * P], ident[:])
                ins.then_inc(S["ps_out"], 1)

            def step(A, B, M, E, T):
                do(spread_gates, T, 0)
                do(hidden, T, 4)
                do(hidden, T, 5)
                do(turn_x, A)
                do(outputs, T, 1)
                do(hidden, T, 6)
                do(hidden, T, 7)
                do(spread_gates, T, 1)
                do(outputs, T, 2)
                do(spread_gates, T, 2)
                do(turn_z, B)
                do(outputs, T, 3)
                do(key_query_logits, B)
                do(conv_high, A)
                do(turn_queries, B)
                do(turn_z2, M)
                do(spread_gates, T, 3)
                do(turn_keys, B)
                do(turn_z3, E)
                do(mlp_hidden, M, 0)
                do(key_sums, B)
                do(route, E)
                do(conv_low, A)
                do(turn_key_sums, B)
                do(turn_query_parts, B)
                do(mlp_hidden, M, 1)
                do(hidden, E, 0)
                do(hidden, E, 1)
                do(value_rows, B)
                do(mlp_out, M)
                do(turn_result, T)
                do(hidden, E, 3)
                do(turn_mlp, M)
                do(turn_tokens, A)
                do(turn_gates, E)
                do(attend, B)
                do(hidden, E, 2)
                do(outputs, E, 0)

            run(pe, step, {0: first_step, 1: attn_prepared, 2: prepare_biases, 3: experts_prepared}, own_first=True)


_INS = ['x', 'L0_tok_filt', 'L0_tok_W_k', 'L0_tok_b_k', 'L0_attn_ln1_g', 'L0_attn_ln1_b', 'L0_attn_Wx',
        'L0_attn_bx', 'L0_attn_Wq', 'L0_attn_Wk', 'L0_attn_Wv', 'L0_attn_Wo', 'L0_attn_bo', 'L0_attn_ln2_g',
        'L0_attn_ln2_b', 'L0_attn_W1', 'L0_attn_b1', 'L0_attn_W2', 'L0_attn_b2', 'L0_ffn_gamma',
        'L0_ffn_beta', 'L0_ffn_Wr', 'L0_ffn_br', 'L0_ffn_W1', 'L0_ffn_b1', 'L0_ffn_W2', 'L0_ffn_b2']


def kernel(**inputs):
    import numpy as _np
    import concourse.bacc as _bacc
    from concourse import mybir as _mybir
    from concourse.bass_utils import run_bass_kernel_spmd as _run

    nc = _bacc.Bacc("TRN2", target_bir_lowering=False, num_devices=1)
    arrays, args = {}, {}
    for name in _INS:
        v = _np.ascontiguousarray(inputs[name])
        arrays[f"in_{name}"] = v
        t = nc.dram_tensor(f"in_{name}", v.shape, _mybir.dt.from_np(v.dtype), kind="ExternalInput")
        args[name.removeprefix("L0_")] = t.ap()
    x, filt, wk = (inputs[n] for n in ('x', 'L0_tok_filt', 'L0_tok_W_k'))
    shape = (x.shape[0], x.shape[1] - filt.shape[0], wk.shape[1])
    res = nc.dram_tensor("out_0", shape, _mybir.dt.from_np(_np.dtype("float32")), kind="ExternalOutput")
    audio_tower_kernel(nc, args, res.ap())
    r = _run(nc, [arrays], core_ids=[0])
    return r.results[0]["out_0"]
```

```python
from contextlib import ExitStack

import concourse.bass as bass
from concourse import mybir

F32 = mybir.dt.float32
F32R = mybir.dt.float32r
U32 = mybir.dt.uint32
ALU = mybir.AluOpType
ACT = mybir.ActivationFunctionType
AX_X = mybir.AxisListType.X
EPS = 1e-05

PE_DONE = """ps_conv ps_pre ps_zT ps_L ps_q ps_k ps_G ps_GT ps_M ps_qT ps_at ps_z2T ps_m0 ps_m1
ps_m2 ps_mT ps_z3T ps_lg ps_w ps_out"""
ACT_DONE = """x_hi late_taps h1 z_hi zT L k_exp q_exp qT z2_hi z2T mlp_g0 mlp_g1 mlp_F z3_hi z3T
th wT"""
DVE_DONE = """x_lo pre a_stats a_mv a_var a_hc z z_lo k_negmax k_rden EkT q_max q_sub q_sum q_rec q_norm
q_hi q_lo G_norm G_heads M_sum M_hi M_stack fx b_stats b_mv b_var b_hc z2 z2_lo m_half h2 m_stats m_mv
m_var m_hc z3 z3_lo lg top idx gap p hot hot_p w w_hi w_lo o_half o"""
POOL_DONE = "h1_kept z_kept h2_kept a_rstd z_res0 z_res b_rstd fxh m_rstd sum0 sum1 sum_all"


def audio_tower_kernel(nc, a, out):
    NB, D, L = a["x"].shape
    TAPS = a["tok_filt"].shape[1]
    C = a["tok_W_k"].shape[1]
    NT = L - TAPS
    CH = 4
    P = NT // CH
    HALF = TAPS // 2
    DH, KR = a["attn_Wq"].shape
    H = a["attn_Wx"].shape[0] // DH
    HR = H * KR
    FF = a["attn_W1"].shape[1]
    NE, _, EH = a["ffn_W1"].shape
    NP = NE // 2
    assert P * CH == NT and 2 * C == 128 and D == 128 and EH == 128 and FF == 256 and HR == 32

    with ExitStack() as ctx:
        def sb(name, shape, dt=F32):
            return ctx.enter_context(nc.sbuf_tensor(name, shape, dt))

        def sem(name):
            return ctx.enter_context(nc.semaphore(name))

        bank = [ctx.enter_context(nc.psum_tensor(f"bank{i}", [128, 512], F32)) for i in range(8)]
        BA, B1, B2, BM, BH0, BH1, BY, BW = bank
        BH = [BH0, BH1]

        ident = sb("ident", [128, 128])
        ident_r = sb("ident_r", [128, 128], F32R)
        iota8 = sb("iota8", [128, NE])
        ones = sb("ones", [128, CH])
        head_rows = sb("head_rows", [32, H, HR])
        head_mask = sb("head_mask", [128, H // 2, HR])
        sel32 = sb("sel32", [128, NP, 2, C])
        sel = sb("sel", [128, NP, 2 * C], F32R)
        minus_half = sb("minus_half", [128, 8])
        filtT = sb("filtT", [D, TAPS])
        wk_sb = sb("wk_sb", [D, TAPS, C])
        wc32 = sb("wc32", [D, HALF, 2, C])
        wc_hi = sb("wc_hi", [D, HALF, 2 * C], F32R)
        wc_lo = sb("wc_lo", [D, HALF, 2 * C], F32R)
        bk_col = sb("bk_col", [C, 1])
        g1_col = sb("g1_col", [128, 1])
        b1_col = sb("b1_col", [C, 1])
        wx_sb = sb("wx_sb", [C, H * DH])
        wxT2 = sb("wxT2", [DH, H, 2, C])
        bxT = sb("bxT", [DH, H])
        bxg = sb("bxg", [DH, H])
        wkq_sb = sb("wkq_sb", [DH, 2 * KR])
        wvT = sb("wvT", [DH, DH])
        wo_sb = sb("wo_sb", [DH, H, C])
        wvo = sb("wvo", [DH, H, C])
        bx_heads = sb("bx_heads", [DH, H, HR])
        u_pair = sb("u_pair", [128, H // 2, C])
        u_bias = sb("u_bias", [HR, C])
        wqk32 = sb("wqk32", [128, 2 * HR])
        wqk_hi = sb("wqk_hi", [128, 2 * HR], F32R)
        wqk_lo = sb("wqk_lo", [128, 2 * HR], F32R)
        bqk_row = sb("bqk_row", [1, 2 * HR])
        bqk_col = sb("bqk_col", [2 * HR, 1])
        bo_rows = sb("bo_rows", [128, C])
        g2_col = sb("g2_col", [128, 1])
        b2ln_col = sb("b2ln_col", [C, 1])
        w1_raw = sb("w1_raw", [128, FF])
        w1_32 = sb("w1_32", [128, FF])
        w1_hi = sb("w1_hi", [128, FF], F32R)
        w1_lo = sb("w1_lo", [128, FF], F32R)
        b1mT = sb("b1mT", [128, 2])
        b1m = sb("b1m", [128, 2])
        w2_sb = sb("w2_sb", [128, 2, C])
        b2m_col = sb("b2m_col", [128, 1])
        gam_col = sb("gam_col", [128, 1])
        bet_col = sb("bet_col", [C, 1])
        wr_raw = sb("wr_raw", [128, NE])
        wr32 = sb("wr32", [128, NE])
        wr_hi = sb("wr_hi", [128, NE], F32R)
        wr_lo = sb("wr_lo", [128, NE], F32R)
        brc = sb("brc", [128, NE])
        bet_rows = sb("bet_rows", [C, 128])
        br_rows = sb("br_rows", [128, NE])
        ew1_raw = sb("ew1_raw", [128, NE, EH])
        ew1_32 = sb("ew1_32", [128, NE * EH])
        ew1_hi = sb("ew1_hi", [128, NE * EH], F32R)
        ew1_lo = sb("ew1_lo", [128, NE * EH], F32R)
        eb1T = sb("eb1T", [128, NE])
        eb1 = sb("eb1", [128, NE])
        ew2 = sb("ew2", [EH, NE, C])
        eb2 = sb("eb2", [128, NP])

        x_sb = sb("x_sb", [D, L])
        x_hi = sb("x_hi", [D, L], F32R)
        x_lo = sb("x_lo", [D, L], F32R)
        late_taps = sb("late_taps", [C, NT])
        pre = sb("pre", [C, NT])
        h1 = sb("h1", [P, CH, C])
        h1_kept = sb("h1_kept", [P, CH, C])
        a_st = sb("a_st", [P, CH, 6])
        a_mv = sb("a_mv", [P, CH, 2])
        a_var = sb("a_var", [P, 2, CH])
        a_rs = sb("a_rs", [P, 2, CH])
        hc = sb("hc", [P, CH, C])
        z = sb("z", [P, CH, C])
        z_kept = sb("z_kept", [P, CH, C])
        zhl = sb("zhl", [P, CH, 2, C], F32R)
        zr0 = sb("zr0", [P, CH, C])
        zr = sb("zr", [P, CH, C])
        zT = sb("zT", [128, NT], F32R)
        kq = sb("kq", [2 * HR, NT])
        k_negmax = sb("k_negmax", [HR, 1])
        k_den = sb("k_den", [HR, 1])
        k_rden = sb("k_rden", [HR, 1])
        EkT = sb("EkT", [P, CH, HR])
        q_max = sb("q_max", [P, CH * H])
        q_sub = sb("q_sub", [P, CH * H, KR])
        q_e = sb("q_e", [P, CH * H, KR])
        q_sum = sb("q_sum", [P, CH * H])
        q_rec = sb("q_rec", [P, CH * H])
        q_n = sb("q_n", [P, CH, HR])
        qhl = sb("qhl", [P, CH, 3, HR], F32R)
        qT = sb("qT", [3 * HR, NT], F32R)
        Gd = sb("Gd", [HR, 2, C])
        Gx = sb("Gx", [128, H // 2, HR])
        Mf = sb("Mf", [HR, C])
        M3 = sb("M3", [3 * HR, C], F32R)
        fx = sb("fx", [P, CH, C])
        fxh = sb("fxh", [P, CH, C])
        b_st = sb("b_st", [P, CH, 6])
        b_mv = sb("b_mv", [P, CH, 2])
        b_var = sb("b_var", [P, CH])
        b_rs = sb("b_rs", [P, CH])
        b_hc = sb("b_hc", [P, CH, C])
        z2 = sb("z2", [P, CH, C])
        z2hl = sb("z2hl", [P, CH, 2, C], F32R)
        z2T = sb("z2T", [128, NT], F32R)
        mg = [sb(f"mg{k}", [128, NT]) for k in range(2)]
        mF = sb("mF", [128, NT])
        m_half = sb("m_half", [P, CH, C])
        h2 = sb("h2", [P, CH, C])
        h2_kept = sb("h2_kept", [P, CH, C])
        m_st = sb("m_st", [P, CH, 6])
        m_mv = sb("m_mv", [P, CH, 2])
        m_var = sb("m_var", [P, CH])
        m_rs = sb("m_rs", [P, CH])
        m_hc = sb("m_hc", [P, CH, C])
        z3 = sb("z3", [P, CH, C])
        z3hl = sb("z3hl", [P, CH, 2, C], F32R)
        z3T = sb("z3T", [128, NT], F32R)
        lg = sb("lg", [P, CH, NE])
        top = sb("top", [P, CH, 8])
        idx = sb("idx", [P, CH, 8], U32)
        gap = sb("gap", [P, CH])
        th = sb("th", [P, CH])
        p12 = sb("p12", [P, CH, 2])
        hot = sb("hot", [P, CH, 2, NE])
        hot_p = sb("hot_p", [P, CH, 2, NE])
        w = sb("w", [P, CH, NE])
        whl = sb("whl", [P, CH, 2, NE], F32R)
        wT = sb("wT", [128, NT], F32R)
        eg = [sb(f"eg{k}", [EH, NT]) for k in range(4)]
        y_ev = [sb(f"y_ev{k}", [128, NT]) for k in range(2)]
        yg = [sb(f"yg{k}", [128, NT]) for k in range(NP)]
        sum0 = sb("sum0", [128, NT])
        sum1 = sb("sum1", [128, NT])
        sum_all = sb("sum_all", [128, NT])
        o_half = sb("o_half", [P, CH, C])
        o_sb = sb("o_sb", [P, CH, C])

        x_in = sem("x_in")
        out_stored = sem("out_stored")
        conv_w_in = sem("conv_w_in")
        attn_w_in = sem("attn_w_in")
        mlp_w_in = sem("mlp_w_in")
        ffn_w_in = sem("ffn_w_in")
        consts = sem("consts")
        rounded_ident = sem("rounded_ident")
        prep_pe = sem("prep_pe")
        prep_dve = sem("prep_dve")
        prep_pool = sem("prep_pool")
        prep_act = sem("prep_act")
        S = {n: sem("s_" + n) for part in (PE_DONE, ACT_DONE, DVE_DONE, POOL_DONE) for n in part.split()}
        ps_h = [sem(f"ps_h{e}") for e in range(NE)]
        gelu = [sem(f"gelu{e}") for e in range(NE)]
        ps_y = [sem(f"ps_y{j}") for j in range(NP)]
        ps_wb = [sem(f"ps_wb{j}") for j in range(NP)]
        yev = [sem(f"yev{j}") for j in range(NP)]
        gated = [sem(f"gated{j}") for j in range(NP)]

        PE_PREP = ["ln_bx", "wqk", "bqk_row", "bqk_col", "wvo", "u", "u_bias", "b1m", "eb1", "br"]
        DVE_PREP = ["wc32", "wc_hi", "wc_lo", "bxg", "wqk32", "wqk_hi", "wqk_lo", "bqk_row", "bqk_col",
                    "bx_heads", "wvo", "u_lo", "u_hi", "u_bias", "b1m", "eb1", "br"]
        ACT_PREP = ["w1_32", "w1_hi", "wr32", "wr_hi", "sel", "ew1_32", "ew1_hi"]
        POOL_PREP = ["bet_rows", "w1_lo", "wr_lo", "ew1_lo"]

        def place(names, n):
            return names.index(n) + 1

        def freed(engine, done, b):
            if not (isinstance(b, int) and b == 0):
                engine.wait_ge(done, b)

        def plain(engine):
            engine.wait_ge(consts, 18)

        def cols(b, n=NT):
            return b[:, 0:n]

        def chunk(t, c):
            return t[:, c * P:(c + 1) * P]

        def row3(b, n, p=P):
            return b[0:p, 0:CH * n].rearrange("p (c n) -> p c n", c=CH)

        def each(t, n=C):
            return t.unsqueeze(2).to_broadcast([P, CH, n])

        CONV_DMAS, ATTN_DMAS, MLP_DMAS, FFN_DMAS = 16 * 3, 16 * 12, 16 * 8, 16 * 12

        BEHIND = (0, 1, 2, 3, 4)
        LAST = BEHIND[-1]
        FULL = LAST

        def do(part, b, *which):
            if b is not None:
                part(b, *which)

        def run(engine, opening, step, closing, before, own_first=False):
            for i in range(FULL):
                if i in before:
                    before[i]()
                if i or not own_first:
                    opening(*(i - n if i >= n else None for n in BEHIND))
            with engine.Fori(FULL, NB) as i:
                step(*(i - n for n in BEHIND))
            for i in range(NB, NB + LAST):
                closing(*(i - n if i - n < NB else None for n in BEHIND))

        block = ctx.enter_context(nc.Block())

        def column(v):
            return v.rearrange("(p o) -> p o", o=1)

        def attn_loads(queue, n):
            if n == 0:
                queue.dma_start(wkq_sb[:, 0:KR], a["attn_Wk"]).then_inc(attn_w_in, 16)
                queue.dma_start(wkq_sb[:, KR:2 * KR], a["attn_Wq"]).then_inc(attn_w_in, 16)
                queue.dma_start(b1_col[:], column(a["attn_ln1_b"])).then_inc(attn_w_in, 16)
                queue.dma_start(bxT[:], a["attn_bx"].rearrange("(h d) -> d h", d=DH), allow_slow_non_contiguous=True).then_inc(attn_w_in, 16)
                queue.dma_start(wo_sb[:], a["attn_Wo"].rearrange("(h d) c -> d h c", d=DH)).then_inc(attn_w_in, 16)
            else:
                for s in range(2):
                    queue.dma_start(wxT2[:, :, s, :], a["attn_Wx"].rearrange("(h d) c -> d h c", d=DH)).then_inc(attn_w_in, 16)
                queue.dma_start(g1_col[0:C, :], column(a["attn_ln1_g"])).then_inc(attn_w_in, 16)
                queue.dma_start(g1_col[C:128, :], column(a["attn_ln1_g"])).then_inc(attn_w_in, 16)
                queue.dma_start(wx_sb[:], a["attn_Wx_rows"]).then_inc(attn_w_in, 16)
                queue.dma_start(wvT[:], a["attn_Wv"]).then_inc(attn_w_in, 16)
                queue.dma_start(bo_rows[:], a["attn_bo"].unsqueeze(0).to_broadcast([128, C])).then_inc(attn_w_in, 16)

        @block.sync
        def _(sp):
            out_dram = out.rearrange("b (c p) k -> b p c k", p=P)

            def load(b):
                sp.wait_ge(S["x_lo"], b)
                sp.dma_start(x_sb[:], a["x"][b]).then_inc(x_in, 16)

            def store(b):
                sp.wait_ge(S["o"], b + 1)
                sp.dma_start(out_dram[b], o_sb[:]).then_inc(out_stored, 16)

            sp.sem_inc(out_stored, 16)
            sp.dma_start(x_sb[:], a["x"][0]).then_inc(x_in, 16)
            sp.dma_start(wk_sb[:], a["tok_W_k"].rearrange("(f d) k -> d f k", d=D)).then_inc(conv_w_in, 16)
            attn_loads(sp, 1)
            load(1)
            sp.dma_start(w1_raw[0:C, :], a["attn_W1"]).then_inc(mlp_w_in, 16)
            sp.dma_start(w1_raw[C:128, :], a["attn_W1"]).then_inc(mlp_w_in, 16)
            sp.dma_start(g2_col[0:C, :], column(a["attn_ln2_g"])).then_inc(mlp_w_in, 16)
            sp.dma_start(g2_col[C:128, :], column(a["attn_ln2_g"])).then_inc(mlp_w_in, 16)
            sp.dma_start(w2_sb[:], a["attn_W2"].rearrange("(k p) c -> p k c", p=128)).then_inc(mlp_w_in, 16)
            sp.dma_start(b2ln_col[:], column(a["attn_ln2_b"])).then_inc(mlp_w_in, 16)
            sp.dma_start(b1mT[:], a["attn_b1"].rearrange("(k p) -> p k", p=128), allow_slow_non_contiguous=True).then_inc(mlp_w_in, 16)
            sp.wait_ge(consts, 8)
            sp.dma_start(b2m_col[0:C, :], column(a["attn_b2"])).then_inc(mlp_w_in, 16)
            sp.dma_start(gam_col[0:C, :], column(a["ffn_gamma"])).then_inc(ffn_w_in, 16)
            sp.dma_start(gam_col[C:128, :], column(a["ffn_gamma"])).then_inc(ffn_w_in, 16)
            sp.dma_start(wr_raw[0:C, :], a["ffn_Wr"]).then_inc(ffn_w_in, 16)
            sp.dma_start(wr_raw[C:128, :], a["ffn_Wr"]).then_inc(ffn_w_in, 16)
            ew1_src = a["ffn_W1"].rearrange("e c h -> c e h")
            sp.dma_start(ew1_raw[0:C, :, :], ew1_src).then_inc(ffn_w_in, 16)
            sp.dma_start(ew1_raw[C:128, :, :], ew1_src).then_inc(ffn_w_in, 16)
            sp.dma_start(bet_col[:], column(a["ffn_beta"])).then_inc(ffn_w_in, 16)
            sp.dma_start(brc[:], a["ffn_br"].unsqueeze(0).to_broadcast([128, NE])).then_inc(ffn_w_in, 16)
            sp.dma_start(eb1T[:], a["ffn_b1"].rearrange("e h -> h e"), allow_slow_non_contiguous=True).then_inc(ffn_w_in, 16)
            for s in range(2):
                sp.dma_start(eb2[s * C:(s + 1) * C, :],
                             a["ffn_b2"].rearrange("(j s) c -> s c j", s=2)[s], allow_slow_non_contiguous=True).then_inc(ffn_w_in, 16)
            sp.dma_start(ew2[:], a["ffn_W2"].rearrange("e h c -> h e c")).then_inc(ffn_w_in, 16)
            with sp.Fori(2, LAST + 2) as b:
                load(b)
            with sp.Fori(LAST + 2, NB) as b:
                store(b - LAST - 2)
                load(b)
            with sp.Fori(NB - LAST - 2, NB) as b:
                store(b)
            sp.wait_ge(out_stored, 16 * NB + 16)

        @block.gpsimd
        def _(pool):
            pool.memset(ident[:], 0.0).then_inc(consts, 1)
            pool.memset(minus_half[:], -0.5).then_inc(consts, 1)
            pool.memset(ones[:], 1.0).then_inc(consts, 1)
            pool.memset(sel32[:], 0.0).then_inc(consts, 1)
            pool.memset(head_rows[:], 1.0).then_inc(consts, 1)
            pool.memset(head_mask[:], 1.0).then_inc(consts, 1)
            pool.memset(wT[:].bitcast(F32), 0.0).then_inc(consts, 1)
            pool.memset(b2m_col[:], 0.0).then_inc(consts, 1)
            pool.iota(iota8[:], [[1, NE]], base=0, channel_multiplier=0,
                      allow_small_or_imprecise_dtypes=True).then_inc(consts, 1)
            pool.wait_ge(consts, 1)
            pool.affine_select(out=ident[:], in_=ident[:], compare_op=ALU.not_equal, fill=1.0, base=0,
                               pattern=[[-1, 128]], channel_multiplier=1).then_inc(consts, 1)
            pool.wait_ge(consts, 9)
            for n, off in enumerate((0, NE)):
                if n:
                    pool.wait_ge(consts, 11)
                pool.affine_select(out=sel32[:], in_=sel32[:], compare_op=ALU.not_equal, fill=1.0,
                                   base=-off, pattern=[[-2, NP], [-1, 2], [0, C]],
                                   channel_multiplier=1).then_inc(consts, 1)
            pool.affine_select(out=head_rows[:], in_=head_rows[:], compare_op=ALU.is_ge, fill=0.0, base=0,
                               pattern=[[-KR, H], [1, HR]], channel_multiplier=0).then_inc(consts, 1)
            for s in range(2):
                pool.wait_ge(consts, 13 + s)
                m = head_mask[s * C:(s + 1) * C, :, :]
                pool.affine_select(out=m, in_=m, compare_op=ALU.is_ge, fill=0.0, base=-KR * s,
                                   pattern=[[-2 * KR, H // 2], [1, HR]], channel_multiplier=0).then_inc(consts, 1)
            pool.wait_ge(consts, 15)
            pool.affine_select(out=head_rows[:], in_=head_rows[:], compare_op=ALU.is_ge, fill=0.0,
                               base=KR - 1, pattern=[[KR, H], [-1, HR]], channel_multiplier=0).then_inc(consts, 1)
            for s in range(2):
                pool.wait_ge(consts, 16 + s)
                m = head_mask[s * C:(s + 1) * C, :, :]
                pool.affine_select(out=m, in_=m, compare_op=ALU.is_ge, fill=0.0, base=KR * s + KR - 1,
                                   pattern=[[2 * KR, H // 2], [-1, HR]], channel_multiplier=0).then_inc(consts, 1)

            def prep(ins):
                ins.then_inc(prep_pool, 1)

            def mlp_weights(b):
                if b == 0:
                    pool.wait_ge(ffn_w_in, FFN_DMAS)
                    prep(pool.tensor_copy(bet_rows[:], bet_col[:, 0:1].to_broadcast([C, 128])))
                    pool.wait_ge(prep_act, place(ACT_PREP, "w1_hi"))
                    prep(pool.tensor_tensor(w1_lo[:], w1_32[:], w1_hi[:].bitcast(F32), ALU.subtract))

            def expert_weights(b):
                if b == 0:
                    pool.wait_ge(prep_act, place(ACT_PREP, "wr_hi"))
                    prep(pool.tensor_tensor(wr_lo[:], wr32[:], wr_hi[:].bitcast(F32), ALU.subtract))
                    pool.wait_ge(prep_act, place(ACT_PREP, "ew1_hi"))
                    prep(pool.tensor_tensor(ew1_lo[:], ew1_32[:], ew1_hi[:].bitcast(F32), ALU.subtract))

            def b_rstd(b):
                pool.wait_ge(S["b_var"], b + 1)
                freed(pool, S["z2"], b)
                pool.tensor_tensor(b_rs[:], b_var[:], minus_half[0:P, 0:CH], ALU.pow).then_inc(S["b_rstd"], 1)

            def m_rstd(b):
                pool.wait_ge(S["m_var"], b + 1)
                freed(pool, S["z3"], b)
                pool.tensor_tensor(m_rs[:], m_var[:], minus_half[0:P, 0:CH], ALU.pow).then_inc(S["m_rstd"], 1)

            def a_rstd(b):
                pool.wait_ge(S["a_var"], b + 1)
                freed(pool, S["z"], b)
                pool.tensor_tensor(a_rs[:], a_var[:],
                                   minus_half[0:P, 0:2 * CH].rearrange("p (a c) -> p a c", a=2),
                                   ALU.pow).then_inc(S["a_rstd"], 1)

            def fx_plus_h1(b):
                pool.wait_ge(S["fx"], b + 1)
                pool.wait_ge(S["h1_kept"], b + 1)
                freed(pool, S["m_half"], b)
                pool.tensor_tensor(fxh[:], fx[:], h1_kept[:], ALU.add).then_inc(S["fxh"], 1)

            def residual(b):
                pool.wait_ge(S["a_hc"], b + 1)
                pool.wait_ge(S["a_rstd"], b + 1)
                pool.tensor_tensor(zr0[:], hc[:], each(a_rs[:, 0, :]), ALU.mult).then_inc(S["z_res0"], 1)
                pool.wait_ge(S["z_res0"], b + 1)
                freed(pool, S["fx"], b)
                if isinstance(b, int) and b == 0:
                    pool.wait_ge(attn_w_in, ATTN_DMAS)
                pool.tensor_tensor(zr[:], zr0[:], bo_rows[0:P, :].unsqueeze(1).to_broadcast([P, CH, C]),
                                   ALU.add).then_inc(S["z_res"], 1)

            def keep_h1(b):
                pool.wait_ge(S["h1"], b + 1)
                freed(pool, S["fxh"], b)
                pool.tensor_tensor(h1_kept[:], h1[:], each(ones[0:P, :]), ALU.mult).then_inc(S["h1_kept"], 1)

            def keep_z(b):
                pool.wait_ge(S["z"], b + 1)
                freed(pool, S["ps_G"], b)
                pool.tensor_tensor(z_kept[:], z[:], each(ones[0:P, :]), ALU.mult).then_inc(S["z_kept"], 1)

            def keep_h2(b):
                pool.wait_ge(S["h2"], b + 1)
                freed(pool, S["o_half"], b)
                pool.tensor_tensor(h2_kept[:], h2[:], each(ones[0:P, :]), ALU.mult).then_inc(S["h2_kept"], 1)

            def sum_first(b):
                pool.wait_ge(gated[0], b + 1)
                pool.wait_ge(gated[1], b + 1)
                pool.tensor_tensor(sum0[:], yg[0][:], yg[1][:], ALU.add).then_inc(S["sum0"], 1)

            def sum_rest(b):
                pool.wait_ge(gated[2], b + 1)
                pool.wait_ge(gated[3], b + 1)
                pool.tensor_tensor(sum1[:], yg[2][:], yg[3][:], ALU.add).then_inc(S["sum1"], 1)
                pool.wait_ge(S["sum0"], b + 1)
                pool.wait_ge(S["sum1"], b + 1)
                pool.tensor_tensor(sum_all[:], sum0[:], sum1[:], ALU.add).then_inc(S["sum_all"], 1)

            def opening(A, B, M, E, T):
                do(a_rstd, B)
                do(b_rstd, M)
                do(m_rstd, E)
                do(keep_z, B)
                do(mlp_weights, B)
                do(residual, B)
                do(fx_plus_h1, M)
                do(keep_h1, B)
                do(expert_weights, B)
                do(keep_h2, E)
                do(sum_rest, T)
                do(sum_first, T)

            def step(A, B, M, E, T):
                do(a_rstd, B)
                do(b_rstd, M)
                do(fx_plus_h1, M)
                do(m_rstd, E)
                do(sum_first, T)
                do(keep_z, B)
                do(residual, B)
                do(keep_h1, B)
                do(sum_rest, T)
                do(keep_h2, E)

            def closing(A, B, M, E, T):
                do(a_rstd, B)
                do(b_rstd, M)
                do(m_rstd, E)
                do(residual, B)
                do(fx_plus_h1, M)
                do(keep_h1, B)
                do(keep_z, B)
                do(sum_first, T)
                do(sum_rest, T)
                do(keep_h2, E)

            run(pool, opening, step, closing, {})

        @block.scalar
        def _(act):
            act.dma_start(filtT[:], a["tok_filt"]).then_inc(conv_w_in, 16)
            act.dma_start(bk_col[:], column(a["tok_b_k"])).then_inc(conv_w_in, 16)
            attn_loads(act, 0)
            act.wait_ge(consts, 10)
            act.activation(ident_r[:], ident[:], ACT.Copy).then_inc(rounded_ident, 1)

            def scaled(out, src, factor):
                act.activation(out, src, ACT.Identity, scale=factor).then_inc(prep_act, 1)

            def mlp_weights(b):
                if b == 0:
                    act.wait_ge(mlp_w_in, MLP_DMAS)
                    scaled(w1_32[:], w1_raw[:], g2_col[:, 0:1])
                    scaled(w1_hi[:], w1_raw[:], g2_col[:, 0:1])

            def expert_weights(b):
                if b == 0:
                    act.wait_ge(ffn_w_in, FFN_DMAS)
                    scaled(wr32[:], wr_raw[:], gam_col[:, 0:1])
                    scaled(wr_hi[:], wr_raw[:], gam_col[:, 0:1])
                    act.activation(sel[:], sel32[:].rearrange("p j s c -> p j (s c)"), ACT.Copy).then_inc(prep_act, 1)
                    scaled(ew1_32[:], ew1_raw[:].rearrange("p e h -> p (e h)"), gam_col[:, 0:1])
                    scaled(ew1_hi[:], ew1_raw[:].rearrange("p e h -> p (e h)"), gam_col[:, 0:1])

            def copy_zT(b):
                act.wait_ge(S["ps_zT"], b + 1)
                freed(act, S["ps_L"], b)
                act.activation(zT[:], cols(B1), ACT.Copy).then_inc(S["zT"], 1)

            def copy_z2T(b):
                act.wait_ge(S["ps_z2T"], b + 1)
                freed(act, S["ps_m1"], b)
                act.activation(z2T[:], cols(BM), ACT.Copy).then_inc(S["z2T"], 1)

            def copy_z3T(b):
                act.wait_ge(S["ps_z3T"], b + 1)
                freed(act, ps_h[NE - 1], b)
                act.activation(z3T[:], cols(BH0), ACT.Copy).then_inc(S["z3T"], 1)

            def x_high(b):
                act.wait_ge(x_in, 16 * b + 16)
                freed(act, S["ps_conv"], b)
                act.activation(x_hi[:], x_sb[:], ACT.Copy).then_inc(S["x_hi"], 1)

            def key_query_logits(b):
                act.wait_ge(S["ps_L"], b + 1)
                freed(act, S["ps_k"], b)
                act.activation(kq[:], B2[0:2 * HR, 0:NT], ACT.Identity, bias=bqk_col[:, 0:1]).then_inc(S["L"], 1)

            def key_exp(b):
                act.wait_ge(S["k_negmax"], b + 1)
                act.wait_ge(S["L"], b + 1)
                freed(act, S["k_rden"], b)
                act.activation(kq[0:HR, :], kq[0:HR, :], ACT.Exp, bias=k_negmax[:, 0:1],
                               accum_out=k_den[:, 0:1]).then_inc(S["k_exp"], 1)

            def query_exp(b):
                act.wait_ge(S["q_sub"], b + 1)
                freed(act, S["q_norm"], b)
                act.activation(q_e[:], q_sub[:], ACT.Exp).then_inc(S["q_exp"], 1)

            def gate_tanh(b):
                act.wait_ge(S["gap"], b + 1)
                freed(act, S["p"], b)
                act.activation(th[:], gap[:], ACT.Tanh, scale=0.5).then_inc(S["th"], 1)

            def copy_late_taps(b):
                act.wait_ge(S["ps_conv"], b + 1)
                freed(act, S["pre"], b)
                act.activation(late_taps[:], BA[C:128, HALF:HALF + NT], ACT.Copy).then_inc(S["late_taps"], 1)

            def copy_qT(b):
                act.wait_ge(S["ps_qT"], b + 1)
                freed(act, S["ps_at"], b)
                act.activation(qT[:], B1[0:3 * HR, 0:NT], ACT.Copy).then_inc(S["qT"], 1)

            def copy_wT(b):
                act.wait_ge(S["ps_w"], b + 1)
                freed(act, ps_wb[NP - 1], b)
                act.activation(wT[0:2 * NE, :], BW[0:2 * NE, 0:NT], ACT.Copy).then_inc(S["wT"], 1)

            def mlp_out(b):
                act.wait_ge(S["ps_m2"], b + 1)
                freed(act, S["ps_mT"], b)
                act.activation(mF[:], cols(BM), ACT.Identity, bias=b2m_col[:, 0:1]).then_inc(S["mlp_F"], 1)

            def z2_high(b):
                act.wait_ge(S["z2"], b + 1)
                freed(act, S["ps_z2T"], b)
                act.activation(z2hl[:, :, 0, :], z2[:], ACT.Copy).then_inc(S["z2_hi"], 1)

            def tokens(b):
                act.wait_ge(S["ps_pre"], b + 1)
                freed(act, S["a_hc"], b)
                freed(act, S["h1_kept"], b)
                act.activation(h1[:], row3(BA, C), ACT.Relu).then_inc(S["h1"], 1)

            def z3_high(b):
                act.wait_ge(S["z3"], b + 1)
                freed(act, S["ps_z3T"], b)
                act.activation(z3hl[:, :, 0, :], z3[:], ACT.Copy).then_inc(S["z3_hi"], 1)

            def z_high(b):
                act.wait_ge(S["z"], b + 1)
                freed(act, S["ps_zT"], b)
                act.activation(zhl[:, :, 0, :], z[:], ACT.Copy).then_inc(S["z_hi"], 1)

            def hidden(b, e):
                act.wait_ge(ps_h[e], b + 1)
                if e < 4:
                    freed(act, ps_y[(e + 4) // 2], b)
                else:
                    act.wait_ge(ps_y[(e - 4) // 2], b + 1)
                act.activation(eg[e % 4][:], cols(BH[e % 2]), ACT.Gelu, bias=eb1[:, e:e + 1]).then_inc(gelu[e], 1)

            def mlp_hidden(b, k):
                act.wait_ge(S["ps_m1"] if k else S["ps_m0"], b + 1)
                freed(act, S["ps_m2"], b)
                act.activation(mg[k][:], cols(BM), ACT.Gelu,
                               bias=b1m[:, k:k + 1]).then_inc(S["mlp_g1"] if k else S["mlp_g0"], 1)

            def outputs(b, j):
                act.wait_ge(ps_y[j], b + 1)
                if j < 2:
                    freed(act, gated[j + 2], b)
                else:
                    act.wait_ge(gated[j - 2], b + 1)
                act.activation(y_ev[j % 2][:], cols(BY), ACT.Identity, bias=eb2[:, j:j + 1]).then_inc(yev[j], 1)

            def attn_prepared():
                act.wait_ge(prep_dve, place(DVE_PREP, "bqk_col"))
                act.wait_ge(consts, 18)

            def mlp_prepared():
                act.wait_ge(prep_dve, place(DVE_PREP, "b1m"))
                act.wait_ge(mlp_w_in, MLP_DMAS)

            def experts_prepared():
                act.wait_ge(prep_dve, place(DVE_PREP, "br"))
                act.wait_ge(ffn_w_in, FFN_DMAS)

            def opening(A, B, M, E, T):
                do(hidden, T, 6)
                do(z_high, B)
                do(x_high, A)
                do(z2_high, M)
                do(copy_zT, B)
                do(z3_high, E)
                do(key_query_logits, B)
                do(mlp_weights, B)
                do(copy_z2T, M)
                do(copy_z3T, E)
                do(key_exp, B)
                do(hidden, T, 7)
                do(outputs, T, 2)
                do(query_exp, B)
                do(mlp_hidden, M, 0)
                do(copy_late_taps, A)
                do(hidden, E, 0)
                do(gate_tanh, E)
                do(mlp_hidden, M, 1)
                do(hidden, E, 1)
                do(expert_weights, B)
                do(outputs, T, 3)
                do(copy_qT, B)
                do(tokens, A)
                do(mlp_out, M)
                do(hidden, E, 2)
                do(hidden, E, 3)
                do(copy_wT, E)
                do(outputs, E, 0)
                do(hidden, E, 4)
                do(hidden, E, 5)
                do(outputs, E, 1)

            def step(A, B, M, E, T):
                do(hidden, T, 6)
                do(z_high, B)
                do(hidden, T, 7)
                do(outputs, T, 2)
                do(x_high, A)
                do(copy_zT, B)
                do(z2_high, M)
                do(z3_high, E)
                do(outputs, T, 3)
                do(key_query_logits, B)
                do(copy_z2T, M)
                do(copy_z3T, E)
                do(key_exp, B)
                do(query_exp, B)
                do(mlp_hidden, M, 0)
                do(copy_late_taps, A)
                do(hidden, E, 0)
                do(gate_tanh, E)
                do(mlp_hidden, M, 1)
                do(tokens, A)
                do(copy_qT, B)
                do(hidden, E, 1)
                do(mlp_out, M)
                do(hidden, E, 2)
                do(copy_wT, E)
                do(hidden, E, 3)
                do(outputs, E, 0)
                do(hidden, E, 4)
                do(hidden, E, 5)
                do(outputs, E, 1)

            def closing(A, B, M, E, T):
                do(hidden, T, 6)
                do(z_high, B)
                do(hidden, T, 7)
                do(outputs, T, 2)
                do(tokens, A)
                do(z2_high, M)
                do(copy_zT, B)
                do(z3_high, E)
                do(outputs, T, 3)
                do(x_high, A)
                do(key_query_logits, B)
                do(copy_z2T, M)
                do(copy_z3T, E)
                do(key_exp, B)
                do(query_exp, B)
                do(mlp_hidden, M, 0)
                do(hidden, E, 0)
                do(gate_tanh, E)
                do(mlp_hidden, M, 1)
                do(hidden, E, 1)
                do(copy_qT, B)
                do(mlp_out, M)
                do(hidden, E, 2)
                do(copy_wT, E)
                do(hidden, E, 3)
                do(outputs, E, 0)
                do(hidden, E, 4)
                do(hidden, E, 5)
                do(outputs, E, 1)
                do(copy_late_taps, A)

            run(act, opening, step, closing, {1: attn_prepared, 2: mlp_prepared, 3: experts_prepared})

        @block.vector
        def _(dve):
            def prep(ins):
                ins.then_inc(prep_dve, 1)

            dve.wait_ge(conv_w_in, CONV_DMAS)
            prep(dve.tensor_tensor(wc32[:].rearrange("d t h k -> d h t k"),
                                   wk_sb[:].rearrange("d (h t) k -> d h t k", h=2),
                                   filtT[:].rearrange("d (h t) -> d h t", h=2).unsqueeze(3)
                                   .to_broadcast([D, 2, HALF, C]), ALU.mult))
            dve.wait_ge(prep_dve, place(DVE_PREP, "wc32"))
            prep(dve.tensor_copy(wc_hi[:], wc32[:].rearrange("d t h k -> d t (h k)")))
            dve.wait_ge(prep_dve, place(DVE_PREP, "wc_hi"))
            prep(dve.tensor_tensor(wc_lo[:], wc32[:].rearrange("d t h k -> d t (h k)"),
                                   wc_hi[:].bitcast(F32), ALU.subtract))

            def made(n):
                dve.wait_ge(prep_dve, place(DVE_PREP, n))

            def summed(n):
                dve.wait_ge(prep_pe, place(PE_PREP, n))

            def prepare_first():
                dve.wait_ge(attn_w_in, ATTN_DMAS)
                dve.wait_ge(consts, 18)
                summed("ln_bx")
                prep(dve.tensor_tensor(bxg[:], BM[0:DH, 0:H], bxT[:], ALU.add))

            def prepare_logits():
                summed("wqk")
                prep(dve.tensor_scalar(wqk32[:].rearrange("p (t h r) -> p t h r", t=2, h=H),
                                       B2[:, 0:2 * HR].rearrange("p (h t r) -> p t h r", t=2, h=H),
                                       g1_col[:, 0:1], None, ALU.mult))
                made("wqk32")
                prep(dve.tensor_copy(wqk_hi[:], wqk32[:]))
                made("wqk_hi")
                prep(dve.tensor_tensor(wqk_lo[:], wqk32[:], wqk_hi[:].bitcast(F32), ALU.subtract))
                summed("bqk_row")
                prep(dve.tensor_copy(bqk_row[:].rearrange("p (t h r) -> p t h r", t=2, h=H),
                                     BH0[0:1, 0:2 * HR].rearrange("p (h t r) -> p t h r", t=2, h=H)))

            def prepare_bias():
                summed("bqk_col")
                prep(dve.tensor_copy(bqk_col[:], BH1[0:2 * HR, 0:1]))

            def values_weights(b):
                if b == 0:
                    prep(dve.tensor_tensor(bx_heads[:], head_rows[:], bxg[:].unsqueeze(2).to_broadcast([DH, H, HR]), ALU.mult))
                    summed("wvo")
                    prep(dve.tensor_copy(wvo[:], BW[0:DH, 0:H * C].rearrange("d (h c) -> d h c", h=H)))

            def rows_weights(b):
                if b == 0:
                    summed("u")
                    for s in range(2):
                        prep(dve.tensor_scalar(u_pair[s * C:(s + 1) * C, :, :],
                                               BY[s * C:(s + 1) * C, 0:H * C].rearrange("p (j s c) -> p j s c", s=2, c=C)[:, :, s, :],
                                               g1_col[s * C:(s + 1) * C, 0:1], None, ALU.mult))
                    summed("u_bias")
                    prep(dve.tensor_copy(u_bias[:], BH0[0:HR, 0:C]))

            def prepare_biases():
                dve.wait_ge(mlp_w_in, MLP_DMAS)
                dve.wait_ge(ffn_w_in, FFN_DMAS)
                summed("b1m")
                prep(dve.tensor_tensor(b1m[:], BH0[:, 0:2], b1mT[:], ALU.add))
                summed("eb1")
                prep(dve.tensor_tensor(eb1[:], BH1[:, 0:NE], eb1T[:], ALU.add))
                summed("br")
                prep(dve.tensor_tensor(br_rows[:], BY[:, 0:NE], brc[:], ALU.add))

            def stats(src, st, done, b):
                for c in range(CH):
                    ins = dve.bn_stats(st[:, c, :], src[:, c, :])
                ins.then_inc(done, 1)

            def mean_variance(st, mv, stats_done, done, b):
                count = b + 1
                plain(dve)
                dve.wait_ge(stats_done, count)
                for c in range(CH):
                    ins = dve.bn_aggr(mv[:, c, :], st[:, c, :])
                ins.then_inc(done, 1)

            def x_low(b):
                dve.wait_ge(S["x_hi"], b + 1)
                freed(dve, S["ps_conv"], b)
                dve.tensor_tensor(x_lo[:], x_sb[:], x_hi[:].bitcast(F32), ALU.subtract).then_inc(S["x_lo"], 1)

            def key_max(b):
                dve.wait_ge(S["L"], b + 1)
                freed(dve, S["k_exp"], b)
                dve.tensor_reduce(k_negmax[:], kq[0:HR, :], AX_X, ALU.max, negate=True).then_inc(S["k_negmax"], 1)

            def query_max(b):
                q_ps = B1[0:P, 0:CH * HR].rearrange("p (g r) -> p g r", r=KR)
                dve.wait_ge(S["ps_q"], b + 1)
                dve.tensor_reduce(q_max[:], q_ps, AX_X, ALU.max).then_inc(S["q_max"], 1)

            def query_shift(b):
                q_ps = B1[0:P, 0:CH * HR].rearrange("p (g r) -> p g r", r=KR)
                dve.wait_ge(S["q_max"], b + 1)
                freed(dve, S["q_exp"], b)
                dve.tensor_tensor(q_sub[:], q_ps, q_max[:].unsqueeze(2).to_broadcast([P, CH * H, KR]),
                                  ALU.subtract).then_inc(S["q_sub"], 1)

            def query_sum(b):
                dve.wait_ge(S["q_exp"], b + 1)
                dve.tensor_reduce(q_sum[:], q_e[:], AX_X, ALU.add).then_inc(S["q_sum"], 1)

            def query_reciprocal(b):
                dve.wait_ge(S["q_sum"], b + 1)
                dve.reciprocal(q_rec[:], q_sum[:]).then_inc(S["q_rec"], 1)

            def query_norm(b):
                dve.wait_ge(S["q_rec"], b + 1)
                dve.tensor_tensor(q_n[:].rearrange("p c (h r) -> p (c h) r", r=KR), q_e[:],
                                  q_rec[:].unsqueeze(2).to_broadcast([P, CH * H, KR]),
                                  ALU.mult).then_inc(S["q_norm"], 1)

            def query_high(b):
                dve.wait_ge(S["q_norm"], b + 1)
                freed(dve, S["ps_qT"], b)
                dve.tensor_copy(qhl[:, :, 0, :], q_n[:])
                dve.tensor_copy(qhl[:, :, 2, :], q_n[:]).then_inc(S["q_hi"], 1)

            def query_low(b):
                dve.wait_ge(S["q_hi"], b + 1)
                dve.tensor_tensor(qhl[:, :, 1, :], q_n[:], qhl[:, :, 0, :].bitcast(F32),
                                  ALU.subtract).then_inc(S["q_lo"], 1)

            def keys(b):
                dve.wait_ge(S["ps_k"], b + 1)
                dve.wait_ge(S["z_kept"], b + 1)
                freed(dve, S["ps_G"], b)
                dve.tensor_copy(EkT[:], row3(B2, HR)).then_inc(S["EkT"], 1)
                dve.wait_ge(S["k_exp"], b + 1)
                dve.reciprocal(k_rden[:], k_den[:]).then_inc(S["k_rden"], 1)

            def key_sums(b):
                dve.wait_ge(S["ps_G"], b + 1)
                dve.wait_ge(S["k_rden"], b + 1)
                freed(dve, S["ps_GT"], b)
                dve.tensor_scalar(Gd[:], B2[0:HR, 0:C].unsqueeze(1).to_broadcast([HR, 2, C]),
                                  k_rden[:, 0:1], None, ALU.mult).then_inc(S["G_norm"], 1)

            def key_sums_by_head(b):
                dve.wait_ge(S["ps_GT"], b + 1)
                freed(dve, S["ps_M"], b)
                dve.tensor_tensor(Gx[:], B2[:, 0:HR].unsqueeze(1).to_broadcast([128, H // 2, HR]),
                                  head_mask[:], ALU.mult).then_inc(S["G_heads"], 1)

            def value_rows_sum(b):
                dve.wait_ge(S["ps_M"], b + 1)
                dve.tensor_tensor(Mf[:], B2[0:HR, 0:C], u_bias[:], ALU.add).then_inc(S["M_sum"], 1)

            def value_rows_high(b):
                dve.wait_ge(S["M_sum"], b + 1)
                freed(dve, S["ps_at"], b)
                dve.tensor_copy(M3[0:HR, :], Mf[:]).then_inc(S["M_hi"], 1)
                dve.tensor_copy(M3[HR:2 * HR, :], Mf[:])

            def value_rows_low(b):
                dve.wait_ge(S["M_hi"], b + 1)
                dve.tensor_tensor(M3[2 * HR:3 * HR, :], Mf[:], M3[0:HR, :].bitcast(F32),
                                  ALU.subtract).then_inc(S["M_stack"], 1)

            def logits(b):
                dve.wait_ge(S["ps_lg"], b + 1)
                dve.tensor_tensor(lg[:], row3(BW, NE), br_rows[0:P, :].unsqueeze(1).to_broadcast([P, CH, NE]),
                                  ALU.add).then_inc(S["lg"], 1)

            def top_two(b):
                count = b + 1
                plain(dve)
                dve.wait_ge(S["lg"], count)
                for c in range(CH):
                    ins = dve.max(top[:, c, :], lg[:, c, :])
                ins.then_inc(S["top"], 1)

            def top_places(b):
                count = b + 1
                plain(dve)
                dve.wait_ge(S["top"], count)
                for c in range(CH):
                    ins = dve.max_index(idx[:, c, :], top[:, c, :], lg[:, c, :])
                ins.then_inc(S["idx"], 1)
                freed(dve, S["th"], b)
                dve.tensor_tensor(gap[:], top[:, :, 1], top[:, :, 0], ALU.subtract).then_inc(S["gap"], 1)

            def one_hot(b):
                dve.wait_ge(S["idx"], b + 1)
                dve.tensor_tensor(hot[:], idx[:, :, 0:2].unsqueeze(3).to_broadcast([P, CH, 2, NE]),
                                  iota8[0:P, :].unsqueeze(1).unsqueeze(1).to_broadcast([P, CH, 2, NE]),
                                  ALU.is_equal).then_inc(S["hot"], 1)

            def gate_pair(b):
                dve.wait_ge(S["th"], b + 1)
                dve.tensor_scalar(p12[:, :, 0], th[:], -0.5, 0.5, ALU.mult, ALU.add)
                dve.tensor_scalar(p12[:, :, 1], th[:], 0.5, 0.5, ALU.mult, ALU.add).then_inc(S["p"], 1)

            def place_gates(b):
                dve.wait_ge(S["p"], b + 1)
                dve.wait_ge(S["hot"], b + 1)
                dve.tensor_tensor(hot_p[:], hot[:], p12[:].unsqueeze(3).to_broadcast([P, CH, 2, NE]),
                                  ALU.mult).then_inc(S["hot_p"], 1)

            def gates(b):
                dve.wait_ge(S["hot_p"], b + 1)
                dve.tensor_tensor(w[:], hot_p[:, :, 0, :], hot_p[:, :, 1, :], ALU.add).then_inc(S["w"], 1)

            def gates_high(b):
                dve.wait_ge(S["w"], b + 1)
                freed(dve, S["ps_w"], b)
                dve.tensor_copy(whl[:, :, 0, :], w[:]).then_inc(S["w_hi"], 1)

            def gates_low(b):
                dve.wait_ge(S["w_hi"], b + 1)
                dve.tensor_tensor(whl[:, :, 1, :], w[:], whl[:, :, 0, :].bitcast(F32),
                                  ALU.subtract).then_inc(S["w_lo"], 1)

            def windows(b):
                dve.wait_ge(S["late_taps"], b + 1)
                freed(dve, S["ps_pre"], b)
                dve.scalar_tensor_tensor(out=pre[:], in0=BA[0:C, 0:NT], scalar=bk_col[:, 0:1],
                                         in1=late_taps[:], op0=ALU.add, op1=ALU.add).then_inc(S["pre"], 1)

            def gate(b, j):
                dve.wait_ge(yev[j], b + 1)
                dve.wait_ge(ps_wb[j], b + 1)
                if j < 2:
                    freed(dve, S["sum0"], b)
                dve.tensor_tensor(yg[j][:], y_ev[j % 2][:], cols(BW), ALU.mult).then_inc(gated[j], 1)

            def attn_residual(b):
                dve.wait_ge(S["ps_at"], b + 1)
                dve.wait_ge(S["z_res"], b + 1)
                freed(dve, S["fxh"], b)
                dve.tensor_tensor(fx[:], row3(B2, C), zr[:], ALU.add).then_inc(S["fx"], 1)

            def b_stats(b):
                dve.wait_ge(S["fx"], b + 1)
                stats(fx, b_st, S["b_stats"], b)

            def b_mean_variance(b):
                mean_variance(b_st, b_mv, S["b_stats"], S["b_mv"], b)

            def b_center(b):
                dve.wait_ge(S["b_mv"], b + 1)
                freed(dve, S["b_rstd"], b)
                dve.tensor_scalar(b_var[:], b_mv[:, :, 1], EPS, None, ALU.add).then_inc(S["b_var"], 1)
                dve.tensor_tensor(b_hc[:], fx[:], each(b_mv[:, :, 0]), ALU.subtract).then_inc(S["b_hc"], 1)

            def b_normed(b):
                dve.wait_ge(S["b_rstd"], b + 1)
                dve.wait_ge(S["b_hc"], b + 1)
                freed(dve, S["z2_hi"], b)
                dve.tensor_tensor(z2[:], b_hc[:], each(b_rs[:]), ALU.mult).then_inc(S["z2"], 1)

            def z2_low(b):
                dve.wait_ge(S["z2_hi"], b + 1)
                dve.tensor_tensor(z2hl[:, :, 1, :], z2[:], z2hl[:, :, 0, :].bitcast(F32),
                                  ALU.subtract).then_inc(S["z2_lo"], 1)

            def mlp_residual_half(b):
                m_ps = row3(BM, 2 * C)
                dve.wait_ge(S["ps_mT"], b + 1)
                dve.wait_ge(S["fxh"], b + 1)
                dve.tensor_tensor(m_half[:], m_ps[:, :, 0:C], fxh[:], ALU.add).then_inc(S["m_half"], 1)

            def mlp_residual(b):
                m_ps = row3(BM, 2 * C)
                dve.wait_ge(S["m_half"], b + 1)
                freed(dve, S["h2_kept"], b)
                dve.tensor_tensor(h2[:], m_ps[:, :, C:2 * C], m_half[:], ALU.add).then_inc(S["h2"], 1)

            def m_stats(b):
                dve.wait_ge(S["h2"], b + 1)
                stats(h2, m_st, S["m_stats"], b)

            def m_mean_variance(b):
                mean_variance(m_st, m_mv, S["m_stats"], S["m_mv"], b)

            def m_center(b):
                dve.wait_ge(S["m_mv"], b + 1)
                freed(dve, S["m_rstd"], b)
                dve.tensor_scalar(m_var[:], m_mv[:, :, 1], 1.0 + EPS, EPS * EPS, ALU.mult, ALU.add).then_inc(S["m_var"], 1)
                dve.tensor_tensor(m_hc[:], h2[:], each(m_mv[:, :, 0]), ALU.subtract).then_inc(S["m_hc"], 1)

            def m_normed(b):
                dve.wait_ge(S["m_rstd"], b + 1)
                dve.wait_ge(S["m_hc"], b + 1)
                freed(dve, S["z3_hi"], b)
                dve.tensor_tensor(z3[:], m_hc[:], each(m_rs[:]), ALU.mult).then_inc(S["z3"], 1)

            def z3_low(b):
                dve.wait_ge(S["z3_hi"], b + 1)
                dve.tensor_tensor(z3hl[:, :, 1, :], z3[:], z3hl[:, :, 0, :].bitcast(F32),
                                  ALU.subtract).then_inc(S["z3_lo"], 1)

            def a_stats(b):
                dve.wait_ge(S["h1"], b + 1)
                stats(h1, a_st, S["a_stats"], b)

            def a_mean_variance(b):
                mean_variance(a_st, a_mv, S["a_stats"], S["a_mv"], b)

            def a_center(b):
                dve.wait_ge(S["a_mv"], b + 1)
                freed(dve, S["a_rstd"], b)
                dve.tensor_scalar(a_var[:, 0, :], a_mv[:, :, 1], EPS, None, ALU.add)
                dve.tensor_scalar(a_var[:, 1, :], a_mv[:, :, 1], 1.0 + EPS, EPS * EPS, ALU.mult,
                                  ALU.add).then_inc(S["a_var"], 1)
                freed(dve, S["z_res0"], b)
                dve.tensor_tensor(hc[:], h1[:], each(a_mv[:, :, 0]), ALU.subtract).then_inc(S["a_hc"], 1)

            def a_normed(b):
                dve.wait_ge(S["a_rstd"], b + 1)
                dve.wait_ge(S["a_hc"], b + 1)
                freed(dve, S["z_kept"], b)
                freed(dve, S["z_hi"], b)
                dve.tensor_tensor(z[:], hc[:], each(a_rs[:, 1, :]), ALU.mult).then_inc(S["z"], 1)

            def z_low(b):
                dve.wait_ge(S["z_hi"], b + 1)
                dve.tensor_tensor(zhl[:, :, 1, :], z[:], zhl[:, :, 0, :].bitcast(F32),
                                  ALU.subtract).then_inc(S["z_lo"], 1)

            def result_half(b):
                o_ps = row3(BY, 2 * C)
                dve.wait_ge(S["ps_out"], b + 1)
                dve.wait_ge(S["h2_kept"], b + 1)
                dve.tensor_tensor(o_half[:], o_ps[:, :, 0:C], h2_kept[:], ALU.add).then_inc(S["o_half"], 1)

            def result(b):
                o_ps = row3(BY, 2 * C)
                dve.wait_ge(S["o_half"], b + 1)
                dve.wait_ge(out_stored, 16 * b + 16)
                dve.tensor_tensor(o_sb[:], o_ps[:, :, C:2 * C], o_half[:], ALU.add).then_inc(S["o"], 1)

            def opening(A, B, M, E, T):
                do(z_low, B)
                do(b_normed, M)
                do(gate, T, 3)
                do(x_low, A)
                do(z2_low, M)
                do(m_normed, E)
                do(z3_low, E)
                do(key_max, B)
                do(values_weights, B)
                do(query_max, B)
                do(query_shift, B)
                do(logits, E)
                do(top_two, E)
                do(keys, B)
                do(query_sum, B)
                do(query_reciprocal, B)
                do(top_places, E)
                do(query_norm, B)
                do(key_sums, B)
                do(query_high, B)
                do(one_hot, E)
                do(query_low, B)
                do(key_sums_by_head, B)
                do(windows, A)
                do(gate_pair, E)
                do(place_gates, E)
                do(gates, E)
                do(rows_weights, B)
                do(value_rows_sum, B)
                do(value_rows_high, B)
                do(gate, T, 2)
                do(gates_high, E)
                do(value_rows_low, B)
                do(gates_low, E)
                do(a_stats, A)
                do(a_mean_variance, A)
                do(attn_residual, B)
                do(a_center, A)
                do(mlp_residual_half, M)
                do(b_stats, B)
                do(result, T)
                do(result_half, T)
                do(mlp_residual, M)
                do(b_mean_variance, B)
                do(m_stats, M)
                do(b_center, B)
                do(gate, E, 0)
                do(a_normed, A)
                do(m_mean_variance, M)
                do(m_center, M)
                do(gate, E, 1)

            def step(A, B, M, E, T):
                do(z_low, B)
                do(m_normed, E)
                do(b_normed, M)
                do(gate, T, 2)
                do(x_low, A)
                do(z2_low, M)
                do(z3_low, E)
                do(gate, T, 3)
                do(key_max, B)
                do(query_max, B)
                do(logits, E)
                do(query_shift, B)
                do(top_two, E)
                do(keys, B)
                do(query_sum, B)
                do(top_places, E)
                do(query_reciprocal, B)
                do(query_norm, B)
                do(key_sums, B)
                do(query_high, B)
                do(one_hot, E)
                do(query_low, B)
                do(key_sums_by_head, B)
                do(windows, A)
                do(gate_pair, E)
                do(value_rows_sum, B)
                do(place_gates, E)
                do(value_rows_high, B)
                do(gates, E)
                do(gates_high, E)
                do(value_rows_low, B)
                do(gates_low, E)
                do(a_stats, A)
                do(result_half, T)
                do(a_mean_variance, A)
                do(result, T)
                do(attn_residual, B)
                do(a_center, A)
                do(mlp_residual_half, M)
                do(b_stats, B)
                do(mlp_residual, M)
                do(b_mean_variance, B)
                do(m_stats, M)
                do(b_center, B)
                do(gate, E, 0)
                do(m_mean_variance, M)
                do(a_normed, A)
                do(m_center, M)
                do(gate, E, 1)

            def closing(A, B, M, E, T):
                do(z_low, B)
                do(a_center, A)
                do(b_normed, M)
                do(m_normed, E)
                do(x_low, A)
                do(gate, T, 2)
                do(z2_low, M)
                do(windows, A)
                do(z3_low, E)
                do(gate, T, 3)
                do(key_max, B)
                do(query_max, B)
                do(logits, E)
                do(query_shift, B)
                do(top_two, E)
                do(top_places, E)
                do(query_sum, B)
                do(keys, B)
                do(query_reciprocal, B)
                do(query_norm, B)
                do(key_sums, B)
                do(one_hot, E)
                do(key_sums_by_head, B)
                do(query_high, B)
                do(gate_pair, E)
                do(query_low, B)
                do(place_gates, E)
                do(a_mean_variance, A)
                do(gates, E)
                do(value_rows_sum, B)
                do(gates_high, E)
                do(result_half, T)
                do(value_rows_high, B)
                do(value_rows_low, B)
                do(gates_low, E)
                do(result, T)
                do(attn_residual, B)
                do(a_normed, A)
                do(mlp_residual_half, M)
                do(b_stats, B)
                do(mlp_residual, M)
                do(a_stats, A)
                do(m_stats, M)
                do(gate, E, 0)
                do(m_mean_variance, M)
                do(b_mean_variance, B)
                do(b_center, B)
                do(m_center, M)
                do(gate, E, 1)

            def first_step():
                x_low(0)
                windows(0)
                prepare_first()
                a_stats(0)
                a_mean_variance(0)
                a_center(0)
                prepare_logits()
                a_normed(0)
                prepare_bias()

            run(dve, opening, step, closing, {0: first_step, 2: prepare_biases}, own_first=True)

        @block.tensor
        def _(pe):
            def made(n):
                pe.wait_ge(prep_dve, place(DVE_PREP, n))

            def prepare_first():
                pe.wait_ge(attn_w_in, ATTN_DMAS)
                pe.wait_ge(consts, 18)
                for h in range(H):
                    ins = pe.matmul(BM[0:DH, h:h + 1], wx_sb[:, h * DH:(h + 1) * DH], b1_col[:], start=True, stop=True)
                ins.then_inc(prep_pe, 1)

            def prepare_rest():
                made("bxg")                                         
                for h in range(H):
                    ins = pe.matmul(B2[:, h * 2 * KR:(h + 1) * 2 * KR], wxT2[:, h, :, :].rearrange("d s c -> d (s c)"),
                                    wkq_sb[:], start=True, stop=True)
                ins.then_inc(prep_pe, 1)
                for h in range(H):
                    ins = pe.matmul(BH0[0:1, h * 2 * KR:(h + 1) * 2 * KR], bxg[:, h:h + 1], wkq_sb[:], start=True, stop=True)
                ins.then_inc(prep_pe, 1)
                made("bqk_row")
                pe.matmul(BH1[0:2 * HR, 0:1], bqk_row[:], ones[0:1, 0:1], start=True, stop=True).then_inc(prep_pe, 1)

            def values_weights(b):
                if b == 0:
                    pe.matmul(BW[0:DH, 0:H * C], wvT[:], wo_sb[:].rearrange("d h c -> d (h c)"),
                              start=True, stop=True).then_inc(prep_pe, 1)

            def rows_weights(b):
                if b == 0:
                    made("wvo")
                    for h in range(H):
                        ins = pe.matmul(BY[:, h * C:(h + 1) * C], wxT2[:, h, :, :].rearrange("d s c -> d (s c)"),
                                        wvo[:, h, :], start=True, stop=True)
                    ins.then_inc(prep_pe, 1)
                    for h in range(H):
                        ins = pe.matmul(BH0[0:HR, 0:C], bx_heads[:, h, :], wvo[:, h, :], start=(h == 0), stop=(h == H - 1))
                    ins.then_inc(prep_pe, 1)

            def first_step():
                conv_high(0)
                conv_low(0)
                prepare_first()
                turn_tokens(0)
                prepare_rest()

            def attn_prepared():
                pe.wait_ge(rounded_ident, 1)
                made("wqk_lo")

            def prepare_biases():
                pe.wait_ge(mlp_w_in, MLP_DMAS)
                for k in range(2):
                    ins = pe.matmul(BH0[:, k:k + 1], w1_raw[0:C, k * 128:(k + 1) * 128], b2ln_col[:], start=True, stop=True)
                ins.then_inc(prep_pe, 1)
                pe.wait_ge(ffn_w_in, FFN_DMAS)
                for e in range(NE):
                    ins = pe.matmul(BH1[:, e:e + 1], ew1_raw[0:C, e, :], bet_col[:], start=True, stop=True)
                ins.then_inc(prep_pe, 1)
                pe.wait_ge(prep_pool, place(POOL_PREP, "bet_rows"))
                pe.matmul(BY[:, 0:NE], bet_rows[:], wr_raw[0:C, :], start=True, stop=True).then_inc(prep_pe, 1)
                pe.wait_ge(prep_pool, place(POOL_PREP, "w1_lo"))

            def experts_prepared():
                made("br")
                pe.wait_ge(prep_act, len(ACT_PREP))
                pe.wait_ge(prep_pool, place(POOL_PREP, "ew1_lo"))

            def turn(dst, src, done):
                for c in range(CH):
                    ins = pe.transpose(chunk(dst, c).bitcast(F32R), src[:, c, :, :].rearrange("p s c -> p (s c)"), ident_r[0:P, 0:P])
                ins.then_inc(done, 1)

            def in_parts(dst, w_hi, w_lo, data):
                pe.matmul(dst, w_hi, data, start=True, stop=False)
                return pe.matmul(dst, w_lo, data, start=False, stop=True)

            def turn_z(b):
                pe.wait_ge(S["z_lo"], b + 1)
                freed(pe, S["qT"], b)
                turn(B1, zhl, S["ps_zT"])

            def turn_z2(b):
                pe.wait_ge(S["z2_lo"], b + 1)
                freed(pe, S["h2"], b)
                turn(BM, z2hl, S["ps_z2T"])

            def turn_z3(b):
                pe.wait_ge(S["z3_lo"], b + 1)
                freed(pe, gelu[NE - 2], b)
                turn(BH0, z3hl, S["ps_z3T"])

            def key_query_logits(b):
                pe.wait_ge(S["zT"], b + 1)
                freed(pe, S["fx"], b)
                in_parts(B2[0:2 * HR, 0:NT], wqk_hi[:], wqk_lo[:], zT[:]).then_inc(S["ps_L"], 1)

            N = NT + HALF

            def conv_high(b):
                pe.wait_ge(S["x_lo"], b + 1)
                freed(pe, S["h1"], b)
                if isinstance(b, int) and b == 0:
                    pe.wait_ge(prep_dve, place(DVE_PREP, "wc_lo"))
                for t in range(HALF):
                    pe.matmul(BA[:, 0:N], wc_hi[:, t, :], x_hi[:, t:t + N], start=(t == 0), stop=False)
                    pe.matmul(BA[:, 0:N], wc_lo[:, t, :], x_hi[:, t:t + N], start=False, stop=False)

            def conv_low(b):
                for t in range(HALF):
                    ins = pe.matmul(BA[:, 0:N], wc_hi[:, t, :], x_lo[:, t:t + N], start=False, stop=(t == HALF - 1))
                ins.then_inc(S["ps_conv"], 1)

            def turn_queries(b):
                count = b + 1
                plain(pe)
                pe.wait_ge(S["L"], count)
                for c in range(CH):
                    ins = pe.transpose(B1[0:P, c * HR:(c + 1) * HR], kq[HR:2 * HR, c * P:(c + 1) * P],
                                       ident[HR:2 * HR, HR:2 * HR])
                ins.then_inc(S["ps_q"], 1)

            def turn_keys(b):
                count = b + 1
                plain(pe)
                pe.wait_ge(S["k_exp"], count)
                for c in range(CH):
                    ins = pe.transpose(B2[0:P, c * HR:(c + 1) * HR], kq[0:HR, c * P:(c + 1) * P], ident[0:HR, 0:HR])
                ins.then_inc(S["ps_k"], 1)

            def route(b):
                pe.wait_ge(S["z3T"], b + 1)
                freed(pe, gated[NP - 1], b)
                for c in range(CH):
                    pe.matmul(BW[0:P, c * NE:(c + 1) * NE], z3T[:, c * P:(c + 1) * P], wr_hi[:], start=True, stop=False)
                    ins = pe.matmul(BW[0:P, c * NE:(c + 1) * NE], z3T[:, c * P:(c + 1) * P], wr_lo[:], start=False, stop=True)
                ins.then_inc(S["ps_lg"], 1)

            def turn_gates(b):
                pe.wait_ge(S["w_lo"], b + 1)
                for c in range(CH):
                    ins = pe.transpose(BW[0:2 * NE, c * P:(c + 1) * P].bitcast(F32R),
                                       whl[:, c, :, :].rearrange("p s e -> p (s e)"), ident_r[0:P, 0:P])
                ins.then_inc(S["ps_w"], 1)

            def mlp_hidden(b, k):
                pe.wait_ge(S["mlp_g0"] if k else S["z2T"], b + 1)
                in_parts(cols(BM), w1_hi[:, k * 128:(k + 1) * 128], w1_lo[:, k * 128:(k + 1) * 128],
                         z2T[:]).then_inc(S["ps_m1"] if k else S["ps_m0"], 1)

            def mlp_out(b):
                pe.wait_ge(S["mlp_g1"], b + 1)
                for k in range(2):
                    ins = pe.matmul(BM[k * C:(k + 1) * C, 0:NT], w2_sb[:, k, :], mg[k][:], start=True, stop=True)
                ins.then_inc(S["ps_m2"], 1)

            def turn_mlp(b):
                pe.wait_ge(S["mlp_F"], b + 1)
                for c in range(CH):
                    ins = pe.transpose(BM[0:P, c * 2 * C:(c + 1) * 2 * C], mF[:, c * P:(c + 1) * P], ident[:])
                ins.then_inc(S["ps_mT"], 1)

            def key_sums(b):
                pe.wait_ge(S["EkT"], b + 1)
                for c in range(CH):
                    ins = pe.matmul(B2[0:HR, 0:C], EkT[:, c, :], z_kept[:, c, :], start=(c == 0), stop=(c == CH - 1))
                ins.then_inc(S["ps_G"], 1)

            def turn_key_sums(b):
                count = b + 1
                plain(pe)
                pe.wait_ge(S["G_norm"], count)
                pe.transpose(B2[:, 0:HR], Gd[:].rearrange("p s c -> p (s c)"), ident[0:HR, 0:HR]).then_inc(S["ps_GT"], 1)

            def value_rows(b):
                pe.wait_ge(S["G_heads"], b + 1)
                if isinstance(b, int) and b == 0:
                    made("u_bias")
                for j in range(H // 2):
                    ins = pe.matmul(B2[0:HR, 0:C], Gx[:, j, :], u_pair[:, j, :], start=(j == 0), stop=(j == H // 2 - 1))
                ins.then_inc(S["ps_M"], 1)

            def turn_query_parts(b):
                pe.wait_ge(S["q_lo"], b + 1)
                for c in range(CH):
                    ins = pe.transpose(B1[0:3 * HR, c * P:(c + 1) * P].bitcast(F32R),
                                       qhl[:, c, :, :].rearrange("p s e -> p (s e)"), ident_r[0:P, 0:P])
                ins.then_inc(S["ps_qT"], 1)

            def attend(b):
                pe.wait_ge(S["M_stack"], b + 1)
                pe.wait_ge(S["qT"], b + 1)
                for c in range(CH):
                    ins = pe.matmul(B2[0:P, c * C:(c + 1) * C], qT[:, c * P:(c + 1) * P], M3[:], start=True, stop=True)
                ins.then_inc(S["ps_at"], 1)

            def turn_tokens(b):
                count = b + 1
                plain(pe)
                pe.wait_ge(S["pre"], count)
                for c in range(CH):
                    ins = pe.transpose(BA[0:P, c * C:(c + 1) * C], pre[:, c * P:(c + 1) * P], ident[0:C, 0:C])
                ins.then_inc(S["ps_pre"], 1)

            def hidden(b, e):
                if e < 2:
                    pe.wait_ge(S["z3T"], b + 1)
                    if e:
                        freed(pe, gelu[NE - 1], b)
                else:
                    pe.wait_ge(gelu[e - 2], b + 1)
                in_parts(cols(BH[e % 2]), ew1_hi[:, e * EH:(e + 1) * EH], ew1_lo[:, e * EH:(e + 1) * EH],
                         z3T[:]).then_inc(ps_h[e], 1)

            def outputs(b, j):
                pe.wait_ge(gelu[2 * j + 1], b + 1)
                if j:
                    pe.wait_ge(yev[j - 1], b + 1)
                else:
                    freed(pe, S["o"], b)
                for s in range(2):
                    ins = pe.matmul(BY[s * C:(s + 1) * C, 0:NT], ew2[:, 2 * j + s, :], eg[(2 * j + s) % 4][:],
                                    start=True, stop=True)
                ins.then_inc(ps_y[j], 1)

            def spread_gates(b, j):
                pe.wait_ge(gated[j - 1] if j else S["wT"], b + 1)
                pe.matmul(cols(BW), sel[:, j, :], wT[:], start=True, stop=True).then_inc(ps_wb[j], 1)

            def turn_result(b):
                pe.wait_ge(yev[NP - 1], b + 1)
                pe.wait_ge(S["sum_all"], b + 1)
                for c in range(CH):
                    ins = pe.transpose(BY[0:P, c * 2 * C:(c + 1) * 2 * C], sum_all[:, c * P:(c + 1) * P], ident[:])
                ins.then_inc(S["ps_out"], 1)

            def opening(A, B, M, E, T):
                do(values_weights, B)
                do(hidden, T, 4)
                do(spread_gates, T, 0)
                do(hidden, T, 6)
                do(outputs, T, 1)
                do(spread_gates, T, 1)
                do(turn_z, B)
                do(hidden, T, 5)
                do(turn_z2, M)
                do(hidden, T, 7)
                do(spread_gates, T, 2)
                do(key_query_logits, B)
                do(turn_z3, E)
                do(conv_high, A)
                do(turn_queries, B)
                do(route, E)
                do(mlp_hidden, M, 0)
                do(turn_keys, B)
                do(conv_low, A)
                do(spread_gates, T, 3)
                do(outputs, T, 2)
                do(outputs, T, 3)
                do(key_sums, B)
                do(hidden, E, 0)
                do(turn_result, T)
                do(rows_weights, B)
                do(hidden, E, 1)
                do(turn_key_sums, B)
                do(mlp_hidden, M, 1)
                do(turn_query_parts, B)
                do(value_rows, B)
                do(turn_tokens, A)
                do(mlp_out, M)
                do(hidden, E, 2)
                do(attend, B)
                do(hidden, E, 3)
                do(turn_gates, E)
                do(turn_mlp, M)
                do(outputs, E, 0)

            def step(A, B, M, E, T):
                do(hidden, T, 4)
                do(hidden, T, 5)
                do(spread_gates, T, 0)
                do(outputs, T, 1)
                do(hidden, T, 6)
                do(hidden, T, 7)
                do(spread_gates, T, 1)
                do(outputs, T, 2)
                do(spread_gates, T, 2)
                do(turn_z, B)
                do(outputs, T, 3)
                do(spread_gates, T, 3)
                do(key_query_logits, B)
                do(turn_z2, M)
                do(turn_z3, E)
                do(conv_high, A)
                do(route, E)
                do(turn_queries, B)
                do(mlp_hidden, M, 0)
                do(turn_keys, B)
                do(conv_low, A)
                do(key_sums, B)
                do(hidden, E, 1)
                do(hidden, E, 0)
                do(turn_key_sums, B)
                do(mlp_hidden, M, 1)
                do(turn_result, T)
                do(value_rows, B)
                do(turn_query_parts, B)
                do(turn_tokens, A)
                do(mlp_out, M)
                do(hidden, E, 2)
                do(attend, B)
                do(hidden, E, 3)
                do(turn_gates, E)
                do(turn_mlp, M)
                do(outputs, E, 0)

            def closing(A, B, M, E, T):
                do(hidden, T, 4)
                do(spread_gates, T, 0)
                do(hidden, T, 5)
                do(outputs, T, 1)
                do(hidden, T, 6)
                do(hidden, T, 7)
                do(spread_gates, T, 1)
                do(outputs, T, 2)
                do(spread_gates, T, 2)
                do(turn_z, B)
                do(outputs, T, 3)
                do(key_query_logits, B)
                do(spread_gates, T, 3)
                do(turn_z2, M)
                do(turn_z3, E)
                do(conv_high, A)
                do(turn_queries, B)
                do(mlp_hidden, M, 0)
                do(route, E)
                do(hidden, E, 0)
                do(hidden, E, 1)
                do(turn_keys, B)
                do(key_sums, B)
                do(turn_key_sums, B)
                do(mlp_hidden, M, 1)
                do(value_rows, B)
                do(conv_low, A)
                do(turn_result, T)
                do(turn_query_parts, B)
                do(mlp_out, M)
                do(hidden, E, 2)
                do(hidden, E, 3)
                do(attend, B)
                do(turn_gates, E)
                do(turn_mlp, M)
                do(outputs, E, 0)
                do(turn_tokens, A)

            run(pe, opening, step, closing, {0: first_step, 1: attn_prepared, 2: prepare_biases, 3: experts_prepared}, own_first=True)


_INS = ['x', 'L0_tok_filt', 'L0_tok_W_k', 'L0_tok_b_k', 'L0_attn_ln1_g', 'L0_attn_ln1_b', 'L0_attn_Wx',
        'L0_attn_bx', 'L0_attn_Wq', 'L0_attn_Wk', 'L0_attn_Wv', 'L0_attn_Wo', 'L0_attn_bo', 'L0_attn_ln2_g',
        'L0_attn_ln2_b', 'L0_attn_W1', 'L0_attn_b1', 'L0_attn_W2', 'L0_attn_b2', 'L0_ffn_gamma',
        'L0_ffn_beta', 'L0_ffn_Wr', 'L0_ffn_br', 'L0_ffn_W1', 'L0_ffn_b1', 'L0_ffn_W2', 'L0_ffn_b2']
_LAST_TWO_AXES_SWAPPED = ['x', 'L0_tok_filt', 'L0_attn_Wx', 'L0_attn_Wv']


def kernel(**inputs):
    import numpy as _np
    import concourse.bacc as _bacc
    from concourse import mybir as _mybir
    from concourse.bass_utils import run_bass_kernel_spmd as _run

    laid_out = {name: inputs[name] for name in _INS}
    laid_out['L0_attn_Wx_rows'] = inputs['L0_attn_Wx']
    for name in _LAST_TWO_AXES_SWAPPED:
        laid_out[name] = _np.swapaxes(inputs[name], -1, -2)
    nc = _bacc.Bacc("TRN2", target_bir_lowering=False, num_devices=1)
    arrays, args = {}, {}
    for name, data in laid_out.items():
        v = _np.ascontiguousarray(data)
        arrays[f"in_{name}"] = v
        t = nc.dram_tensor(f"in_{name}", v.shape, _mybir.dt.from_np(v.dtype), kind="ExternalInput")
        args[name.removeprefix("L0_")] = t.ap()
    x, filt, wk = (inputs[n] for n in ('x', 'L0_tok_filt', 'L0_tok_W_k'))
    shape = (x.shape[0], x.shape[1] - filt.shape[0], wk.shape[1])
    res = nc.dram_tensor("out_0", shape, _mybir.dt.from_np(_np.dtype("float32")), kind="ExternalOutput")
    audio_tower_kernel(nc, args, res.ap())
    r = _run(nc, [arrays], core_ids=[0])
    return r.results[0]["out_0"]
```
